# Optimizing a Trainium2 kernel written in Bass

```python
import numpy as np
import jax
import jax.numpy as jnp

def _softmax(x, axis=-1):
    return jax.nn.softmax(x, axis=axis)

def _gelu(x):
    return jax.nn.gelu(x, approximate=True)

def _silu(x):
    return jax.nn.silu(x)

def _sigmoid(x):
    return jax.nn.sigmoid(x)

def _layernorm(x, axis=-1, eps=1e-05):
    m = jnp.mean(x, axis=axis, keepdims=True)
    v = jnp.var(x, axis=axis, keepdims=True)
    return (x - m) / jnp.sqrt(v + eps)

def _scatter_add(tgt, idx, src, axis=0):
    return tgt.at[idx].add(src)

def _segment_sum(src, seg, n):
    return jax.ops.segment_sum(src, seg, n)
kernel_name = 'mk_seq_preln_d2_jaxref_r8_27074c'

def setup_inputs(seed: int=0):
    np.random.seed(seed)
    _w = jnp.asarray

    def _L0_attn_setup():
        import jax, jax.numpy as jnp
        import numpy as np
        D_MODEL = 128
        N_HEADS = 16
        HEAD_DIM = D_MODEL // N_HEADS
        SCALE = HEAD_DIM ** (-0.5)
        key = jax.random.key(seed)
        ks = jax.random.split(key, 9)
        s = 1.0 / np.sqrt(D_MODEL)
        x = jax.random.normal(ks[0], (2, 256, D_MODEL), dtype=jnp.float32)
        Wq = jax.random.uniform(ks[1], (D_MODEL, D_MODEL), jnp.float32, -s, s)
        bq = jax.random.uniform(ks[2], (D_MODEL,), jnp.float32, -s, s)
        Wk = jax.random.uniform(ks[3], (D_MODEL, D_MODEL), jnp.float32, -s, s)
        bk = jax.random.uniform(ks[4], (D_MODEL,), jnp.float32, -s, s)
        Wv = jax.random.uniform(ks[5], (D_MODEL, D_MODEL), jnp.float32, -s, s)
        bv = jax.random.uniform(ks[6], (D_MODEL,), jnp.float32, -s, s)
        Wo = jax.random.uniform(ks[7], (D_MODEL, D_MODEL), jnp.float32, -s, s)
        bo = jax.random.uniform(ks[8], (D_MODEL,), jnp.float32, -s, s)
        return {'x': x, 'Wq': Wq, 'bq': bq, 'Wk': Wk, 'bk': bk, 'Wv': Wv, 'bv': bv, 'Wo': Wo, 'bo': bo}
    _L0_attn_in = _L0_attn_setup()

    def _L0_ffn_setup():
        import jax, jax.numpy as jnp
        import numpy as np
        DIM = 128
        DEPTH = 6
        HEADS = 16
        DIM_HEAD = 64
        WINDOW = 32
        INNER = HEADS * DIM_HEAD
        DIM_INNER = int(DIM * 4 * 2 / 3)
        QK_SCALE = 8.0

        def shift_tokens(t):
            a, s = jnp.split(t, 2, -1)
            s = jnp.pad(s, ((0, 0), (1, 0), (0, 0)))[:, :-1]
            return jnp.concatenate([a, s], -1)

        def l2norm(t):
            return t / jnp.maximum(jnp.linalg.norm(t, axis=-1, keepdims=True), 1e-12)

        def rotate_half(x):
            x1, x2 = jnp.split(x, 2, -1)
            return jnp.concatenate([-x2, x1], -1)

        def rotary_tables(n):
            half = jnp.arange(0, DIM_HEAD, 2, dtype=jnp.float32)
            inv_freq = 1.0 / 10000.0 ** (half / DIM_HEAD)
            t = jnp.arange(n, dtype=jnp.float32)
            freqs = t[:, None] * inv_freq[None, :]
            freqs = jnp.concatenate([freqs, freqs], -1)
            base_scale = (half + 0.4 * DIM_HEAD) / (1.4 * DIM_HEAD)
            power = (t - n // 2) / (WINDOW // 2)
            scale = base_scale[None, :] ** power[:, None]
            scale = jnp.concatenate([scale, scale], -1)
            return (freqs, scale)

        def local_attention(q, k, v):
            b, h, n, d = q.shape
            w = WINDOW
            nw = n // w
            bq = q.reshape(b, h, nw, w, d)
            bk = k.reshape(b, h, nw, w, d)
            bv = v.reshape(b, h, nw, w, d)

            def look(t):
                p = jnp.pad(t, ((0, 0), (0, 0), (1, 0), (0, 0), (0, 0)))
                return jnp.concatenate([p[:, :, :nw], p[:, :, 1:]], axis=3)
            bk2, bv2 = (look(bk), look(bv))
            seq = jnp.arange(n).reshape(nw, w)
            seq_p = jnp.pad(seq, ((1, 0), (0, 0)), constant_values=-1)
            jt = jnp.concatenate([seq_p[:nw], seq_p[1:]], axis=1)
            it = seq[:, :, None]
            jb = jt[:, None, :]
            mask = (it < jb) | (it > jb + w) | (jb == -1)
            sim = jnp.einsum('bhwie,bhwje->bhwij', bq, bk2) * QK_SCALE
            sim = jnp.where(mask, -jnp.finfo(sim.dtype).max, sim)
            attn = jax.nn.softmax(sim, -1)
            out = jnp.einsum('bhwij,bhwje->bhwie', attn, bv2)
            return out.reshape(b, h, n, d)

        def attn_layer(x, Wqkv, qs, ksc, Wo):
            b, n, _ = x.shape
            qkv = x @ Wqkv
            q, k, v = jnp.split(qkv, 3, -1)
            sh = lambda t: t.reshape(b, n, HEADS, DIM_HEAD).transpose(0, 2, 1, 3)
            q, k, v = (sh(q), sh(k), sh(v))
            q = l2norm(q) * qs
            k = l2norm(k) * ksc
            freqs, scale = rotary_tables(n)
            cos, sin = (jnp.cos(freqs), jnp.sin(freqs))
            q = q * cos * scale + rotate_half(q) * sin * scale
            inv = 1.0 / scale
            k = k * cos * inv + rotate_half(k) * sin * inv
            out = local_attention(q, k, v)
            out = out.transpose(0, 2, 1, 3).reshape(b, n, INNER)
            return out @ Wo

        def ffn_layer(x, g, bln, W1, b1, W2, b2):
            mu = x.mean(-1, keepdims=True)
            var = ((x - mu) ** 2).mean(-1, keepdims=True)
            xn = (x - mu) / jnp.sqrt(var + 1e-05) * g + bln
            hg = xn @ W1 + b1
            a, gate = jnp.split(hg, 2, -1)
            return a * jax.nn.gelu(gate, approximate=False) @ W2 + b2
        key = jax.random.key(seed)
        ks = jax.random.split(key, 8)
        B, N = (2, 256)
        init = lambda k, shape: jax.random.normal(k, shape, jnp.float32) * 0.02
        return {'x': jax.random.normal(ks[0], (B, N, DIM), jnp.float32), 'Wqkv': init(ks[1], (DEPTH, DIM, 3 * INNER)), 'q_scale': jnp.ones((DEPTH, DIM_HEAD), jnp.float32), 'k_scale': jnp.ones((DEPTH, DIM_HEAD), jnp.float32), 'Wo': init(ks[2], (DEPTH, INNER, DIM)), 'ln_g': jnp.ones((DEPTH, DIM), jnp.float32), 'ln_b': jnp.zeros((DEPTH, DIM), jnp.float32), 'W1': init(ks[3], (DEPTH, DIM, 2 * DIM_INNER)), 'b1': jnp.zeros((DEPTH, 2 * DIM_INNER), jnp.float32), 'W2': init(ks[4], (DEPTH, DIM_INNER, DIM)), 'b2': jnp.zeros((DEPTH, DIM), jnp.float32)}
    _L0_ffn_in = _L0_ffn_setup()

    def _L1_attn_setup():
        import jax, jax.numpy as jnp
        import numpy as np
        B, L, D, H = (2, 256, 128, 16)
        HD = D // H
        ROPE_BASE = 10000.0

        def _rope(x):
            seq, hd = (x.shape[2], x.shape[3])
            inv_freq = 1.0 / ROPE_BASE ** (jnp.arange(0, hd, 2, dtype=jnp.float32) / hd)
            freqs = jnp.arange(seq, dtype=jnp.float32)[:, None] * inv_freq
            cos = jnp.repeat(jnp.cos(freqs), 2, axis=-1)
            sin = jnp.repeat(jnp.sin(freqs), 2, axis=-1)
            xp = x.reshape(*x.shape[:-1], hd // 2, 2)
            x_rot = jnp.stack([-xp[..., 1], xp[..., 0]], axis=-1).reshape(x.shape)
            return x * cos + x_rot * sin
        key = jax.random.key(seed)
        ks = jax.random.split(key, 9)
        s = 1.0 / np.sqrt(D)
        mk = lambda k: jax.random.normal(k, (D, D), dtype=jnp.float32) * s
        return {'x': jax.random.normal(ks[0], (B, L, D), dtype=jnp.float32), 'Wq': mk(ks[1]), 'bq': jnp.zeros((D,), jnp.float32), 'Wk': mk(ks[2]), 'bk': jnp.zeros((D,), jnp.float32), 'Wv': mk(ks[3]), 'bv': jnp.zeros((D,), jnp.float32), 'Wp': mk(ks[4]), 'bp': jnp.zeros((D,), jnp.float32)}
    _L1_attn_in = _L1_attn_setup()

    def _L1_ffn_setup():
        import jax, jax.numpy as jnp
        import numpy as np
        DIM = 128

        def _reference_tuple_inner(x, W_r, W_k, W_v, mu_r, mu_k):
            B, T, C = x.shape
            x_prev = jnp.concatenate([jnp.zeros((B, 1, C), x.dtype), x[:, :-1, :]], axis=1)
            xr = mu_r * x + (1.0 - mu_r) * x_prev
            xk = mu_k * x + (1.0 - mu_k) * x_prev
            r = jax.nn.sigmoid(jnp.einsum('btc,dc->btd', xr, W_r))
            k = jnp.einsum('btc,dc->btd', xk, W_k)
            k_act = jnp.square(jax.nn.relu(k))
            out = r * jnp.einsum('btc,dc->btd', k_act, W_v)
            new_state = x[:, -1, :]
            return (out, new_state)
        key = jax.random.key(seed)
        ks = jax.random.split(key, 6)
        B, T, C = (8, 256, DIM)
        x = jax.random.normal(ks[0], (B, T, C), dtype=jnp.float32)
        s = 1.0 / np.sqrt(C)
        W_r = jax.random.uniform(ks[1], (C, C), jnp.float32, -s, s)
        W_k = jax.random.uniform(ks[2], (C, C), jnp.float32, -s, s)
        W_v = jax.random.uniform(ks[3], (C, C), jnp.float32, -s, s)
        mu_r = jax.random.uniform(ks[4], (C,), jnp.float32)
        mu_k = jax.random.uniform(ks[5], (C,), jnp.float32)
        return {'x': x, 'W_r': W_r, 'W_k': W_k, 'W_v': W_v, 'mu_r': mu_r, 'mu_k': mu_k}
    _L1_ffn_in = _L1_ffn_setup()
    _d = {'L0_attn_x': _L0_attn_in['x'], 'L0_attn_Wq': _L0_attn_in['Wq'], 'L0_attn_bq': _L0_attn_in['bq'], 'L0_attn_Wk': _L0_attn_in['Wk'], 'L0_attn_bk': _L0_attn_in['bk'], 'L0_attn_Wv': _L0_attn_in['Wv'], 'L0_attn_bv': _L0_attn_in['bv'], 'L0_attn_Wo': _L0_attn_in['Wo'], 'L0_attn_bo': _L0_attn_in['bo'], 'L0_ffn_Wqkv': _L0_ffn_in['Wqkv'], 'L0_ffn_q_scale': _L0_ffn_in['q_scale'], 'L0_ffn_k_scale': _L0_ffn_in['k_scale'], 'L0_ffn_Wo': _L0_ffn_in['Wo'], 'L0_ffn_ln_g': _L0_ffn_in['ln_g'], 'L0_ffn_ln_b': _L0_ffn_in['ln_b'], 'L0_ffn_W1': _L0_ffn_in['W1'], 'L0_ffn_b1': _L0_ffn_in['b1'], 'L0_ffn_W2': _L0_ffn_in['W2'], 'L0_ffn_b2': _L0_ffn_in['b2'], 'L1_attn_Wq': _L1_attn_in['Wq'], 'L1_attn_bq': _L1_attn_in['bq'], 'L1_attn_Wk': _L1_attn_in['Wk'], 'L1_attn_bk': _L1_attn_in['bk'], 'L1_attn_Wv': _L1_attn_in['Wv'], 'L1_attn_bv': _L1_attn_in['bv'], 'L1_attn_Wp': _L1_attn_in['Wp'], 'L1_attn_bp': _L1_attn_in['bp'], 'L1_ffn_W_r': _L1_ffn_in['W_r'], 'L1_ffn_W_k': _L1_ffn_in['W_k'], 'L1_ffn_W_v': _L1_ffn_in['W_v'], 'L1_ffn_mu_r': _L1_ffn_in['mu_r'], 'L1_ffn_mu_k': _L1_ffn_in['mu_k']}
    _x0 = _d['L0_attn_x']
    _d['L0_attn_x'] = jax.random.normal(jax.random.fold_in(jax.random.key(seed), 1), (8, 512, 128), dtype=_x0.dtype)
    del _x0
    return _d

def reference(L0_attn_x, L0_attn_Wq, L0_attn_bq, L0_attn_Wk, L0_attn_bk, L0_attn_Wv, L0_attn_bv, L0_attn_Wo, L0_attn_bo, L0_ffn_Wqkv, L0_ffn_q_scale, L0_ffn_k_scale, L0_ffn_Wo, L0_ffn_ln_g, L0_ffn_ln_b, L0_ffn_W1, L0_ffn_b1, L0_ffn_W2, L0_ffn_b2, L1_attn_Wq, L1_attn_bq, L1_attn_Wk, L1_attn_bk, L1_attn_Wv, L1_attn_bv, L1_attn_Wp, L1_attn_bp, L1_ffn_W_r, L1_ffn_W_k, L1_ffn_W_v, L1_ffn_mu_r, L1_ffn_mu_k):

    def _L0_attn_ref(x, Wq, bq, Wk, bk, Wv, bv, Wo, bo):
        import jax, jax.numpy as jnp
        import numpy as np
        D_MODEL = 128
        N_HEADS = 16
        HEAD_DIM = D_MODEL // N_HEADS
        SCALE = HEAD_DIM ** (-0.5)
        B, S, _ = x.shape

        def heads(t):
            return t.reshape(B, S, N_HEADS, HEAD_DIM).transpose(0, 2, 1, 3)
        q = heads(x @ Wq + bq)
        k = heads(x @ Wk + bk)
        v = heads(x @ Wv + bv)
        attn = jnp.einsum('bhqd,bhkd->bhqk', q, k) * SCALE
        attn_w = jax.nn.softmax(attn, axis=-1)
        out = jnp.einsum('bhqk,bhkd->bhqd', attn_w, v)
        out = out.transpose(0, 2, 1, 3).reshape(B, S, D_MODEL)
        return out @ Wo + bo

    def _L0_ffn_ref(x, Wqkv, q_scale, k_scale, Wo, ln_g, ln_b, W1, b1, W2, b2):
        import jax, jax.numpy as jnp
        import numpy as np
        DIM = 128
        DEPTH = 6
        HEADS = 16
        DIM_HEAD = 64
        WINDOW = 32
        INNER = HEADS * DIM_HEAD
        DIM_INNER = int(DIM * 4 * 2 / 3)
        QK_SCALE = 8.0

        def shift_tokens(t):
            a, s = jnp.split(t, 2, -1)
            s = jnp.pad(s, ((0, 0), (1, 0), (0, 0)))[:, :-1]
            return jnp.concatenate([a, s], -1)

        def l2norm(t):
            return t / jnp.maximum(jnp.linalg.norm(t, axis=-1, keepdims=True), 1e-12)

        def rotate_half(x):
            x1, x2 = jnp.split(x, 2, -1)
            return jnp.concatenate([-x2, x1], -1)

        def rotary_tables(n):
            half = jnp.arange(0, DIM_HEAD, 2, dtype=jnp.float32)
            inv_freq = 1.0 / 10000.0 ** (half / DIM_HEAD)
            t = jnp.arange(n, dtype=jnp.float32)
            freqs = t[:, None] * inv_freq[None, :]
            freqs = jnp.concatenate([freqs, freqs], -1)
            base_scale = (half + 0.4 * DIM_HEAD) / (1.4 * DIM_HEAD)
            power = (t - n // 2) / (WINDOW // 2)
            scale = base_scale[None, :] ** power[:, None]
            scale = jnp.concatenate([scale, scale], -1)
            return (freqs, scale)

        def local_attention(q, k, v):
            b, h, n, d = q.shape
            w = WINDOW
            nw = n // w
            bq = q.reshape(b, h, nw, w, d)
            bk = k.reshape(b, h, nw, w, d)
            bv = v.reshape(b, h, nw, w, d)

            def look(t):
                p = jnp.pad(t, ((0, 0), (0, 0), (1, 0), (0, 0), (0, 0)))
                return jnp.concatenate([p[:, :, :nw], p[:, :, 1:]], axis=3)
            bk2, bv2 = (look(bk), look(bv))
            seq = jnp.arange(n).reshape(nw, w)
            seq_p = jnp.pad(seq, ((1, 0), (0, 0)), constant_values=-1)
            jt = jnp.concatenate([seq_p[:nw], seq_p[1:]], axis=1)
            it = seq[:, :, None]
            jb = jt[:, None, :]
            mask = (it < jb) | (it > jb + w) | (jb == -1)
            sim = jnp.einsum('bhwie,bhwje->bhwij', bq, bk2) * QK_SCALE
            sim = jnp.where(mask, -jnp.finfo(sim.dtype).max, sim)
            attn = jax.nn.softmax(sim, -1)
            out = jnp.einsum('bhwij,bhwje->bhwie', attn, bv2)
            return out.reshape(b, h, n, d)

        def attn_layer(x, Wqkv, qs, ksc, Wo):
            b, n, _ = x.shape
            qkv = x @ Wqkv
            q, k, v = jnp.split(qkv, 3, -1)
            sh = lambda t: t.reshape(b, n, HEADS, DIM_HEAD).transpose(0, 2, 1, 3)
            q, k, v = (sh(q), sh(k), sh(v))
            q = l2norm(q) * qs
            k = l2norm(k) * ksc
            freqs, scale = rotary_tables(n)
            cos, sin = (jnp.cos(freqs), jnp.sin(freqs))
            q = q * cos * scale + rotate_half(q) * sin * scale
            inv = 1.0 / scale
            k = k * cos * inv + rotate_half(k) * sin * inv
            out = local_attention(q, k, v)
            out = out.transpose(0, 2, 1, 3).reshape(b, n, INNER)
            return out @ Wo

        def ffn_layer(x, g, bln, W1, b1, W2, b2):
            mu = x.mean(-1, keepdims=True)
            var = ((x - mu) ** 2).mean(-1, keepdims=True)
            xn = (x - mu) / jnp.sqrt(var + 1e-05) * g + bln
            hg = xn @ W1 + b1
            a, gate = jnp.split(hg, 2, -1)
            return a * jax.nn.gelu(gate, approximate=False) @ W2 + b2
        for i in range(DEPTH):
            x = attn_layer(shift_tokens(x), Wqkv[i], q_scale[i], k_scale[i], Wo[i]) + x
            x = ffn_layer(shift_tokens(x), ln_g[i], ln_b[i], W1[i], b1[i], W2[i], b2[i]) + x
        return x

    def _L1_attn_ref(x, Wq, bq, Wk, bk, Wv, bv, Wp, bp):
        import jax, jax.numpy as jnp
        import numpy as np
        B, L, D, H = (2, 256, 128, 16)
        HD = D // H
        ROPE_BASE = 10000.0

        def _rope(x):
            seq, hd = (x.shape[2], x.shape[3])
            inv_freq = 1.0 / ROPE_BASE ** (jnp.arange(0, hd, 2, dtype=jnp.float32) / hd)
            freqs = jnp.arange(seq, dtype=jnp.float32)[:, None] * inv_freq
            cos = jnp.repeat(jnp.cos(freqs), 2, axis=-1)
            sin = jnp.repeat(jnp.sin(freqs), 2, axis=-1)
            xp = x.reshape(*x.shape[:-1], hd // 2, 2)
            x_rot = jnp.stack([-xp[..., 1], xp[..., 0]], axis=-1).reshape(x.shape)
            return x * cos + x_rot * sin
        b, l, d = x.shape
        to_heads = lambda t: t.reshape(b, l, H, HD).transpose(0, 2, 1, 3)
        q = to_heads(x @ Wq + bq)
        k = to_heads(x @ Wk + bk)
        v = to_heads(x @ Wv + bv)
        q = _rope(q)
        k = _rope(k)
        scores = jnp.einsum('bhic,bhjc->bhij', q, k) / np.sqrt(HD)
        attn = jax.nn.softmax(scores, axis=-1)
        out = jnp.einsum('bhij,bhjc->bhic', attn, v)
        out = out.transpose(0, 2, 1, 3).reshape(b, l, d)
        return out @ Wp + bp

    def _L1_ffn_ref(x, W_r, W_k, W_v, mu_r, mu_k):
        import jax, jax.numpy as jnp
        import numpy as np
        DIM = 128

        def _reference_tuple_inner(x, W_r, W_k, W_v, mu_r, mu_k):
            B, T, C = x.shape
            x_prev = jnp.concatenate([jnp.zeros((B, 1, C), x.dtype), x[:, :-1, :]], axis=1)
            xr = mu_r * x + (1.0 - mu_r) * x_prev
            xk = mu_k * x + (1.0 - mu_k) * x_prev
            r = jax.nn.sigmoid(jnp.einsum('btc,dc->btd', xr, W_r))
            k = jnp.einsum('btc,dc->btd', xk, W_k)
            k_act = jnp.square(jax.nn.relu(k))
            out = r * jnp.einsum('btc,dc->btd', k_act, W_v)
            new_state = x[:, -1, :]
            return (out, new_state)
        return _reference_tuple_inner(x, W_r, W_k, W_v, mu_r, mu_k)[0]
    x = L0_attn_x
    x = x + _L0_attn_ref(_layernorm(x, axis=-1), L0_attn_Wq, L0_attn_bq, L0_attn_Wk, L0_attn_bk, L0_attn_Wv, L0_attn_bv, L0_attn_Wo, L0_attn_bo)
    x = x + _L0_ffn_ref(_layernorm(x, axis=-1), L0_ffn_Wqkv, L0_ffn_q_scale, L0_ffn_k_scale, L0_ffn_Wo, L0_ffn_ln_g, L0_ffn_ln_b, L0_ffn_W1, L0_ffn_b1, L0_ffn_W2, L0_ffn_b2)
    x = x + _L1_attn_ref(_layernorm(x, axis=-1), L1_attn_Wq, L1_attn_bq, L1_attn_Wk, L1_attn_bk, L1_attn_Wv, L1_attn_bv, L1_attn_Wp, L1_attn_bp)
    x = x + _L1_ffn_ref(_layernorm(x, axis=-1), L1_ffn_W_r, L1_ffn_W_k, L1_ffn_W_v, L1_ffn_mu_r, L1_ffn_mu_k)
    return x

_drawn_inputs = setup_inputs


def setup_inputs(seed=0):
    import zlib

    import numpy as np

    out = dict(_drawn_inputs(seed))
    spreads = {'L0_ffn_q_scale': (1.0, 0.6),
     'L0_ffn_k_scale': (1.0, 0.6),
     'L0_ffn_ln_g': (1.0, 0.6),
     'L0_ffn_ln_b': (0.0, 0.8),
     'L0_ffn_b1': (0.0, 0.8),
     'L0_ffn_b2': (0.0, 0.1),
     'L1_attn_bq': (0.0, 2.0),
     'L1_attn_bk': (0.0, 2.0),
     'L1_attn_bv': (0.0, 0.456),
     'L1_attn_bp': (0.0, 0.466)}
    factors = {'L0_attn_Wq': 5.035,
     'L0_attn_bq': 8.0,
     'L0_attn_Wk': 5.059,
     'L0_attn_bk': 64.0,
     'L0_attn_Wv': 3.008,
     'L0_ffn_W1': 3.64,
     'L0_ffn_W2': 3.556,
     'L1_ffn_W_r': 25.203,
     'L1_ffn_mu_r': 46.496,
     'L1_attn_Wq': 3.678,
     'L1_attn_Wk': 3.202,
     'L1_ffn_W_k': 3.024,
     'L1_ffn_W_v': 2.869,
     'L1_ffn_mu_k': 5.865}
    for name, (base, spread) in spreads.items():
        noise = np.random.default_rng([zlib.crc32(name.encode()), seed]).standard_normal(out[name].shape)
        drawn = base * np.exp(spread * noise) if base else spread * noise
        out[name] = jnp.asarray(drawn.astype(out[name].dtype))
    for name, factor in factors.items():
        out[name] = (out[name] * factor).astype(out[name].dtype)
    return out
```

```python
import math
from contextlib import ExitStack, contextmanager

import numpy as np

import concourse.bass as bass
from concourse import mybir

F32 = mybir.dt.float32
BF16 = mybir.dt.bfloat16
I32 = mybir.dt.int32
ALU = mybir.AluOpType
ACT = mybir.ActivationFunctionType
AX = mybir.AxisListType

D = 128
NB = 8
T = 512
NT = T // 128
LN_EPS = 1e-5

H = 16
HD = D // H
SPLIT = 3
KROWS = SPLIT * SPLIT * HD
ROWS = KROWS + SPLIT
VW = 32

DEPTH = 6
DH = 64
HALF = DH // 2
INNER = H * DH
WIN = 32
NC = 4
CH = H // NC
KC = T + WIN
DI = int(D * 4 * 2 / 3)
FCH = [128, 128, DI - 256]
MASKED = -1e37
QK_SCALE = 8.0
NVEC = 13

RSQRT_MAGIC = float(0x5F3759DF)


class Tally:

    def __init__(self):
        self.used = {}

    def next(self, sem, n=1):
        count = self.used.get(sem.name, (sem, 0))[1] + n
        self.used[sem.name] = (sem, count)
        return count

    def settle(self, eng):
        for sem, count in self.used.values():
            eng.sem_inc(sem, -count)
        self.used = {}


@contextmanager
def semaphore_set(nc, prefix):
    with ExitStack() as ctx:
        taken = []

        def sem(name):
            taken.append(ctx.enter_context(nc.semaphore(f"{prefix}_{name}")))
            return taken[-1]

        yield sem
        with nc.Block() as block:
            @block.sync
            def _(sp):
                for s in taken:
                    sp.sem_clear(s)


def rsqrt(nc, v, tally, step, a, t, y):
    nc.vector.tensor_scalar(t.bitcast(I32), a.bitcast(I32), 1, None, ALU.logical_shift_right).then_inc(step, 1)
    v.wait_ge(step, tally.next(step))
    nc.vector.tensor_scalar(y.bitcast(I32), t.bitcast(I32), -1.0, RSQRT_MAGIC, ALU.mult, ALU.add).then_inc(step, 1)
    for i in range(3):
        v.wait_ge(step, tally.next(step))
        nc.vector.scalar_tensor_tensor(out=t, in0=y, scalar=-0.5, in1=y, op0=ALU.mult, op1=ALU.mult).then_inc(step, 1)
        v.wait_ge(step, tally.next(step))
        nc.vector.tensor_tensor(t, t, a, ALU.mult).then_inc(step, 1)
        v.wait_ge(step, tally.next(step))
        last = nc.vector.scalar_tensor_tensor(out=y, in0=t, scalar=1.5, in1=y, op0=ALU.add, op1=ALU.mult)
        if i < 2:
            last.then_inc(step, 1)
    return last


def layernorm_pass(nc, name, C, src, dst_parts):
    with ExitStack() as ctx:
        def sb(n, shape, dt=F32):
            return ctx.enter_context(nc.sbuf_tensor(f"{name}_{n}", shape, dt))

        sem = ctx.enter_context(semaphore_set(nc, name))

        xc = sb("xc", [D, NB, T])
        sq = sb("sq", [D, 2, T])
        var = sb("var", [D, NB * NT])
        tmp = sb("tmp", [D, NB * NT])
        rstd = sb("rstd", [D, NB * NT])
        mean_ps = [ctx.enter_context(nc.psum_tensor(f"{name}_mean{i}", [D, T], F32)) for i in range(2)]
        var_ps = ctx.enter_context(nc.psum_tensor(f"{name}_varp", [D, NB * NT], F32))
        bc_ps = [ctx.enter_context(nc.psum_tensor(f"{name}_bc{i}", [D, T], F32)) for i in range(2)]
        mean_ready, centred, squared, var_ready = sem("mean"), sem("centred"), sem("squared"), sem("varr")
        sq_used, rstd_ready, bc_ready, bc_used, step = sem("squsd"), sem("rstd"), sem("bc"), sem("bcused"), sem("step")
        block = ctx.enter_context(nc.Block())

        @block.tensor
        def _(pe):
            def mean(b):
                if b >= 2:
                    pe.wait_ge(centred, b - 1)
                nc.tensor.matmul(mean_ps[b % 2][:], C["inv"][:], src[:, b, :], start=True, stop=True).then_inc(mean_ready, 1)

            mean(0)
            for b in range(NB):
                if b + 1 < NB:
                    mean(b + 1)
                pe.wait_ge(squared, b + 1)
                for t in range(NT):
                    last = nc.tensor.matmul(var_ps[:, b * NT + t:b * NT + t + 1], sq[:, b % 2, 128 * t:128 * t + 128],
                                            C["inv"][:, 0:1], start=True, stop=True)
                last.then_inc(var_ready, 1)
            pe.wait_ge(rstd_ready, 1)
            for b in range(NB):
                if b >= 2:
                    pe.wait_ge(bc_used, b - 1)
                for t in range(NT):
                    last = nc.tensor.transpose(bc_ps[b % 2][:, 128 * t:128 * t + 128],
                                               rstd[:, b * NT + t:b * NT + t + 1].to_broadcast([128, 128]), C["ident"][:])
                last.then_inc(bc_ready, 1)

        @block.scalar
        def _(act):
            for b in range(NB):
                act.wait_ge(centred, b + 1)
                if b >= 2:
                    act.wait_ge(var_ready, b - 1)
                nc.scalar.activation(sq[:, b % 2, :], xc[:, b, :], ACT.Square).then_inc(squared, 1)

        @block.vector
        def _(v):
            tally = Tally()
            for b in range(NB):
                v.wait_ge(mean_ready, b + 1)
                nc.vector.tensor_tensor(xc[:, b, :], src[:, b, :], mean_ps[b % 2][:], ALU.subtract).then_inc(centred, 1)
            v.wait_ge(var_ready, NB)
            nc.vector.tensor_scalar(var[:], var_ps[:], LN_EPS, None, ALU.add).then_inc(step, 1)
            v.wait_ge(step, tally.next(step))
            rsqrt(nc, v, tally, step, var[:], tmp[:], rstd[:]).then_inc(rstd_ready, 1)
            for b in range(NB):
                v.wait_ge(bc_ready, b + 1)
                for part, dst in dst_parts(b):
                    last = nc.vector.tensor_tensor(dst, xc[part, b, :], bc_ps[b % 2][part, :], ALU.mult)
                last.then_inc(bc_used, 1)


def attention_pass(nc, name, C, x, xn, w, rope):
    wq_d, bqkv_d, wk_d, wv_d, bv_d, wo_d, bo_d = w
    with ExitStack() as ctx:
        def sb(n, shape, dt=F32):
            return ctx.enter_context(nc.sbuf_tensor(f"{name}_{n}", shape, dt))

        sem = ctx.enter_context(semaphore_set(nc, name))

        wq, wk, wv, wo = sb("wq", [D, D]), sb("wk", [D, D]), sb("wv", [D, D]), sb("wo", [D, D])
        bqk = sb("bqk", [D, 2])
        bo = sb("bo", [D, 1])
        bv = sb("bv", [D, D])
        if rope is not None:
            cos, sin, turn = sb("cos", [D, T]), sb("sin", [D, T]), sb("turn", [D, D])
            rc = sb("rc", [D, 2, T])
            rs = sb("rs", [D, 2, T])
        xs = sb("xs", [D, T])
        qk = sb("qk", [D, 2, T])
        qkr = sb("qkr", [D, 2, T])
        parts = sb("parts", [D, 2, SPLIT, T], BF16)
        left = sb("left", [D, 2, T])
        qs = [sb(f"qs{i}", [ROWS, H, T], BF16) for i in range(2)]
        ks = [sb(f"ks{i}", [ROWS, H, T], BF16) for i in range(2)]
        vt = [sb(f"vt{i}", [D, NT, H, VW]) for i in range(2)]
        nmax = sb("nmax", [D, H, NT])
        rows = sb("rows", [H // 2, T])
        rleft = sb("rleft", [H // 2, T])
        rparts = sb("rparts", [H // 2, SPLIT, T], BF16)
        pt = [sb(f"pt{i}", [D, NT, T]) for i in range(2)]
        oe = sb("oe", [D, T])
        rsum = sb("rsum", [D, NT, 4])
        ot = sb("ot", [D, NT, D])
        of = sb("of", [D, T])
        scratch = [nc.dram_tensor(f"{name}_scr{i}", [2, SPLIT, D, T], BF16).ap() for i in range(2)]
        rscratch = [nc.dram_tensor(f"{name}_rscr{i}", [SPLIT, H // 2, T], BF16).ap() for i in range(2)]

        pair = [ctx.enter_context(nc.psum_tensor(f"{name}_pair{i}", [D, 2, T], F32)) for i in range(2)]
        st = [ctx.enter_context(nc.psum_tensor(f"{name}_st{i}", [D, T], F32)) for i in range(2)]
        op = [ctx.enter_context(nc.psum_tensor(f"{name}_o{i}", [D, T], F32)) for i in range(2)]

        loaded_pe, loaded_act, loaded_dve = sem("wpe"), sem("wact"), sem("wdve")
        loaded_pool = sem("wpool")
        xs_ready = sem("xs")
        proj_ready = sem("proj")
        v_ready = sem("vps")
        pair_act = sem("pair_act")
        pair_dve = [sem("pair_dve0"), sem("pair_dve1")]
        qk_pool = sem("qkpool")
        turned = sem("turned")
        sin_ready = sem("sinr")
        qk_split = sem("qksplit")
        pool_step, dve_step = sem("pstep"), sem("dstep")
        scratch_full = sem("scrf")
        qs_full = sem("qsf")
        s_ready = sem("sready")
        rows_ps = sem("rowsps")
        rows_ready = sem("rowsr")
        rows_split = sem("rowss")
        rscratch_full = sem("rscrf")
        rows_full = [sem("rowsf0"), sem("rowsf1")]
        st_ready = sem("stready")
        exp_done = sem("exp")
        pv_done = sem("pv")
        oe_ready = sem("oeready")
        otr_ready = sem("otr")
        of_ps = sem("ofps")
        of_ready = sem("ofr")
        wo_ready = sem("wor")
        ones_ready = sem("ones")
        rows_used = sem("rowsused")
        rparts_free = sem("rpfree")
        block = ctx.enter_context(nc.Block())

        SC = HD ** -0.5

        def program(eng, unit):
            unit(0, 0, None, 1)
            with eng.Fori(0, NB // 2 - 1) as i:
                unit(2 * i + 1, 1, 2 * i, 0)
                unit(2 * i + 2, 0, 2 * i + 1, 1)
            unit(NB - 1, 1, NB - 2, 0)
            unit(None, 0, NB - 1, 1)

        max_slots = {}
        for m in range(H):
            max_slots.setdefault(4 + (m * 12) // H, []).append(m)

        @block.sync
        def _(sp):
            for dst, src in ((wq, wq_d), (wk, wk_d), (wv, wv_d), (wo, wo_d)):
                sp.dma_start(dst[:], src).then_inc(loaded_pe, 16)
            if rope is not None:
                sp.dma_start(turn[:], rope[2]).then_inc(loaded_pe, 16)
                sp.dma_start(sin[:], rope[1]).then_inc(loaded_dve, 16)
                sp.dma_start(cos[:], rope[0]).then_inc(loaded_pool, 16)
            sp.dma_start(bqk[:], bqkv_d).then_inc(loaded_act, 16)
            sp.dma_start(bo[:], bo_d).then_inc(loaded_dve, 16)
            sp.dma_start(bv[:], bv_d.partition_broadcast(D)).then_inc(loaded_dve, 16)

            sp.wait_ge(ones_ready, 1)

            def unit(pb, pp, eb, ep):
                seen = Tally()
                if pb is None:
                    return
                sp.wait_ge(qk_split, seen.next(qk_split))
                for a in range(2):
                    for i in range(SPLIT):
                        sp.dma_start(scratch[pp][a, i], parts[:, a, i, :]).then_inc(scratch_full, 16)
                sp.wait_ge(scratch_full, seen.next(scratch_full, 2 * SPLIT * 16))
                for i in range(SPLIT):
                    for j in range(SPLIT):
                        r = (i * SPLIT + j) * HD
                        sp.dma_start(qs[pp][r:r + HD], scratch[pp][0, i].rearrange("(h e) t -> e h t", e=HD)).then_inc(qs_full, 16)
                        sp.dma_start(ks[pp][r:r + HD], scratch[pp][1, j].rearrange("(h e) t -> e h t", e=HD)).then_inc(qs_full, 16)
                for half in range(2):
                    sp.wait_ge(rows_split, seen.next(rows_split))
                    sp.dma_start(rscratch[half].rearrange("s h t -> h s t"), rparts[:]).then_inc(rscratch_full, 16)
                    sp.wait_ge(rscratch_full, seen.next(rscratch_full, 16))
                    sp.sem_inc(rparts_free, 1)
                    sp.dma_start(qs[pp][KROWS:ROWS, 8 * half:8 * half + 8, :], rscratch[half]).then_inc(rows_full[half], 16)
                seen.settle(sp)

            program(sp, unit)

        @block.gpsimd
        def _(pool):
            if rope is not None:
                pool.wait_ge(loaded_pool, 16)

            def split(seen, src, rest, dst):
                for i in range(SPLIT):
                    last = nc.gpsimd.tensor_copy(dst[i], src if i == 0 else rest)
                    if i < SPLIT - 1:
                        last.then_inc(pool_step, 1)
                        pool.wait_ge(pool_step, seen.next(pool_step))
                        nc.gpsimd.tensor_tensor(rest, src if i == 0 else rest, dst[i], ALU.subtract).then_inc(pool_step, 1)
                        pool.wait_ge(pool_step, seen.next(pool_step))
                return last

            def unit(pb, pp, eb, ep):
                seen = Tally()
                if pb is None:
                    return
                first = eb is None
                src = qk
                pool.wait_ge(qk_pool, seen.next(qk_pool))
                if rope is not None:
                    for a in range(2):
                        nc.gpsimd.tensor_tensor(rc[:, a, :], qk[:, a, :], cos[:], ALU.mult).then_inc(pool_step, 1)
                    pool.wait_ge(pool_step, seen.next(pool_step, 2))
                    pool.wait_ge(sin_ready, seen.next(sin_ready))
                    for a in range(2):
                        nc.gpsimd.tensor_tensor(qkr[:, a, :], rc[:, a, :], rs[:, a, :], ALU.add).then_inc(pool_step, 1)
                    pool.wait_ge(pool_step, seen.next(pool_step, 2))
                    src = qkr
                for a in range(2):
                    last = split(seen, src[:, a, :], left[:, a, :], [parts[:, a, i, :] for i in range(SPLIT)])
                last.then_inc(qk_split, 1)
                for half in range(2):
                    pool.wait_ge(rows_ready, seen.next(rows_ready))
                    if half or not first:
                        pool.wait_ge(rparts_free, seen.next(rparts_free))
                    split(seen, rows[:], rleft[:], [rparts[:, i, :] for i in range(SPLIT)]).then_inc(rows_split, 1)
                    pool.drain().then_inc(rows_used, 1)
                seen.settle(pool)

            program(pool, unit)

        @block.scalar
        def _(act):
            act.wait_ge(loaded_act, 16)

            def unit(pb, pp, eb, ep):
                seen = Tally()
                if pb is not None:
                    nc.scalar.activation(xs[:], xn[:, pb, :], ACT.Copy).then_inc(xs_ready, 1)
                for h in range(H):
                    if pb is not None and h == 0:
                        act.wait_ge(proj_ready, seen.next(proj_ready))
                        nc.scalar.activation(qk[:, 0, :], pair[0][:, 0, :], ACT.Identity, bias=bqk[:, 0:1])
                        nc.scalar.activation(qk[:, 1, :], pair[0][:, 1, :], ACT.Identity, bias=bqk[:, 1:2]).then_inc(qk_pool, 1)
                        act.drain().then_inc(pair_act, 1)
                    if eb is not None:
                        for kt in range(NT):
                            act.wait_ge(st_ready, seen.next(st_ready))
                            if kt == 0 and h >= 2:
                                act.wait_ge(pv_done, h - 1)
                            nc.scalar.activation(pt[h % 2][:, kt, :], st[kt % 2][:], ACT.Exp, scale=SC).then_inc(exp_done, 1)
                        if h % 4 == 0 and h >= 4:
                            act.wait_ge(pv_done, h)
                            nc.scalar.activation(oe[:], op[(h // 4 - 1) % 2][:], ACT.Copy).then_inc(oe_ready, 1)
                    if pb is not None and h == 11:
                        act.wait_ge(rows_ps, seen.next(rows_ps))
                        if eb is not None:
                            act.wait_ge(rows_used, seen.next(rows_used))
                        nc.scalar.activation(rows[:], pair[0][0:H // 2, 0, :], ACT.Copy).then_inc(rows_ready, 1)
                        act.drain().then_inc(pair_act, 1)
                if eb is not None:
                    act.wait_ge(pv_done, seen.next(pv_done, H))
                    nc.scalar.activation(oe[:], op[1][:], ACT.Copy).then_inc(oe_ready, 1)
                if pb is not None:
                    act.wait_ge(rows_ps, seen.next(rows_ps))
                    act.wait_ge(rows_used, seen.next(rows_used))
                    nc.scalar.activation(rows[:], pair[0][0:H // 2, 0, :], ACT.Copy).then_inc(rows_ready, 1)
                    act.drain().then_inc(pair_act, 1)
                if eb is not None:
                    act.wait_ge(of_ps, seen.next(of_ps))
                    nc.scalar.activation(of[:], pair[0][:, 0, :], ACT.Copy).then_inc(of_ready, 1)
                seen.settle(act)

            program(act, unit)

        @block.vector
        def _(v):
            for i in range(2):
                nc.vector.memset(vt[i][:], 0.0).then_inc(dve_step, 1)
                nc.vector.memset(ks[i][64:ROWS], 1.0)
            v.wait_ge(dve_step, 2)
            for i in range(2):
                nc.vector.memset(vt[i][:, :, :, HD:HD + 1], 1.0).then_inc(dve_step, 1)
            v.wait_ge(dve_step, 4)
            v.sem_inc(dve_step, -4)
            v.sem_inc(ones_ready, 1)
            v.wait_ge(loaded_dve, 32 if rope is None else 48)

            def unit(pb, pp, eb, ep):
                seen = Tally()

                def normalise(g):
                    v.wait_ge(otr_ready, seen.next(otr_ready))
                    o = pair[1][:, 0, :].rearrange("p (t r c) -> p t r c", t=NT, r=4)
                    nc.vector.reciprocal(rsum[:], o[:, :, :, HD]).then_inc(dve_step, 1)
                    v.wait_ge(dve_step, seen.next(dve_step))
                    nc.vector.tensor_tensor(ot[:, :, 4 * HD * g:4 * HD * (g + 1)].rearrange("p t (r e) -> p t r e", r=4),
                                            o[:, :, :, 0:HD], rsum[:].unsqueeze(3).to_broadcast([D, NT, 4, HD]),
                                            ALU.mult).then_inc(pair_dve[1], 1)

                for h in range(H):
                    if pb is not None and h == 0:
                        v.wait_ge(v_ready, seen.next(v_ready))
                        for kt in range(NT):
                            last = nc.vector.tensor_tensor(
                                vt[pp][:, kt, :, 0:HD], pair[1][:, 0, 128 * kt:128 * kt + 128].rearrange("p (h e) -> p h e", e=HD),
                                bv[:].rearrange("p (h e) -> p h e", e=HD), ALU.add)
                        last.then_inc(pair_dve[1], 1)
                    if pb is not None and rope is not None and h == 1:
                        v.wait_ge(turned, seen.next(turned))
                        for a in range(2):
                            last = nc.vector.tensor_tensor(rs[:, a, :], pair[1][:, a, :], sin[:], ALU.mult)
                        last.then_inc(sin_ready, 1)
                        v.drain().then_inc(pair_dve[1], 1)
                    if pb is not None:
                        for m in max_slots.get(h, []):
                            for i in range(2):
                                v.wait_ge(s_ready, seen.next(s_ready))
                                nc.vector.tensor_reduce(out=nmax[:, m, 2 * i:2 * i + 2], in_=pair[i][:], op=ALU.max,
                                                        axis=AX.X, negate=True).then_inc(pair_dve[i], 1)
                    if eb is not None and h in (5, 9, 13):
                        normalise(h // 4 - 1)
                if eb is not None:
                    normalise(3)
                    v.wait_ge(wo_ready, seen.next(wo_ready))
                    nc.vector.scalar_tensor_tensor(out=x[:, eb, :], in0=pair[1][:, 0, :], scalar=bo[:, 0:1], in1=x[:, eb, :],
                                                   op0=ALU.add, op1=ALU.add).then_inc(pair_dve[1], 1)
                seen.settle(v)

            program(v, unit)

        @block.tensor
        def _(pe):
            pe.wait_ge(loaded_pe, 64 if rope is None else 80)
            due = {0: None, 1: None}

            def unit(pb, pp, eb, ep):
                seen = Tally()

                def claim(i, released_by):
                    if due[i] is not None:
                        pe.wait_ge(due[i], seen.next(due[i]))
                    due[i] = released_by

                def pv(h):
                    pe.wait_ge(exp_done, 4 * (h + 1))
                    r, bank = h % 4, op[(h // 4) % 2]
                    for kt in range(NT):
                        last = nc.tensor.matmul(bank[32 * r:32 * r + 32, :], vt[ep][:, kt, h, :], pt[h % 2][:, kt, :],
                                                start=(kt == 0), stop=(kt == NT - 1))
                    last.then_inc(pv_done, 1)

                def transposed_output(g):
                    pe.wait_ge(oe_ready, seen.next(oe_ready))
                    claim(1, pair_dve[1])
                    for t in range(NT):
                        last = nc.tensor.transpose(pair[1][:, 0, 128 * t:128 * t + 128], oe[:, 128 * t:128 * t + 128], C["ident"][:])
                    last.then_inc(otr_ready, 1)

                def row_maxima(half):
                    claim(0, pair_act)
                    if due[1] is not None:
                        pe.wait_ge(due[1], seen.next(due[1]))
                        due[1] = None
                    for t in range(NT):
                        last = nc.tensor.transpose(pair[0][0:H // 2, 0, 128 * t:128 * t + 128],
                                                   nmax[:, 8 * half:8 * half + 8, t], C["ident"][:])
                    last.then_inc(rows_ps, 1)

                for h in range(H):
                    if pb is not None and h == 0:
                        pe.wait_ge(xs_ready, seen.next(xs_ready))
                        claim(0, pair_act)
                        nc.tensor.matmul(pair[0][:, 0, :], wq[:], xs[:], start=True, stop=True)
                        nc.tensor.matmul(pair[0][:, 1, :], wk[:], xs[:], start=True, stop=True).then_inc(proj_ready, 1)
                        claim(1, pair_dve[1])
                        for t in range(NT):
                            last = nc.tensor.matmul(pair[1][:, 0, 128 * t:128 * t + 128], xs[:, 128 * t:128 * t + 128], wv[:],
                                                    start=True, stop=True)
                        last.then_inc(v_ready, 1)
                    if pb is not None and rope is not None and h == 1:
                        pe.wait_ge(due[0], seen.next(due[0]))
                        due[0] = None
                        claim(1, pair_dve[1])
                        for a in range(2):
                            last = nc.tensor.matmul(pair[1][:, a, :], turn[:], qk[:, a, :], start=True, stop=True)
                        last.then_inc(turned, 1)
                    if eb is not None:
                        if h % 8 == 0:
                            half = h // 8
                            pe.wait_ge(rows_full[half], seen.next(rows_full[half], 16))
                        for kt in range(NT):
                            n = 4 * h + kt
                            if n >= 2:
                                pe.wait_ge(exp_done, n - 1)
                            nc.tensor.matmul(st[kt % 2][:], ks[ep][0:ROWS, h, 128 * kt:128 * kt + 128], qs[ep][0:ROWS, h, :],
                                             start=True, stop=True).then_inc(st_ready, 1)
                    if pb is not None:
                        for m in max_slots.get(h, []):
                            if m == 0:
                                pe.wait_ge(qs_full, seen.next(qs_full, 2 * SPLIT * SPLIT * 16))
                            for i in range(2):
                                claim(i, pair_dve[i])
                                for j in range(2):
                                    q0 = 128 * (2 * i + j)
                                    last = nc.tensor.matmul(pair[i][:, j, :], qs[pp][0:KROWS, m, q0:q0 + 128],
                                                            ks[pp][0:KROWS, m, :], start=True, stop=True)
                                last.then_inc(s_ready, 1)
                        if h == 10:
                            row_maxima(0)
                    if eb is not None and h >= 1:
                        pv(h - 1)
                    if eb is not None and h in (5, 9, 13):
                        transposed_output(h // 4 - 1)
                if eb is not None:
                    pv(H - 1)
                    seen.next(exp_done, 4 * H)
                if pb is not None:
                    row_maxima(1)
                if eb is not None:
                    transposed_output(3)
                    claim(0, None)
                    pe.wait_ge(due[1], seen.next(due[1]))
                    due[1] = None
                    for t in range(NT):
                        last = nc.tensor.transpose(pair[0][:, 0, 128 * t:128 * t + 128], ot[:, t, :], C["ident"][:])
                    last.then_inc(of_ps, 1)
                    pe.wait_ge(of_ready, seen.next(of_ready))
                    claim(1, pair_dve[1])
                    nc.tensor.matmul(pair[1][:, 0, :], wo[:], of[:], start=True, stop=True).then_inc(wo_ready, 1)
                for i in range(2):
                    if due[i] is not None:
                        pe.wait_ge(due[i], seen.next(due[i]))
                        due[i] = None
                seen.settle(pe)

            program(pe, unit)


def local_stack(nc, C, xs, A):
    with ExitStack() as ctx:
        def sb(n, shape, dt=F32):
            return ctx.enter_context(nc.sbuf_tensor(f"l_{n}", shape, dt))

        sem = ctx.enter_context(semaphore_set(nc, "l"))

        wqkv, wo, w1, w2 = sb("wqkv", [D, 3 * INNER]), sb("wo", [D, INNER // D, D]), sb("w1", [D, 2 * DI]), sb("w2", [D, 3, D])
        vec = sb("vec", [D, NVEC])
        vec_act = sb("vec_act", [D, NVEC])
        tab = sb("tab", [D, 4, T])
        mask = sb("mask", [D, 2, T], BF16)
        ident16 = sb("ident16", [D, D], BF16)
        block4 = sb("block4", [D, CH])
        xc = sb("xc", [D, T])
        t = [sb(f"t{i}", [D, T]) for i in range(4)]
        u = [[sb(f"u{p}{i}", [D, T]) for i in range(4)] for p in range(2)]
        sq = [sb(f"sq{a}", [D, 2, T]) for a in range(2)]
        sqs = [sb(f"sqs{a}", [D, T]) for a in range(2)]
        qn = [sb(f"qn{i}", [D, T]) for i in range(2)]
        kn = [sb(f"kn{i}", [D, T]) for i in range(2)]
        kbd = [sb(f"kbd{i}", [D, CH, KC]) for i in range(2)]
        norm = sb("norm", [D, NT * 2 * CH + NT])
        ntmp = sb("ntmp", [D, NT * 2 * CH + NT])
        rn = sb("rn", [D, NT * 2 * CH + NT])
        NSS = NT * 2 * CH
        rnx = sb("rnx", [D, NSS, HALF])
        p = sb("p", [D, NT * CH, 2 * WIN])
        pn = sb("pn", [D, NT * CH, 2 * WIN])
        pt = sb("pt", [D, NT * CH * 2 * WIN])
        smax = sb("smax", [D, NT * CH])
        ssum = sb("ssum", [D, NT * CH])
        srec = sb("srec", [D, NT * CH])
        pbd = sb("pbd", [D, 4, NT * CH * 2 * WIN])
        va = [sb(f"va{c}", [D, NT, CH * DH]) for c in range(NC)]
        vp = [sb(f"vp{c}", [D, NT, CH * DH]) for c in range(NC)]
        ot = sb("ot", [D, INNER // D, T])
        xcn, fsq = sb("xcn", [D, T]), sb("fsq", [D, T])
        xng = fsq
        xnf = sb("xnf", [D, T])
        hid = [sb(f"hid{i}", [D, T]) for i in range(3)]

        R = [ctx.enter_context(nc.psum_tensor(f"l_r{i}", [D, 2, T], F32)) for i in range(4)]

        names = ("w_pe w_act w_dve consts_pe consts_dve layer_done xc_ready q_dve q_act k_dve k_act v_act sq_free "
                 "r2_act r0_dve r1_dve r3_dve rq_ready ra_ready sq_sum ss_ready rn_ready rnx_ready b_ready r0_dve_b "
                 "qn_ready kn_ready kbd_full s_ready t_ready p_ready rec_ready pn_ready pt_ready pt_free pbd_free pbd_full "
                 "va_ready vp_full pv_ready ot_ready wo_ready x_ready mean_ready centred fsq_ready bc_ready xng_ready "
                 "xnf_ready g_ready a_ready gelu_ready h_ready f_ready ffn_done step pstep init mask_full").split()
        S = {n: sem(n) for n in names}
        block = ctx.enter_context(nc.Block())

        def layers(eng, body):
            with eng.Fori(0, DEPTH) as l:
                body(l, 0, None)
                with eng.Fori(1, NB) as b:
                    body(l, b, b - 1)
                body(l, None, NB - 1)

        def live(c, lag, b, prev):
            return b is not None if c >= lag else prev is not None

        @block.sync
        def _(sp):
            sp.dma_start(pn[:].rearrange("p a b -> p (a b)"), A["mask"]).then_inc(S["mask_full"], 16)
            sp.dma_start(block4[:], A["block4"]).then_inc(S["consts_pe"], 16)
            sp.dma_start(tab[:], A["tab"]).then_inc(S["consts_dve"], 16)

            def body(l, b, prev):
                seen = Tally()
                if prev is None:
                    sp.wait_ge(S["layer_done"], seen.next(S["layer_done"]))
                    sp.dma_start(wqkv[:], A["wqkv"][l]).then_inc(S["w_pe"], 16)
                    sp.dma_start(wo[:], A["wo"][l]).then_inc(S["w_pe"], 16)
                    sp.dma_start(w1[:], A["w1"][l]).then_inc(S["w_pe"], 16)
                    sp.dma_start(w2[:], A["w2"][l]).then_inc(S["w_pe"], 16)
                    sp.dma_start(vec[:], A["vec"][l]).then_inc(S["w_dve"], 16)
                    sp.dma_start(vec_act[:], A["vec"][l]).then_inc(S["w_act"], 16)
                for c in range(NC):
                    if live(c, 3, b, prev):
                        sp.wait_ge(S["pbd_free"], seen.next(S["pbd_free"]))
                        sp.sem_inc(S["pt_free"], 1)
                        sp.wait_ge(S["pt_ready"], seen.next(S["pt_ready"]))
                        for w in range(4):
                            q = slice(32 * w, 32 * w + 32)
                            sp.dma_start(pbd[q, w, :], pt[q, :]).then_inc(S["pbd_full"], 16)
                    if b is not None:
                        sp.wait_ge(S["va_ready"], seen.next(S["va_ready"]))
                        sp.dma_start(vp[c][32:128], va[c][0:96]).then_inc(S["vp_full"], 16)
                        sp.dma_start(vp[c][0:32, 1:NT, :], va[c][96:128, 0:NT - 1, :]).then_inc(S["vp_full"], 16)
                    if live(c, 1, b, prev):
                        sp.wait_ge(S["kn_ready"], seen.next(S["kn_ready"]))
                        for i in range(2):
                            for r in range(CH):
                                q = slice(32 * r, 32 * r + 32)
                                sp.dma_start(kbd[i][q, r, WIN:KC], kn[i][q, :]).then_inc(S["kbd_full"], 16)
                seen.settle(sp)

            layers(sp, body)

        @block.gpsimd
        def _(pool):
            def body(l, b, prev):
                seen = Tally()
                for c in range(NC):
                    par = c % 2
                    if b is not None:
                        for a in range(2):
                            pool.wait_ge(S["rq_ready"], seen.next(S["rq_ready"]))
                            nc.gpsimd.tensor_tensor(u[par][2 * a][:], t[0][:], t[1][:], ALU.subtract)
                            nc.gpsimd.tensor_tensor(u[par][2 * a + 1][:], t[2][:], t[3][:], ALU.add).then_inc(S["ra_ready"], 1)
                        nc.gpsimd.tensor_tensor(sqs[0][:], sq[0][:, 0, :], sq[0][:, 1, :], ALU.add)
                        nc.gpsimd.tensor_tensor(sqs[1][:], sq[1][:, 0, :], sq[1][:, 1, :], ALU.add).then_inc(S["sq_sum"], 1)
                        pool.drain().then_inc(S["sq_free"], 1)
                    if live(c, 2, b, prev):
                        pool.wait_ge(S["rec_ready"], seen.next(S["rec_ready"]))
                        nc.gpsimd.tensor_tensor(pn[:], p[:], srec[:].unsqueeze(2).to_broadcast([D, NT * CH, 2 * WIN]),
                                                ALU.mult).then_inc(S["pn_ready"], 1)
                seen.settle(pool)

            layers(pool, body)

        @block.scalar
        def _(act):
            act.sem_inc(S["sq_free"], 1)

            def body(l, b, prev):
                seen = Tally()
                if prev is None:
                    act.wait_ge(S["w_act"], seen.next(S["w_act"], 16))
                if b is not None:
                    nc.scalar.activation(xc[:], xs[:, b, 0:T], ACT.Copy).then_inc(S["xc_ready"], 1)
                for c in range(NC):
                    if b is not None:
                        act.wait_ge(S["sq_free"], seen.next(S["sq_free"]))
                        act.wait_ge(S["q_act"], seen.next(S["q_act"]))
                        nc.scalar.activation(sq[0][:], R[0][:], ACT.Square).then_inc(S["q_dve"], 1)
                        act.wait_ge(S["k_act"], seen.next(S["k_act"]))
                        nc.scalar.activation(sq[1][:], R[1][:], ACT.Square).then_inc(S["k_dve"], 1)
                        act.wait_ge(S["v_act"], seen.next(S["v_act"]))
                        nc.scalar.activation(va[c][:], R[2][:].rearrange("p a (k f) -> p (a k) f", k=2), ACT.Copy).then_inc(S["va_ready"], 1)
                        act.drain().then_inc(S["r2_act"], 1)
                    if live(c, 1, b, prev) or (c == 3 and prev is not None):
                        act.wait_ge(S["rn_ready"], seen.next(S["rn_ready"]))
                        if live(c, 1, b, prev):
                            nc.scalar.activation(rnx[:], rn[:, 0:NSS].unsqueeze(2).to_broadcast([D, NSS, HALF]), ACT.Copy)\
                                .then_inc(S["rnx_ready"], 1)
                        else:
                            act.sem_inc(S["rnx_ready"], 1)
                    if live(c, 2, b, prev):
                        act.wait_ge(S["t_ready"], seen.next(S["t_ready"]))
                        nc.scalar.activation(p[:], p[:], ACT.Exp, scale=QK_SCALE).then_inc(S["p_ready"], 1)
                    if c == 3 and prev is not None:
                        act.wait_ge(S["xng_ready"], seen.next(S["xng_ready"]))
                        nc.scalar.activation(xnf[:], xng[:], ACT.Identity, bias=vec_act[:, 9:10]).then_inc(S["xnf_ready"], 1)
                    if live(c, 3, b, prev):
                        act.wait_ge(S["pv_ready"], seen.next(S["pv_ready"]))
                        cc = (c - 3) % NC
                        nc.scalar.activation(ot[:, 2 * cc:2 * cc + 2, :], R[1][:], ACT.Copy).then_inc(S["ot_ready"], 1)
                    if c == 2 and prev is not None:
                        act.wait_ge(S["centred"], seen.next(S["centred"]))
                        nc.scalar.activation(fsq[:], xcn[:], ACT.Square).then_inc(S["fsq_ready"], 1)
                    if c == 3 and prev is not None:
                        for i, n in enumerate(FCH):
                            act.wait_ge(S["g_ready"], seen.next(S["g_ready"]))
                            nc.scalar.activation(hid[i][0:n, :], R[(2, 3, 0)[i]][0:n, 0, :], ACT.Gelu,
                                                 bias=vec_act[0:n, 10 + i:11 + i]).then_inc(S["gelu_ready"], 1)
                seen.settle(act)

            layers(act, body)

        @block.vector
        def _(v):
            v.wait_ge(S["mask_full"], 16)
            nc.vector.tensor_copy(mask[:], pn[:].rearrange("p a b -> p (a b)").rearrange("p (a b) -> p a b", a=2))
            nc.vector.tensor_copy(ident16[:], C["ident"][:])
            for i in range(2):
                nc.vector.memset(kbd[i][:], 0.0)
            nc.vector.memset(pbd[:], 0.0)
            for c in range(NC):
                nc.vector.memset(vp[c][:], 0.0)
            v.drain().then_inc(S["init"], 1)
            v.wait_ge(S["consts_dve"], 16)
            unread = {"ra": 0}

            def body(l, b, prev):
                seen = Tally()
                if prev is None:
                    v.wait_ge(S["w_dve"], seen.next(S["w_dve"], 16))

                def halves_of_pool():
                    if unread["ra"]:
                        v.wait_ge(S["ra_ready"], seen.next(S["ra_ready"]))
                        unread["ra"] = 0

                def rotate(a):
                    halves_of_pool()
                    src, cos, sin = R[a], tab[:, 2 * a, :], tab[:, 2 * a + 1, :]
                    for i, (half, table) in enumerate(((0, cos), (1, sin), (1, cos), (0, sin))):
                        last = nc.vector.scalar_tensor_tensor(out=t[i][:], in0=src[:, half, :], scalar=vec[:, 2 * a + half:2 * a + half + 1],
                                                              in1=table, op0=ALU.mult, op1=ALU.mult)
                    last.then_inc(S["rq_ready"], 1)
                    unread["ra"] = 1
                    v.drain().then_inc(S["r0_dve"] if a == 0 else S["r1_dve"], 1)

                for c in range(NC):
                    par1 = (c - 1) % 2
                    if b is not None:
                        v.wait_ge(S["q_dve"], seen.next(S["q_dve"]))
                        rotate(0)
                    if live(c, 3, b, prev):
                        v.wait_ge(S["pt_free"], seen.next(S["pt_free"]))
                        v.wait_ge(S["pn_ready"], seen.next(S["pn_ready"]))
                        nc.vector.transpose(pt[:], pn[:].rearrange("p a b -> p (a b)")).then_inc(S["pt_ready"], 1)
                    has_ss, has_var = live(c, 1, b, prev), c == 3 and prev is not None
                    if has_ss or has_var:
                        v.wait_ge(S["ss_ready"], seen.next(S["ss_ready"]))
                        lo, hi = (0 if has_ss else NSS), (NSS + NT if has_var else NSS)
                        if has_ss:
                            nc.vector.tensor_scalar(norm[:, 0:NSS], R[3][:, 0, 0:NSS], 1e-24, None, ALU.max).then_inc(S["step"], 1)
                            v.wait_ge(S["step"], seen.next(S["step"]))
                        if has_var:
                            nc.vector.tensor_scalar(norm[:, NSS:], R[3][:, 1, 0:NT], LN_EPS, None, ALU.add).then_inc(S["step"], 1)
                            v.wait_ge(S["step"], seen.next(S["step"]))
                        rsqrt(nc, v, seen, S["step"], norm[:, lo:hi], ntmp[:, lo:hi], rn[:, lo:hi]).then_inc(S["rn_ready"], 1)
                    if b is not None:
                        v.wait_ge(S["k_dve"], seen.next(S["k_dve"]))
                        rotate(1)
                    if live(c, 2, b, prev):
                        v.wait_ge(S["s_ready"], seen.next(S["s_ready"]))
                        sc = R[3][:].rearrange("p a b -> p (a b)").rearrange("p (u k) -> p u k", k=2 * WIN)
                        nc.vector.tensor_reduce(out=smax[:], in_=sc, op=ALU.max, axis=AX.X).then_inc(S["step"], 1)
                        v.wait_ge(S["step"], seen.next(S["step"]))
                        nc.vector.tensor_tensor(p[:], sc, smax[:].unsqueeze(2).to_broadcast([D, NT * CH, 2 * WIN]),
                                                ALU.subtract).then_inc(S["t_ready"], 1)
                        v.drain().then_inc(S["r3_dve"], 1)
                    if has_ss:
                        v.wait_ge(S["b_ready"], seen.next(S["b_ready"]))
                        halves_of_pool()
                        for i in range(2):
                            last = nc.vector.tensor_tensor(qn[i][:], u[par1][i][:], R[0][:, 0, :], ALU.mult)
                        last.then_inc(S["qn_ready"], 1)
                        for i in range(2):
                            last = nc.vector.tensor_tensor(kn[i][:], u[par1][2 + i][:], R[0][:, 1, :], ALU.mult)
                        last.then_inc(S["kn_ready"], 1)
                        v.drain().then_inc(S["r0_dve_b"], 1)
                    if has_var:
                        v.wait_ge(S["bc_ready"], seen.next(S["bc_ready"]))
                        nc.vector.scalar_tensor_tensor(out=xng[:], in0=xcn[:], scalar=vec[:, 4:5], in1=R[2][:, 0, :],
                                                       op0=ALU.mult, op1=ALU.mult).then_inc(S["xng_ready"], 1)
                    if live(c, 2, b, prev):
                        v.wait_ge(S["p_ready"], seen.next(S["p_ready"]))
                        nc.vector.tensor_reduce(out=ssum[:], in_=p[:], op=ALU.add, axis=AX.X).then_inc(S["step"], 1)
                        v.wait_ge(S["step"], seen.next(S["step"]))
                        nc.vector.reciprocal(srec[:], ssum[:]).then_inc(S["rec_ready"], 1)
                    if c == 2 and prev is not None:
                        v.wait_ge(S["wo_ready"], seen.next(S["wo_ready"]))
                        nc.vector.tensor_tensor(xs[0:64, prev, 0:T], xs[0:64, prev, 0:T], R[2][0:64, 0, :], ALU.add).then_inc(S["step"], 1)
                        nc.vector.tensor_tensor(xs[64:128, prev, 1:T + 1], xs[64:128, prev, 1:T + 1], R[2][64:128, 0, :],
                                                ALU.add).then_inc(S["x_ready"], 1)
                        v.wait_ge(S["step"], seen.next(S["step"]))
                        v.wait_ge(S["mean_ready"], seen.next(S["mean_ready"]))
                        nc.vector.tensor_tensor(xcn[:], xs[:, prev, 0:T], R[2][:, 1, :], ALU.subtract).then_inc(S["centred"], 1)
                    if c == 3:
                        if prev is not None:
                            for i, n in enumerate(FCH):
                                v.wait_ge(S["a_ready"], seen.next(S["a_ready"]))
                                v.wait_ge(S["gelu_ready"], seen.next(S["gelu_ready"]))
                                nc.vector.scalar_tensor_tensor(out=hid[i][0:n, :], in0=R[(2, 3, 0)[i]][0:n, 1, :],
                                                               scalar=vec[0:n, 5 + i:6 + i], in1=hid[i][0:n, :],
                                                               op0=ALU.add, op1=ALU.mult).then_inc(S["h_ready"], 1)
                            v.wait_ge(S["f_ready"], seen.next(S["f_ready"]))
                            nc.vector.scalar_tensor_tensor(out=xs[0:64, prev, 0:T], in0=R[2][0:64, 0, :], scalar=vec[0:64, 8:9],
                                                           in1=xs[0:64, prev, 0:T], op0=ALU.add, op1=ALU.add)
                            nc.vector.scalar_tensor_tensor(out=xs[64:128, prev, 1:T + 1], in0=R[2][64:128, 0, :], scalar=vec[64:128, 8:9],
                                                           in1=xs[64:128, prev, 1:T + 1], op0=ALU.add, op1=ALU.add).then_inc(S["ffn_done"], 1)
                        else:
                            v.sem_inc(S["ffn_done"], 1)
                seen.settle(v)

            layers(v, body)

        @block.tensor
        def _(pe):
            pe.sem_inc(S["pbd_free"], 1)
            pe.wait_ge(S["init"], 1)
            pe.wait_ge(S["consts_pe"], 16)
            pe.sem_inc(S["layer_done"], 1)
            due = {0: [], 1: [], 2: [], 3: []}

            def body(l, b, prev):
                seen = Tally()
                if prev is None:
                    pe.wait_ge(S["w_pe"], seen.next(S["w_pe"], 64))

                def read(i):
                    for n in due[i]:
                        pe.wait_ge(S[n], seen.next(S[n]))
                    due[i] = []

                def claim(i, *released_by):
                    read(i)
                    due[i] = list(released_by)

                for c in range(NC):
                    pv_before = live(c - 1, 3, b, prev) if c else prev is not None
                    if b is not None:
                        claim(0, "r0_dve")
                        for half in range(2):
                            o = 2 * D * c + D * half
                            last = nc.tensor.matmul(R[0][:, half, :], wqkv[:, o:o + D], xs[:, b, 0:T], start=True, stop=True)
                            if half == 0 and pv_before:
                                last.then_inc(S["pbd_free"], 1)
                        last.then_inc(S["q_act"], 1)
                        claim(1, "r1_dve")
                        for half in range(2):
                            o = INNER + 2 * D * c + D * half
                            last = nc.tensor.matmul(R[1][:, half, :], wqkv[:, o:o + D], xs[:, b, 0:T], start=True, stop=True)
                        last.then_inc(S["k_act"], 1)
                    elif pv_before:
                        pe.drain().then_inc(S["pbd_free"], 1)
                    has_ss, has_var = live(c, 1, b, prev), c == 3 and prev is not None
                    if has_ss or has_var:
                        claim(3)
                        if has_ss:
                            pe.wait_ge(S["sq_sum"], seen.next(S["sq_sum"]))
                            for k in range(NT):
                                for a in range(2):
                                    o = (k * 2 + a) * CH
                                    last = nc.tensor.matmul(R[3][:, 0, o:o + CH], sqs[a][:, 128 * k:128 * k + 128], block4[:],
                                                            start=True, stop=True)
                        if has_var:
                            pe.wait_ge(S["fsq_ready"], seen.next(S["fsq_ready"]))
                            for k in range(NT):
                                last = nc.tensor.matmul(R[3][:, 1, k:k + 1], fsq[:, 128 * k:128 * k + 128], C["inv"][:, 0:1],
                                                        start=True, stop=True)
                        last.then_inc(S["ss_ready"], 1)
                        due[3] = ["rnx_ready"]
                    if b is not None:
                        if c == 0:
                            pe.wait_ge(S["xc_ready"], seen.next(S["xc_ready"]))
                        claim(2, "r2_act")
                        for k in range(NT):
                            o = 2 * INNER + CH * DH * c
                            last = nc.tensor.matmul(R[2][:, k // 2, 256 * (k % 2):256 * (k % 2) + 256], xc[:, 128 * k:128 * k + 128],
                                                    wqkv[:, o:o + CH * DH], start=True, stop=True)
                        last.then_inc(S["v_act"], 1)
                    if live(c, 2, b, prev):
                        claim(3, "r3_dve")
                        pe.wait_ge(S["qn_ready"], seen.next(S["qn_ready"]))
                        pe.wait_ge(S["kbd_full"], seen.next(S["kbd_full"], 2 * CH * 16))
                        for bank in range(2):
                            nc.tensor.matmul(R[3][:, bank, :], ident16[:], mask[:, bank, :], start=True, stop=False, skip_group_check=True)
                            for w in range(8):
                                W, q = 8 * bank + w, 32 * (w % 4)
                                for half in range(2):
                                    last = nc.tensor.matmul(R[3][q:q + 32, bank, 256 * (w // 4):256 * (w // 4) + 256],
                                                            qn[half][:, WIN * W:WIN * W + WIN], kbd[half][:, :, WIN * W:WIN * W + 2 * WIN],
                                                            start=False, stop=(half == 1), skip_group_check=True)
                        last.then_inc(S["s_ready"], 1)
                    if has_ss or has_var:
                        if due[3] == ["rnx_ready"]:
                            read(3)
                    if has_ss:
                        claim(0, "r0_dve_b")
                        for a in range(2):
                            for k in range(NT):
                                o = (k * 2 + a) * CH
                                last = nc.tensor.transpose(R[0][:, a, 128 * k:128 * k + 128],
                                                           rnx[:, o:o + CH, :].rearrange("p h i -> p (h i)"), C["ident"][:])
                        last.then_inc(S["b_ready"], 1)
                    if has_var:
                        claim(2)
                        for k in range(NT):
                            last = nc.tensor.transpose(R[2][:, 0, 128 * k:128 * k + 128], rn[:, NSS + k:NSS + k + 1].to_broadcast([D, D]),
                                                       C["ident"][:])
                        last.then_inc(S["bc_ready"], 1)
                    if live(c, 3, b, prev):
                        claim(1, "ot_ready")
                        cc = (c - 3) % NC
                        pe.wait_ge(S["vp_full"], seen.next(S["vp_full"], 32))
                        pe.wait_ge(S["pbd_full"], seen.next(S["pbd_full"], 64))
                        for h in range(CH):
                            q = 64 * (h % 2)
                            for g in range(NT):
                                for half, vv in enumerate((vp[cc], va[cc])):
                                    o = ((g * CH + h) * 2 + half) * WIN
                                    last = nc.tensor.matmul(R[1][q:q + 64, h // 2, 128 * g:128 * g + 128], vv[:, g, DH * h:DH * h + DH],
                                                            pbd[:, :, o:o + WIN], start=(half == 0), stop=(half == 1))
                        last.then_inc(S["pv_ready"], 1)
                    if c == 2 and prev is not None:
                        read(1)
                        claim(2)
                        for j in range(INNER // D):
                            last = nc.tensor.matmul(R[2][:, 0, :], wo[:, j, :], ot[:, j, :], start=(j == 0), stop=(j == INNER // D - 1))
                        last.then_inc(S["wo_ready"], 1)
                        pe.wait_ge(S["x_ready"], seen.next(S["x_ready"]))
                        nc.tensor.matmul(R[2][:, 1, :], C["inv"][:], xs[:, prev, 0:T], start=True, stop=True).then_inc(S["mean_ready"], 1)
                    if c == 3 and prev is not None:
                        pe.wait_ge(S["xnf_ready"], seen.next(S["xnf_ready"]))
                        o = 0
                        for i, n in enumerate(FCH):
                            r = R[(2, 3, 0)[i]]
                            claim((2, 3, 0)[i])
                            nc.tensor.matmul(r[0:n, 0, :], w1[:, DI + o:DI + o + n], xnf[:], start=True, stop=True).then_inc(S["g_ready"], 1)
                            nc.tensor.matmul(r[0:n, 1, :], w1[:, o:o + n], xnf[:], start=True, stop=True).then_inc(S["a_ready"], 1)
                            o += n
                        for i, n in enumerate(FCH):
                            pe.wait_ge(S["h_ready"], seen.next(S["h_ready"]))
                            last = nc.tensor.matmul(R[2][:, 0, :], w2[0:n, i, :], hid[i][0:n, :], start=(i == 0), stop=(i == 2))
                        last.then_inc(S["f_ready"], 1)
                        due[2] = ["ffn_done"]
                    if c == 3 and prev is None:
                        for i in (0, 2, 3):
                            read(i)
                        due[2] = ["ffn_done"]
                if b is None:
                    for i in range(4):
                        read(i)
                    pe.drain().then_inc(S["layer_done"], 1)
                seen.settle(pe)

            layers(pe, body)


def gated_mix_pass(nc, C, x, xn, wr_d, wk_d, wv_d, mu_d, out):
    with ExitStack() as ctx:
        def sb(n, shape, dt=F32):
            return ctx.enter_context(nc.sbuf_tensor(f"d_{n}", shape, dt))

        sem = ctx.enter_context(semaphore_set(nc, "d"))

        wr, wk, wv = sb("wr", [D, D]), sb("wk", [D, D]), sb("wv", [D, D])
        mu, comu = sb("mu", [D, 2]), sb("comu", [D, 2])
        prev = [[sb(f"prev{p}{a}", [D, T]) for a in range(2)] for p in range(2)]
        mix = [[sb(f"mix{p}{a}", [D, T]) for a in range(2)] for p in range(2)]
        gate = [sb(f"gate{p}", [D, T]) for p in range(2)]
        act_k = [sb(f"act_k{p}", [D, T]) for p in range(2)]
        res = [sb(f"res{p}", [D, T]) for p in range(2)]
        r_ps, k_ps, v_ps = ([ctx.enter_context(nc.psum_tensor(f"d_{n}{p}", [D, T], F32)) for p in range(2)] for n in "rkv")
        w_pe, w_dve, comu_ready = sem("wpe"), sem("wdve"), sem("comu")
        prev_ready, mix_ready, r_ready, k_ready = sem("prev"), sem("mix"), sem("r"), sem("k")
        relu_ready, sq_ready, v_ready, out_ready = sem("relu"), sem("sqr"), sem("v"), sem("out")
        stored, res_free, step = sem("stored"), sem("resfree"), sem("step")
        block = ctx.enter_context(nc.Block())

        @block.sync
        def _(sp):
            for dst, src in ((wr, wr_d), (wk, wk_d), (wv, wv_d)):
                sp.dma_start(dst[:], src).then_inc(w_pe, 16)
            sp.dma_start(mu[:], mu_d).then_inc(w_dve, 16)
            with sp.Fori(0, NB // 2) as i:
                for p in range(2):
                    sp.wait_ge(out_ready, p + 1)
                    sp.dma_start(out[:, 2 * i + p, :], res[p][:]).then_inc(stored, 16)
                sp.sem_inc(out_ready, -2)
                sp.wait_ge(stored, 32)
                sp.sem_inc(stored, -32)
                sp.sem_inc(res_free, 1)

        @block.scalar
        def _(act):
            act.wait_ge(comu_ready, 1)
            with act.Fori(0, NB // 2) as i:
                for p in range(2):
                    for a in range(2):
                        last = nc.scalar.activation(prev[p][a][:], xn[:, 2 * i + p, 0:T], ACT.Copy, scale=comu[:, a:a + 1])
                    last.then_inc(prev_ready, 1)
                for p in range(2):
                    act.wait_ge(r_ready, p + 1)
                    nc.scalar.activation(gate[p][:], r_ps[p][:], ACT.Sigmoid)
                    act.wait_ge(k_ready, p + 1)
                    nc.scalar.activation(act_k[p][:], k_ps[p][:], ACT.Relu).then_inc(relu_ready, 1)
                act.sem_inc(r_ready, -2)
                act.sem_inc(k_ready, -2)

        @block.vector
        def _(v):
            v.sem_inc(res_free, 1)
            v.wait_ge(w_dve, 16)
            nc.vector.tensor_scalar(comu[:], mu[:], -1.0, 1.0, ALU.mult, ALU.add).then_inc(comu_ready, 1)
            with v.Fori(0, NB // 2) as i:
                for p in range(2):
                    v.wait_ge(prev_ready, p + 1)
                    for a in range(2):
                        last = nc.vector.scalar_tensor_tensor(out=mix[p][a][:], in0=xn[:, 2 * i + p, 1:T + 1], scalar=mu[:, a:a + 1],
                                                              in1=prev[p][a][:], op0=ALU.mult, op1=ALU.add)
                    last.then_inc(mix_ready, 1)
                for p in range(2):
                    v.wait_ge(relu_ready, p + 1)
                    nc.vector.tensor_tensor(act_k[p][:], act_k[p][:], act_k[p][:], ALU.mult).then_inc(sq_ready, 1)
                v.wait_ge(res_free, 1)
                for p in range(2):
                    v.wait_ge(v_ready, p + 1)
                    nc.vector.tensor_tensor(res[p][:], v_ps[p][:], gate[p][:], ALU.mult).then_inc(step, 1)
                for p in range(2):
                    v.wait_ge(step, p + 1)
                    nc.vector.tensor_tensor(res[p][:], res[p][:], x[:, 2 * i + p, :], ALU.add).then_inc(out_ready, 1)
                for s, n in ((prev_ready, 2), (relu_ready, 2), (res_free, 1), (v_ready, 2), (step, 2)):
                    v.sem_inc(s, -n)

        @block.tensor
        def _(pe):
            pe.wait_ge(w_pe, 48)
            with pe.Fori(0, NB // 2) as i:
                for p in range(2):
                    pe.wait_ge(mix_ready, p + 1)
                    nc.tensor.matmul(r_ps[p][:], wr[:], mix[p][0][:], start=True, stop=True).then_inc(r_ready, 1)
                    nc.tensor.matmul(k_ps[p][:], wk[:], mix[p][1][:], start=True, stop=True).then_inc(k_ready, 1)
                for p in range(2):
                    pe.wait_ge(sq_ready, p + 1)
                    nc.tensor.matmul(v_ps[p][:], wv[:], act_k[p][:], start=True, stop=True).then_inc(v_ready, 1)
                pe.sem_inc(mix_ready, -2)
                pe.sem_inc(sq_ready, -2)


def make_constants(nc, C):
    with ExitStack() as ctx:
        step = ctx.enter_context(semaphore_set(nc, "const"))("step")
        block = ctx.enter_context(nc.Block())

        @block.gpsimd
        def _(pool):
            nc.gpsimd.memset(C["ident"][:], 0.0).then_inc(step, 1)
            nc.gpsimd.memset(C["inv"][:], 1.0 / D)
            pool.wait_ge(step, 1)
            nc.gpsimd.affine_select(out=C["ident"][:], in_=C["ident"][:], compare_op=ALU.not_equal, fill=1.0, base=0,
                                    pattern=[[-1, D]], channel_multiplier=1)


def run_in_block(nc, name, engine, work):
    with ExitStack() as ctx:
        done = ctx.enter_context(semaphore_set(nc, name))("done")
        block = ctx.enter_context(nc.Block())
        if engine == "sync":
            @block.sync
            def _(eng):
                work(eng, done)
        else:
            @block.vector
            def _(eng):
                work(eng, done)


def model(nc, A, out):
    with ExitStack() as ctx:
        C = {"ident": ctx.enter_context(nc.sbuf_tensor("ident", [D, D], F32)),
             "inv": ctx.enter_context(nc.sbuf_tensor("inv", [D, D], F32))}
        make_constants(nc, C)
        x_in = A["x"].rearrange("d (b t) -> d b t", b=NB)
        x_out = out.rearrange("d (b t) -> d b t", b=NB)
        x_kept = nc.dram_tensor("x_kept", [D, NB, T], F32).ap()
        xs = ctx.enter_context(nc.sbuf_tensor("xs", [D, NB, T + 1], F32))

        def copy(name, dst, src):
            def work(sp, done):
                sp.dma_start(dst, src).then_inc(done, 16)
                sp.wait_ge(done, 16)
            run_in_block(nc, name, "sync", work)

        def skewed(b):
            return [(slice(0, 64), xs[0:64, b, 0:T]), (slice(64, 128), xs[64:128, b, 1:T + 1])]

        def attend(name, x, w, rope):
            with ExitStack() as c1:
                xn = c1.enter_context(nc.sbuf_tensor(f"{name}_xn", [D, NB, T], F32))
                layernorm_pass(nc, f"{name}_ln", C, x, lambda b: [(slice(0, D), xn[:, b, :])])
                attention_pass(nc, name, C, x, xn, w, rope)

        with ExitStack() as c1:
            x = c1.enter_context(nc.sbuf_tensor("x_first", [D, NB, T], F32))
            copy("load", x[:], x_in)
            attend("a0", x, [A[k] for k in ("L0_wq", "L0_bqk", "L0_wk", "L0_wv", "L0_bv", "L0_wo", "L0_bo")], None)
            layernorm_pass(nc, "b_ln", C, x, skewed)
            copy("keep", x_kept, x[:])

        def zero_before(v, done):
            nc.vector.memset(xs[64:128, :, 0:1], 0.0).then_inc(done, 1)
            v.wait_ge(done, 1)

        run_in_block(nc, "zero_before", "vector", zero_before)
        local_stack(nc, C, xs, A)

        x = ctx.enter_context(nc.sbuf_tensor("x_second", [D, NB, T], F32))
        copy("fetch", x[:], x_kept)

        def add_stack(v, done):
            for b in range(NB):
                for q, y in skewed(b):
                    nc.vector.tensor_tensor(x[q, b, :], x[q, b, :], y, ALU.add).then_inc(done, 1)
            v.wait_ge(done, 2 * NB)

        run_in_block(nc, "add_stack", "vector", add_stack)
        attend("a1", x, [A[k] for k in ("L1_wq", "L1_bqk", "L1_wk", "L1_wv", "L1_bv", "L1_wo", "L1_bo")],
               (A["cos1"], A["sin1"], A["turn1"]))

        xn = ctx.enter_context(nc.sbuf_tensor("d_xn", [D, NB, T + 1], F32))

        def zero_first(v, done):
            nc.vector.memset(xn[:, :, 0:1], 0.0).then_inc(done, 1)
            v.wait_ge(done, 1)

        run_in_block(nc, "zero_first", "vector", zero_first)
        layernorm_pass(nc, "d_ln", C, x, lambda b: [(slice(0, D), xn[:, b, 1:T + 1])])
        gated_mix_pass(nc, C, x, xn, A["d_wr"], A["d_wk"], A["d_wv"], A["d_mu"], x_out)


def rope_tables(n, width):
    inv = np.float32(1.0) / np.float32(10000.0) ** (np.arange(0, width, 2, dtype=np.float32) / np.float32(width))
    freqs = np.arange(n, dtype=np.float32)[:, None] * inv[None, :].astype(np.float32)
    return np.cos(freqs).astype(np.float32), np.sin(freqs).astype(np.float32)


def layouts(inputs):
    g = {k: np.asarray(v) for k, v in inputs.items()}
    col = lambda *v: np.ascontiguousarray(np.stack(v, axis=-1))
    a = {"x": np.ascontiguousarray(g["L0_attn_x"].reshape(NB * T, D).T)}
    for n, p in ((0, "L0_attn_"), (1, "L1_attn_")):
        a[f"L{n}_wq"], a[f"L{n}_wk"], a[f"L{n}_wv"] = g[p + "Wq"], g[p + "Wk"], g[p + "Wv"]
        a[f"L{n}_bqk"] = col(g[p + "bq"], g[p + "bk"])
        a[f"L{n}_bv"] = g[p + "bv"]
        a[f"L{n}_wo"] = g[p + ("Wo" if n == 0 else "Wp")]
        a[f"L{n}_bo"] = g[p + ("bo" if n == 0 else "bp")].reshape(D, 1)
    cos, sin = rope_tables(T, HD)
    a["cos1"] = np.tile(np.repeat(cos, 2, axis=1).T, (H, 1))
    a["sin1"] = np.tile(np.repeat(sin, 2, axis=1).T, (H, 1))
    turn = np.zeros((D, D), np.float32)
    for i in range(0, D, 2):
        turn[i + 1, i], turn[i, i + 1] = -1.0, 1.0
    a["turn1"] = turn

    w = g["L0_ffn_Wqkv"]
    qk = w[:, :, :2 * INNER].reshape(DEPTH, D, 2, NC, CH, 2, HALF).transpose(0, 1, 2, 3, 5, 4, 6).reshape(DEPTH, D, 2 * INNER)
    a["wqkv"] = np.concatenate([qk, w[:, :, 2 * INNER:]], axis=2)
    a["wo"] = g["L0_ffn_Wo"].reshape(DEPTH, INNER // D, D, D).transpose(0, 2, 1, 3)
    a["w1"] = g["L0_ffn_W1"]
    w2 = np.zeros((DEPTH, 3 * D, D), np.float32)
    w2[:, :DI] = g["L0_ffn_W2"]
    a["w2"] = w2.reshape(DEPTH, 3, D, D).transpose(0, 2, 1, 3)
    vec = np.zeros((DEPTH, D, NVEC), np.float32)
    for i, n in enumerate(("L0_ffn_q_scale", "L0_ffn_k_scale")):
        for half in range(2):
            vec[:, :, 2 * i + half] = np.tile(g[n][:, HALF * half:HALF * half + HALF], (1, CH))
    vec[:, :, 4], vec[:, :, 8], vec[:, :, 9] = g["L0_ffn_ln_g"], g["L0_ffn_b2"], g["L0_ffn_ln_b"]
    o = 0
    for i, n in enumerate(FCH):
        vec[:, :n, 5 + i] = g["L0_ffn_b1"][:, o:o + n]
        vec[:, :n, 10 + i] = g["L0_ffn_b1"][:, DI + o:DI + o + n]
        o += n
    a["vec"] = vec
    cos, sin = rope_tables(T, DH)
    half = np.arange(0, DH, 2, dtype=np.float32)
    base = (half + np.float32(0.4 * DH)) / np.float32(1.4 * DH)
    power = (np.arange(T, dtype=np.float32) - T // 2) / np.float32(WIN // 2)
    scale = (base[None, :] ** power[:, None]).astype(np.float32)
    inv = (np.float32(1.0) / scale).astype(np.float32)
    a["tab"] = np.stack([np.tile((m * f).T, (CH, 1)) for f in (scale, inv) for m in (cos, sin)], axis=1)
    i, j = np.arange(D)[:, None] % WIN, np.arange(2 * WIN)[None, :]
    hidden = np.where(j < WIN, i > j, j - WIN > i)
    first = hidden | ((np.arange(D)[:, None] < WIN) & (j < WIN))
    tiles = [first] + [hidden] * (NT - 1)
    a["mask"] = np.concatenate([np.tile(m, (1, CH)) for m in tiles], axis=1).astype(np.float32) * np.float32(MASKED)
    a["d_wr"], a["d_wk"], a["d_wv"] = (g[f"L1_ffn_W_{n}"].T for n in "rkv")
    a["d_mu"] = col(g["L1_ffn_mu_r"], g["L1_ffn_mu_k"])
    a["block4"] = (np.arange(D)[:, None] // HALF == np.arange(CH)[None, :]).astype(np.float32)
    return {k: np.ascontiguousarray(v, dtype=np.float32) for k, v in a.items()}


def kernel(**inputs):
    import concourse.bacc as bacc
    from concourse.bass_utils import run_bass_kernel_spmd

    nc = bacc.Bacc("TRN2", target_bir_lowering=False, num_devices=1)
    arrays = layouts(inputs)
    aps = {k: nc.dram_tensor(f"in_{k}", v.shape, mybir.dt.from_np(v.dtype), kind="ExternalInput").ap()
           for k, v in arrays.items()}
    out = nc.dram_tensor("out", (D, NB * T), F32, kind="ExternalOutput").ap()
    model(nc, aps, out)
    r = run_bass_kernel_spmd(nc, [{f"in_{k}": v for k, v in arrays.items()}], core_ids=[0])
    return np.ascontiguousarray(np.asarray(r.results[0]["out"]).T.reshape(NB, T, D))
```

```python
import math
from contextlib import ExitStack, contextmanager

import numpy as np

import concourse.bass as bass
from concourse import mybir

F32 = mybir.dt.float32
BF16 = mybir.dt.bfloat16
I32 = mybir.dt.int32
ALU = mybir.AluOpType
ACT = mybir.ActivationFunctionType
AX = mybir.AxisListType

D = 128
NB = 8
T = 512
NT = T // 128
LN_EPS = 1e-5

H = 16
HD = D // H
SPLIT = 3
KROWS = SPLIT * SPLIT * HD
ROWS = KROWS + SPLIT
VW = 32

DEPTH = 6
DH = 64
HALF = DH // 2
INNER = H * DH
WIN = 32
NC = 4
CH = H // NC
KC = T + WIN
DI = int(D * 4 * 2 / 3)
FCH = [128, 128, DI - 256]
MASKED = -1e37
QK_SCALE = 8.0
NVEC = 13

RSQRT_MAGIC = float(0x5F3759DF)


class Tally:

    def __init__(self):
        self.used = {}

    def next(self, sem, n=1):
        count = self.used.get(sem.name, (sem, 0))[1] + n
        self.used[sem.name] = (sem, count)
        return count

    def settle(self, eng):
        for sem, count in self.used.values():
            if count:
                eng.sem_inc(sem, -count)
        self.used = {}


@contextmanager
def semaphore_set(nc, prefix):
    with ExitStack() as ctx:
        taken = []

        def sem(name):
            taken.append(ctx.enter_context(nc.semaphore(f"{prefix}_{name}")))
            return taken[-1]

        yield sem
        with nc.Block() as block:
            @block.sync
            def _(sp):
                for s in taken:
                    sp.sem_clear(s)


def rsqrt(nc, v, tally, step, a, t, y):
    nc.vector.tensor_scalar(t.bitcast(I32), a.bitcast(I32), 1, None, ALU.logical_shift_right).then_inc(step, 1)
    v.wait_ge(step, tally.next(step))
    nc.vector.tensor_scalar(y.bitcast(I32), t.bitcast(I32), -1.0, RSQRT_MAGIC, ALU.mult, ALU.add).then_inc(step, 1)
    for i in range(3):
        v.wait_ge(step, tally.next(step))
        nc.vector.scalar_tensor_tensor(out=t, in0=y, scalar=-0.5, in1=y, op0=ALU.mult, op1=ALU.mult).then_inc(step, 1)
        v.wait_ge(step, tally.next(step))
        nc.vector.tensor_tensor(t, t, a, ALU.mult).then_inc(step, 1)
        v.wait_ge(step, tally.next(step))
        last = nc.vector.scalar_tensor_tensor(out=y, in0=t, scalar=1.5, in1=y, op0=ALU.add, op1=ALU.mult)
        if i < 2:
            last.then_inc(step, 1)
    return last


def layernorm_pass(nc, name, C, src, dst_parts):
    with ExitStack() as ctx:
        def sb(n, shape, dt=F32):
            return ctx.enter_context(nc.sbuf_tensor(f"{name}_{n}", shape, dt))

        sem = ctx.enter_context(semaphore_set(nc, name))

        xc = sb("xc", [D, NB, T])
        sq = sb("sq", [D, 2, T])
        var = sb("var", [D, NB * NT])
        tmp = sb("tmp", [D, NB * NT])
        rstd = sb("rstd", [D, NB * NT])
        mean_ps = [ctx.enter_context(nc.psum_tensor(f"{name}_mean{i}", [D, T], F32)) for i in range(2)]
        var_ps = ctx.enter_context(nc.psum_tensor(f"{name}_varp", [D, NB * NT], F32))
        bc_ps = [ctx.enter_context(nc.psum_tensor(f"{name}_bc{i}", [D, T], F32)) for i in range(2)]
        mean_ready, centred, squared, var_ready = sem("mean"), sem("centred"), sem("squared"), sem("varr")
        sq_used, rstd_ready, bc_ready, bc_used, step = sem("squsd"), sem("rstd"), sem("bc"), sem("bcused"), sem("step")
        block = ctx.enter_context(nc.Block())

        @block.tensor
        def _(pe):
            def mean(b):
                if b >= 2:
                    pe.wait_ge(centred, b - 1)
                nc.tensor.matmul(mean_ps[b % 2][:], C["inv"][:], src[:, b, :], start=True, stop=True).then_inc(mean_ready, 1)

            mean(0)
            for b in range(NB):
                if b + 1 < NB:
                    mean(b + 1)
                pe.wait_ge(squared, b + 1)
                for t in range(NT):
                    last = nc.tensor.matmul(var_ps[:, b * NT + t:b * NT + t + 1], sq[:, b % 2, 128 * t:128 * t + 128],
                                            C["inv"][:, 0:1], start=True, stop=True)
                last.then_inc(var_ready, 1)
            pe.wait_ge(rstd_ready, 1)
            for b in range(NB):
                if b >= 2:
                    pe.wait_ge(bc_used, b - 1)
                for t in range(NT):
                    last = nc.tensor.transpose(bc_ps[b % 2][:, 128 * t:128 * t + 128],
                                               rstd[:, b * NT + t:b * NT + t + 1].to_broadcast([128, 128]), C["ident"][:])
                last.then_inc(bc_ready, 1)

        @block.scalar
        def _(act):
            for b in range(NB):
                act.wait_ge(centred, b + 1)
                if b >= 2:
                    act.wait_ge(var_ready, b - 1)
                nc.scalar.activation(sq[:, b % 2, :], xc[:, b, :], ACT.Square).then_inc(squared, 1)

        @block.vector
        def _(v):
            tally = Tally()
            for b in range(NB):
                v.wait_ge(mean_ready, b + 1)
                nc.vector.tensor_tensor(xc[:, b, :], src[:, b, :], mean_ps[b % 2][:], ALU.subtract).then_inc(centred, 1)
            v.wait_ge(var_ready, NB)
            nc.vector.tensor_scalar(var[:], var_ps[:], LN_EPS, None, ALU.add).then_inc(step, 1)
            v.wait_ge(step, tally.next(step))
            rsqrt(nc, v, tally, step, var[:], tmp[:], rstd[:]).then_inc(rstd_ready, 1)
            for b in range(NB):
                v.wait_ge(bc_ready, b + 1)
                for part, dst in dst_parts(b):
                    last = nc.vector.tensor_tensor(dst, xc[part, b, :], bc_ps[b % 2][part, :], ALU.mult)
                last.then_inc(bc_used, 1)


def attention_pass(nc, name, C, x, xn, w, rope):
    wq_d, bqkv_d, wk_d, wv_d, bv_d, wo_d, bo_d = w
    with ExitStack() as ctx:
        def sb(n, shape, dt=F32):
            return ctx.enter_context(nc.sbuf_tensor(f"{name}_{n}", shape, dt))

        sem = ctx.enter_context(semaphore_set(nc, name))

        wq, wk, wv, wo = sb("wq", [D, D]), sb("wk", [D, D]), sb("wv", [D, D]), sb("wo", [D, D])
        bqk = sb("bqk", [D, 2])
        bo = sb("bo", [D, 1])
        bv = sb("bv", [D, D])
        if rope is not None:
            cos, sin, turn = sb("cos", [D, T]), sb("sin", [D, T]), sb("turn", [D, D])
            rs = sb("rs", [D, 2, T])
        xs = sb("xs", [D, T])
        qk = sb("qk", [D, 2, T])
        parts = sb("parts", [D, SPLIT, 2, T], BF16)
        left = sb("left", [D, 2, T])
        qs = [sb(f"qs{i}", [ROWS, H, T], BF16) for i in range(2)]
        ks = [sb(f"ks{i}", [ROWS, H, T], BF16) for i in range(2)]
        vt = [sb(f"vt{i}", [D, NT, H, VW]) for i in range(2)]
        nmax = sb("nmax", [D, H, NT])
        rows = sb("rows", [H // 2, T])
        rleft = sb("rleft", [H // 2, T])
        rparts = sb("rparts", [H // 2, SPLIT, T], BF16)
        pt = [sb(f"pt{i}", [D, 4, T]) for i in range(2)]
        oe = sb("oe", [D, T])
        rsum = sb("rsum", [D, NT, 4])
        ot = sb("ot", [D, NT, D])
        of = sb("of", [D, T])
        scratch = [nc.dram_tensor(f"{name}_scr{i}", [2, SPLIT, D, T], BF16).ap() for i in range(2)]
        rscratch = [nc.dram_tensor(f"{name}_rscr{i}", [SPLIT, H // 2, T], BF16).ap() for i in range(2)]

        pair = [ctx.enter_context(nc.psum_tensor(f"{name}_pair{i}", [D, 2, T], F32)) for i in range(2)]
        st = [ctx.enter_context(nc.psum_tensor(f"{name}_st{i}", [D, T], F32)) for i in range(2)]
        op = [ctx.enter_context(nc.psum_tensor(f"{name}_o{i}", [D, T], F32)) for i in range(2)]

        loaded_pe, loaded_act, loaded_dve = sem("wpe"), sem("wact"), sem("wdve")
        loaded_pool = sem("wpool")
        xs_ready = sem("xs")
        proj_ready = sem("proj")
        v_ready = sem("vps")
        pair_act = sem("pair_act")
        pair_dve = [sem("pair_dve0"), sem("pair_dve1")]
        qk_ready = sem("qkready")
        turned = sem("turned")
        sin_ready = sem("sinr")
        rotated = sem("rotated")
        qk_split = sem("qksplit")
        pool_step, dve_step = sem("pstep"), sem("dstep")
        scratch_full = sem("scrf")
        qs_used = [sem("qsused0"), sem("qsused1")]
        qs_full = [sem("qsf0"), sem("qsf1")]
        s_ready = sem("sready")
        rows_ps = sem("rowsps")
        rows_ready = sem("rowsr")
        rows_split = sem("rowss")
        rscratch_full = sem("rscrf")
        rows_full = [sem("rowsf0"), sem("rowsf1")]
        st_ready = sem("stready")
        exp_done = sem("exp")
        pv_done = sem("pv")
        oe_ready = sem("oeready")
        otr_ready = sem("otr")
        of_ps = sem("ofps")
        of_ready = sem("ofr")
        wo_ready = sem("wor")
        ones_ready = sem("ones")
        rows_used = sem("rowsused")
        rparts_free = sem("rpfree")
        block = ctx.enter_context(nc.Block())

        SC = HD ** -0.5

        def program(eng, unit):
            unit(1, 0, None, None, None)
            unit(0, 1, 0, None, None)
            unit(1, 2, 1, 0, None)
            with eng.Fori(0, NB // 2 - 2) as i:
                unit(0, 2 * i + 3, 2 * i + 2, 2 * i + 1, 2 * i)
                unit(1, 2 * i + 4, 2 * i + 3, 2 * i + 2, 2 * i + 1)
            unit(0, NB - 1, NB - 2, NB - 3, NB - 4)
            unit(1, None, NB - 1, NB - 2, NB - 3)
            unit(0, None, None, NB - 1, NB - 2)
            unit(1, None, None, None, NB - 1)

        @block.sync
        def _(sp):
            for dst, src in ((wq, wq_d), (wk, wk_d), (wv, wv_d), (wo, wo_d)):
                sp.dma_start(dst[:], src).then_inc(loaded_pe, 16)
            sp.dma_start(bqk[:], bqkv_d).then_inc(loaded_act, 16)
            if rope is not None:
                sp.dma_start(turn[:], rope[2]).then_inc(loaded_pe, 16)
                sp.dma_start(sin[:], rope[1]).then_inc(loaded_dve, 16)
                sp.dma_start(cos[:], rope[0]).then_inc(loaded_pool, 16)
            sp.dma_start(bo[:], bo_d).then_inc(loaded_dve, 16)
            sp.dma_start(bv[:], bv_d.partition_broadcast(D)).then_inc(loaded_dve, 16)

            sp.wait_ge(ones_ready, 1)

            def unit(par, s, m, e, f):
                seen = Tally()

                def load_heads(half, p):
                    h = slice(8 * half, 8 * half + 8)
                    for i in range(SPLIT):
                        r = i * SPLIT * HD
                        sp.dma_start(ks[p][r:r + SPLIT * HD, h, :],
                                     scratch[p][1].rearrange("j (e h) t -> (j e) h t", e=HD)[:, h, :]).then_inc(qs_full[half], 16)
                        for j in range(SPLIT):
                            r = (i * SPLIT + j) * HD
                            sp.dma_start(qs[p][r:r + HD, h, :],
                                         scratch[p][0, i].rearrange("(e h) t -> e h t", e=HD)[:, h, :]).then_inc(qs_full[half], 16)

                def load_rows(half, p):
                    sp.wait_ge(rows_split, seen.next(rows_split))
                    sp.dma_start(rscratch[half].rearrange("s h t -> h s t"), rparts[:]).then_inc(rscratch_full, 16)
                    sp.wait_ge(rscratch_full, seen.next(rscratch_full, 16))
                    sp.sem_inc(rparts_free, 1)
                    sp.dma_start(qs[p][KROWS:ROWS, 8 * half:8 * half + 8, :], rscratch[half]).then_inc(rows_full[half], 16)

                if m is not None:
                    if f is not None:
                        sp.wait_ge(qs_used[1], seen.next(qs_used[1]))
                    load_heads(1, par)
                if e is not None:
                    load_rows(1, 1 - par)
                if s is not None:
                    sp.wait_ge(qk_split, seen.next(qk_split))
                    for i in range(SPLIT):
                        sp.dma_start(scratch[1 - par][:, i].rearrange("a d t -> d a t"), parts[:, i]).then_inc(scratch_full, 16)
                    sp.wait_ge(scratch_full, seen.next(scratch_full, SPLIT * 16))
                    if e is not None:
                        sp.wait_ge(qs_used[0], seen.next(qs_used[0]))
                    load_heads(0, 1 - par)
                if m is not None:
                    load_rows(0, par)
                seen.settle(sp)

            program(sp, unit)

        @block.gpsimd
        def _(pool):
            if rope is not None:
                pool.wait_ge(loaded_pool, 16)

            def unit(par, s, m, e, f):
                seen = Tally()

                def split_rows(wait):
                    pool.wait_ge(rows_ready, seen.next(rows_ready))
                    if wait:
                        pool.wait_ge(rparts_free, seen.next(rparts_free))
                    for i in range(SPLIT):
                        last = nc.gpsimd.tensor_copy(rparts[:, i, :], rows[:] if i == 0 else rleft[:])
                        if i < SPLIT - 1:
                            last.then_inc(pool_step, 1)
                            pool.wait_ge(pool_step, seen.next(pool_step))
                            nc.gpsimd.tensor_tensor(rleft[:], rows[:] if i == 0 else rleft[:], rparts[:, i, :],
                                                    ALU.subtract).then_inc(pool_step, 1)
                            pool.wait_ge(pool_step, seen.next(pool_step))
                    last.then_inc(rows_split, 1)
                    pool.drain().then_inc(rows_used, 1)

                if e is not None:
                    split_rows(True)
                if rope is not None and s is not None:
                    pool.wait_ge(qk_ready, seen.next(qk_ready))
                    pool.wait_ge(sin_ready, seen.next(sin_ready))
                    for a in range(2):
                        nc.gpsimd.tensor_tensor(qk[:, a, :], qk[:, a, :], cos[:], ALU.mult).then_inc(pool_step, 1)
                    for a in range(2):
                        pool.wait_ge(pool_step, seen.next(pool_step))
                        last = nc.gpsimd.tensor_tensor(qk[:, a, :], qk[:, a, :], rs[:, a, :], ALU.add)
                    last.then_inc(rotated, 1)
                if m is not None:
                    split_rows(e is not None)
                seen.settle(pool)

            program(pool, unit)

        @block.scalar
        def _(act):
            act.wait_ge(loaded_act, 16)

            def unit(par, s, m, e, f):
                seen = Tally()
                before = 0 if f is None else 2

                def exponentials(n, r):
                    act.wait_ge(st_ready, seen.next(st_ready))
                    if r == 0 and n - 1 + before > 0:
                        act.wait_ge(pv_done, n - 1 + before)
                    nc.scalar.activation(pt[n % 2][:, r, :], st[r % 2][:], ACT.Exp, scale=SC).then_inc(exp_done, 1)

                def output_copy(count, g):
                    act.wait_ge(pv_done, count)
                    nc.scalar.activation(oe[:], op[g % 2][:], ACT.Copy).then_inc(oe_ready, 1)

                def rows_copy(wait):
                    act.wait_ge(rows_ps, seen.next(rows_ps))
                    if wait:
                        act.wait_ge(rows_used, seen.next(rows_used))
                    nc.scalar.activation(rows[:], pair[0][0:H // 2, 0, :], ACT.Copy).then_inc(rows_ready, 1)
                    act.drain().then_inc(pair_act, 1)

                for n in range(H):
                    if e is not None:
                        for r in range(2):
                            exponentials(n, r)
                    if n == 1 and e is not None:
                        rows_copy(True)
                    if n == 1 and m is not None:
                        nc.scalar.activation(xs[:], xn[:, m, :], ACT.Copy).then_inc(xs_ready, 1)
                    if n == 4 and f is not None:
                        act.wait_ge(of_ps, seen.next(of_ps))
                        nc.scalar.activation(of[:], pair[0][:, 0, :], ACT.Copy).then_inc(of_ready, 1)
                    if n == 5 and s is not None:
                        act.wait_ge(proj_ready, seen.next(proj_ready))
                        nc.scalar.activation(qk[:, 0, :], pair[0][:, 0, :], ACT.Identity, bias=bqk[:, 0:1])
                        nc.scalar.activation(qk[:, 1, :], pair[0][:, 1, :], ACT.Identity, bias=bqk[:, 1:2]).then_inc(qk_ready, 1)
                        act.drain().then_inc(pair_act, 1)
                    if n == 9 and m is not None:
                        rows_copy(e is not None)
                    if e is not None:
                        for r in range(2, 4):
                            exponentials(n, r)
                        if n in (4, 8, 12):
                            output_copy(before + n, n // 4 - 1)
                    if f is not None and n == 0:
                        output_copy(2, 3)
                seen.next(pv_done, before + (H - 2 if e is not None else 0))
                seen.settle(act)

            program(act, unit)

        @block.vector
        def _(v):
            for i in range(2):
                nc.vector.memset(vt[i][:], 0.0).then_inc(dve_step, 1)
                nc.vector.memset(ks[i][64:ROWS], 1.0)
            v.wait_ge(dve_step, 2)
            for i in range(2):
                nc.vector.memset(vt[i][:, :, :, HD:HD + 1], 1.0).then_inc(dve_step, 1)
            v.wait_ge(dve_step, 4)
            v.sem_inc(dve_step, -4)
            v.sem_inc(ones_ready, 1)
            v.wait_ge(loaded_dve, 32 if rope is None else 48)

            def unit(par, s, m, e, f):
                seen = Tally()

                def normalise(g):
                    v.wait_ge(otr_ready, seen.next(otr_ready))
                    o = pair[1][:, 0, :].rearrange("p (t r c) -> p t r c", t=NT, r=4)
                    nc.vector.reciprocal(rsum[:], o[:, :, :, HD]).then_inc(dve_step, 1)
                    v.wait_ge(dve_step, seen.next(dve_step))
                    nc.vector.tensor_tensor(ot[:, :, 4 * HD * g:4 * HD * (g + 1)].rearrange("p t (r e) -> p t r e", r=4),
                                            o[:, :, :, 0:HD], rsum[:].unsqueeze(3).to_broadcast([D, NT, 4, HD]),
                                            ALU.mult).then_inc(pair_dve[1], 1)

                def split(i):
                    src = qk if i == 0 else left
                    if i > 0:
                        v.wait_ge(dve_step, seen.next(dve_step))
                    last = nc.vector.tensor_copy(parts[:, i], src[:])
                    if i == SPLIT - 1:
                        last.then_inc(qk_split, 1)
                    else:
                        last.then_inc(dve_step, 1)
                        v.wait_ge(dve_step, seen.next(dve_step))
                        nc.vector.tensor_tensor(left[:], src[:], parts[:, i], ALU.subtract).then_inc(dve_step, 1)

                first_split = 6 if rope is None else 9
                for n in range(H):
                    if m is not None:
                        for i in range(2):
                            v.wait_ge(s_ready, seen.next(s_ready))
                            nc.vector.tensor_reduce(out=nmax[:, n, 2 * i:2 * i + 2], in_=pair[i][:], op=ALU.max,
                                                    axis=AX.X, negate=True).then_inc(pair_dve[i], 1)
                    if f is not None and n == 1:
                        normalise(3)
                    if m is not None and n == 2:
                        v.wait_ge(v_ready, seen.next(v_ready))
                        nc.vector.tensor_tensor(vt[par][:, :, :, 0:HD], pair[1][:, 0, :].rearrange("p (k h e) -> p k h e", k=NT, e=HD),
                                                bv[:].rearrange("p (h e) -> p h e", e=HD).unsqueeze(1).to_broadcast([D, NT, H, HD]),
                                                ALU.add).then_inc(pair_dve[1], 1)
                    if f is not None and n == 4:
                        v.wait_ge(wo_ready, seen.next(wo_ready))
                        nc.vector.scalar_tensor_tensor(out=x[:, f, :], in0=pair[1][:, 0, :], scalar=bo[:, 0:1], in1=x[:, f, :],
                                                       op0=ALU.add, op1=ALU.add).then_inc(pair_dve[1], 1)
                    if e is not None and n in (5, 9, 13):
                        normalise(n // 4 - 1)
                    if s is not None and rope is not None and n == 6:
                        v.wait_ge(turned, seen.next(turned))
                        for a in range(2):
                            last = nc.vector.tensor_tensor(rs[:, a, :], pair[1][:, a, :], sin[:], ALU.mult)
                        last.then_inc(sin_ready, 1)
                        v.drain().then_inc(pair_dve[1], 1)
                    if s is not None and n - first_split in range(SPLIT):
                        if n == first_split:
                            ready = qk_ready if rope is None else rotated
                            v.wait_ge(ready, seen.next(ready))
                        split(n - first_split)
                seen.settle(v)

            program(v, unit)

        @block.tensor
        def _(pe):
            pe.wait_ge(loaded_pe, 64 if rope is None else 80)
            due = {0: None, 1: None}

            def unit(par, s, m, e, f):
                seen = Tally()
                before = 0 if f is None else 4

                def read(i):
                    if due[i] is not None:
                        pe.wait_ge(due[i], seen.next(due[i]))
                    due[i] = None

                def claim(i, released_by):
                    read(i)
                    due[i] = released_by

                def scores(n, r):
                    k, h, kt = 4 * n + r, 4 * (n // 4) + r, n % 4
                    if k - 1 + before > 0:
                        pe.wait_ge(exp_done, k - 1 + before)
                    nc.tensor.matmul(st[r % 2][:], ks[1 - par][0:ROWS, h, 128 * kt:128 * kt + 128], qs[1 - par][0:ROWS, h, :],
                                     start=True, stop=True).then_inc(st_ready, 1)

                def pv(n, buf, count):
                    pe.wait_ge(exp_done, count)
                    for r in range(4):
                        last = nc.tensor.matmul(op[(n // 4) % 2][32 * r:32 * r + 32, :], vt[buf][:, n % 4, 4 * (n // 4) + r, :],
                                                pt[n % 2][:, r, :], start=(n % 4 == 0), stop=(n % 4 == 3), skip_group_check=True)
                    last.then_inc(pv_done, 1)

                def maxima(n, i):
                    claim(i, pair_dve[i])
                    for j in range(2):
                        q0 = 128 * (2 * i + j)
                        last = nc.tensor.matmul(pair[i][:, j, :], qs[par][0:KROWS, n, q0:q0 + 128], ks[par][0:KROWS, n, :],
                                                start=True, stop=True)
                    last.then_inc(s_ready, 1)

                def transposed_output():
                    pe.wait_ge(oe_ready, seen.next(oe_ready))
                    claim(1, pair_dve[1])
                    for t in range(NT):
                        last = nc.tensor.transpose(pair[1][:, 0, 128 * t:128 * t + 128], oe[:, 128 * t:128 * t + 128], C["ident"][:])
                    last.then_inc(otr_ready, 1)

                def row_maxima(half):
                    claim(0, pair_act)
                    if m is None:
                        read(1)
                    for t in range(NT):
                        last = nc.tensor.transpose(pair[0][0:H // 2, 0, 128 * t:128 * t + 128],
                                                   nmax[:, 8 * half:8 * half + 8, t], C["ident"][:])
                    last.then_inc(rows_ps, 1)

                for n in range(H):
                    if n % 8 == 0:
                        half = n // 8
                        if e is not None:
                            if half == 1:
                                pe.wait_ge(rows_full[1], seen.next(rows_full[1], 16))
                            else:
                                pe.wait_ge(rows_full[0], seen.next(rows_full[0], 16))
                        if m is not None:
                            pe.wait_ge(qs_full[half], seen.next(qs_full[half], SPLIT * (SPLIT + 1) * 16))
                    if e is not None:
                        scores(n, 0)
                        scores(n, 1)
                    if m is not None:
                        maxima(n, 0)
                    if e is not None:
                        scores(n, 2)
                    if n == 0 and f is not None:
                        pv(H - 1, par, 4)
                    if n > 0 and e is not None:
                        pv(n - 1, 1 - par, before + 4 * n)
                    if e is not None:
                        scores(n, 3)
                        if n % 8 == 7:
                            pe.drain().then_inc(qs_used[n // 8], 1)
                    if m is not None:
                        maxima(n, 1)
                    if n == 0 and e is not None:
                        row_maxima(1)
                    if n == 1 and f is not None:
                        transposed_output()
                    if n == 2 and m is not None:
                        pe.wait_ge(xs_ready, seen.next(xs_ready))
                        claim(1, pair_dve[1])
                        for t in range(NT):
                            last = nc.tensor.matmul(pair[1][:, 0, 128 * t:128 * t + 128], xs[:, 128 * t:128 * t + 128], wv[:],
                                                    start=True, stop=True)
                        last.then_inc(v_ready, 1)
                    if n == 3 and f is not None:
                        if m is None:
                            read(1)
                        claim(0, of_ready)
                        for t in range(NT):
                            last = nc.tensor.transpose(pair[0][:, 0, 128 * t:128 * t + 128], ot[:, t, :], C["ident"][:])
                        last.then_inc(of_ps, 1)
                    if n == 4 and f is not None:
                        if m is None:
                            read(0)
                        claim(1, pair_dve[1])
                        nc.tensor.matmul(pair[1][:, 0, :], wo[:], of[:], start=True, stop=True).then_inc(wo_ready, 1)
                    if n == 4 and s is not None:
                        claim(0, pair_act)
                        nc.tensor.matmul(pair[0][:, 0, :], wq[:], xn[:, s, :], start=True, stop=True)
                        nc.tensor.matmul(pair[0][:, 1, :], wk[:], xn[:, s, :], start=True, stop=True).then_inc(proj_ready, 1)
                    if n in (5, 9, 13) and e is not None:
                        transposed_output()
                    if n == 6 and rope is not None and s is not None:
                        if m is None:
                            read(0)
                        claim(1, pair_dve[1])
                        for a in range(2):
                            last = nc.tensor.matmul(pair[1][:, a, :], turn[:], qk[:, a, :], start=True, stop=True)
                        last.then_inc(turned, 1)
                    if n == 8 and m is not None:
                        row_maxima(0)
                seen.next(exp_done, before + (4 * H - 4 if e is not None else 0))
                if m is None:
                    read(0)
                    read(1)
                seen.settle(pe)

            program(pe, unit)


def local_stack(nc, C, xs, A):
    with ExitStack() as ctx:
        def sb(n, shape, dt=F32):
            return ctx.enter_context(nc.sbuf_tensor(f"l_{n}", shape, dt))

        sem = ctx.enter_context(semaphore_set(nc, "l"))

        wqkv, wo, w1, w2 = sb("wqkv", [D, 3 * INNER]), sb("wo", [D, INNER // D, D]), sb("w1", [D, 2 * DI]), sb("w2", [D, 3, D])
        vec = sb("vec", [D, NVEC])
        vec_act = sb("vec_act", [D, NVEC])
        tab = sb("tab", [D, 4, T])
        mask = sb("mask", [D, 2, T], BF16)
        ident16 = sb("ident16", [D, D], BF16)
        block4 = sb("block4", [D, CH])
        xc = sb("xc", [D, T])
        t = [sb(f"t{i}", [D, T]) for i in range(4)]
        u = [[sb(f"u{p}{i}", [D, T]) for i in range(4)] for p in range(2)]
        sq = [sb(f"sq{a}", [D, 2, T]) for a in range(2)]
        sqs = [sb(f"sqs{a}", [D, T]) for a in range(2)]
        qn = [sb(f"qn{i}", [D, T]) for i in range(2)]
        kn = [sb(f"kn{i}", [D, T]) for i in range(2)]
        kbd = [sb(f"kbd{i}", [D, CH, KC]) for i in range(2)]
        norm = sb("norm", [D, NT * 2 * CH + NT])
        ntmp = sb("ntmp", [D, NT * 2 * CH + NT])
        rn = sb("rn", [D, NT * 2 * CH + NT])
        NSS = NT * 2 * CH
        rnx = sb("rnx", [D, NSS, HALF])
        p = sb("p", [D, NT * CH, 2 * WIN])
        pn = sb("pn", [D, NT * CH, 2 * WIN])
        pt = sb("pt", [D, NT * CH * 2 * WIN])
        smax = sb("smax", [D, NT * CH])
        ssum = sb("ssum", [D, NT * CH])
        srec = sb("srec", [D, NT * CH])
        pbd = sb("pbd", [D, 4, NT * CH * 2 * WIN])
        va = [sb(f"va{c}", [D, NT, CH * DH]) for c in range(NC)]
        vp = [sb(f"vp{c}", [D, NT, CH * DH]) for c in range(NC)]
        ot = sb("ot", [D, INNER // D, T])
        xcn, fsq = sb("xcn", [D, T]), sb("fsq", [D, T])
        xng = fsq
        xnf = sb("xnf", [D, T])
        hid = [sb(f"hid{i}", [D, T]) for i in range(3)]

        R = [ctx.enter_context(nc.psum_tensor(f"l_r{i}", [D, 2, T], F32)) for i in range(4)]

        names = ("w_pe w_act w_dve consts_pe consts_dve layer_done xc_ready q_dve q_act k_dve k_act v_act sq_free "
                 "r2_act r0_dve r1_dve r3_dve rq_ready ra_ready sq_sum ss_ready rn_ready rnx_ready b_ready r0_dve_b "
                 "qn_ready kn_ready kbd_full s_ready t_ready p_ready rec_ready pn_ready pt_ready pt_free pbd_free pbd_full "
                 "va_ready vp_full pv_ready ot_ready wo_ready x_ready mean_ready centred fsq_ready bc_ready xng_ready "
                 "xnf_ready g_ready a_ready gelu_ready h_ready f_ready ffn_done step pstep init mask_full").split()
        S = {n: sem(n) for n in names}
        block = ctx.enter_context(nc.Block())

        def layers(eng, body):
            with eng.Fori(0, DEPTH) as l:
                body(l, 0, None)
                with eng.Fori(1, NB) as b:
                    body(l, b, b - 1)
                body(l, None, NB - 1)

        def live(c, lag, b, prev):
            return b is not None if c >= lag else prev is not None

        @block.sync
        def _(sp):
            sp.dma_start(pn[:].rearrange("p a b -> p (a b)"), A["mask"]).then_inc(S["mask_full"], 16)
            sp.dma_start(block4[:], A["block4"]).then_inc(S["consts_pe"], 16)
            sp.dma_start(tab[:], A["tab"]).then_inc(S["consts_dve"], 16)

            def body(l, b, prev):
                seen = Tally()
                if prev is None:
                    sp.wait_ge(S["layer_done"], seen.next(S["layer_done"]))
                    sp.dma_start(wqkv[:], A["wqkv"][l]).then_inc(S["w_pe"], 16)
                    sp.dma_start(wo[:], A["wo"][l]).then_inc(S["w_pe"], 16)
                    sp.dma_start(w1[:], A["w1"][l]).then_inc(S["w_pe"], 16)
                    sp.dma_start(w2[:], A["w2"][l]).then_inc(S["w_pe"], 16)
                    sp.dma_start(vec[:], A["vec"][l]).then_inc(S["w_dve"], 16)
                    sp.dma_start(vec_act[:], A["vec"][l]).then_inc(S["w_act"], 16)
                for c in range(NC):
                    if live(c, 3, b, prev):
                        sp.wait_ge(S["pbd_free"], seen.next(S["pbd_free"]))
                        sp.sem_inc(S["pt_free"], 1)
                        sp.wait_ge(S["pt_ready"], seen.next(S["pt_ready"]))
                        for w in range(4):
                            q = slice(32 * w, 32 * w + 32)
                            sp.dma_start(pbd[q, w, :], pt[q, :]).then_inc(S["pbd_full"], 16)
                    if b is not None:
                        sp.wait_ge(S["va_ready"], seen.next(S["va_ready"]))
                        sp.dma_start(vp[c][32:128], va[c][0:96]).then_inc(S["vp_full"], 16)
                        sp.dma_start(vp[c][0:32, 1:NT, :], va[c][96:128, 0:NT - 1, :]).then_inc(S["vp_full"], 16)
                    if live(c, 1, b, prev):
                        sp.wait_ge(S["kn_ready"], seen.next(S["kn_ready"]))
                        for i in range(2):
                            for r in range(CH):
                                q = slice(32 * r, 32 * r + 32)
                                sp.dma_start(kbd[i][q, r, WIN:KC], kn[i][q, :]).then_inc(S["kbd_full"], 16)
                seen.settle(sp)

            layers(sp, body)

        @block.gpsimd
        def _(pool):
            def body(l, b, prev):
                seen = Tally()
                for c in range(NC):
                    par = c % 2
                    if b is not None:
                        for a in range(2):
                            pool.wait_ge(S["rq_ready"], seen.next(S["rq_ready"]))
                            nc.gpsimd.tensor_tensor(u[par][2 * a][:], t[0][:], t[1][:], ALU.subtract)
                            nc.gpsimd.tensor_tensor(u[par][2 * a + 1][:], t[2][:], t[3][:], ALU.add).then_inc(S["ra_ready"], 1)
                        nc.gpsimd.tensor_tensor(sqs[0][:], sq[0][:, 0, :], sq[0][:, 1, :], ALU.add)
                        nc.gpsimd.tensor_tensor(sqs[1][:], sq[1][:, 0, :], sq[1][:, 1, :], ALU.add).then_inc(S["sq_sum"], 1)
                        pool.drain().then_inc(S["sq_free"], 1)
                    if live(c, 2, b, prev):
                        pool.wait_ge(S["rec_ready"], seen.next(S["rec_ready"]))
                        nc.gpsimd.tensor_tensor(pn[:], p[:], srec[:].unsqueeze(2).to_broadcast([D, NT * CH, 2 * WIN]),
                                                ALU.mult).then_inc(S["pn_ready"], 1)
                seen.settle(pool)

            layers(pool, body)

        @block.scalar
        def _(act):
            act.sem_inc(S["sq_free"], 1)

            def body(l, b, prev):
                seen = Tally()
                if prev is None:
                    act.wait_ge(S["w_act"], seen.next(S["w_act"], 16))
                if b is not None:
                    nc.scalar.activation(xc[:], xs[:, b, 0:T], ACT.Copy).then_inc(S["xc_ready"], 1)
                for c in range(NC):
                    if b is not None:
                        act.wait_ge(S["sq_free"], seen.next(S["sq_free"]))
                        act.wait_ge(S["q_act"], seen.next(S["q_act"]))
                        nc.scalar.activation(sq[0][:], R[0][:], ACT.Square).then_inc(S["q_dve"], 1)
                        act.wait_ge(S["k_act"], seen.next(S["k_act"]))
                        nc.scalar.activation(sq[1][:], R[1][:], ACT.Square).then_inc(S["k_dve"], 1)
                        act.wait_ge(S["v_act"], seen.next(S["v_act"]))
                        nc.scalar.activation(va[c][:], R[2][:].rearrange("p a (k f) -> p (a k) f", k=2), ACT.Copy).then_inc(S["va_ready"], 1)
                        act.drain().then_inc(S["r2_act"], 1)
                    if live(c, 1, b, prev) or (c == 3 and prev is not None):
                        act.wait_ge(S["rn_ready"], seen.next(S["rn_ready"]))
                        if live(c, 1, b, prev):
                            nc.scalar.activation(rnx[:], rn[:, 0:NSS].unsqueeze(2).to_broadcast([D, NSS, HALF]), ACT.Copy)\
                                .then_inc(S["rnx_ready"], 1)
                        else:
                            act.sem_inc(S["rnx_ready"], 1)
                    if live(c, 2, b, prev):
                        act.wait_ge(S["t_ready"], seen.next(S["t_ready"]))
                        nc.scalar.activation(p[:], p[:], ACT.Exp, scale=QK_SCALE).then_inc(S["p_ready"], 1)
                    if c == 3 and prev is not None:
                        act.wait_ge(S["xng_ready"], seen.next(S["xng_ready"]))
                        nc.scalar.activation(xnf[:], xng[:], ACT.Identity, bias=vec_act[:, 9:10]).then_inc(S["xnf_ready"], 1)
                    if live(c, 3, b, prev):
                        act.wait_ge(S["pv_ready"], seen.next(S["pv_ready"]))
                        cc = (c - 3) % NC
                        nc.scalar.activation(ot[:, 2 * cc:2 * cc + 2, :], R[1][:], ACT.Copy).then_inc(S["ot_ready"], 1)
                    if c == 2 and prev is not None:
                        act.wait_ge(S["centred"], seen.next(S["centred"]))
                        nc.scalar.activation(fsq[:], xcn[:], ACT.Square).then_inc(S["fsq_ready"], 1)
                    if c == 3 and prev is not None:
                        for i, n in enumerate(FCH):
                            act.wait_ge(S["g_ready"], seen.next(S["g_ready"]))
                            nc.scalar.activation(hid[i][0:n, :], R[(2, 3, 0)[i]][0:n, 0, :], ACT.Gelu,
                                                 bias=vec_act[0:n, 10 + i:11 + i]).then_inc(S["gelu_ready"], 1)
                seen.settle(act)

            layers(act, body)

        @block.vector
        def _(v):
            v.wait_ge(S["mask_full"], 16)
            nc.vector.tensor_copy(mask[:], pn[:].rearrange("p a b -> p (a b)").rearrange("p (a b) -> p a b", a=2))
            nc.vector.tensor_copy(ident16[:], C["ident"][:])
            for i in range(2):
                nc.vector.memset(kbd[i][:], 0.0)
            nc.vector.memset(pbd[:], 0.0)
            for c in range(NC):
                nc.vector.memset(vp[c][:], 0.0)
            v.drain().then_inc(S["init"], 1)
            v.wait_ge(S["consts_dve"], 16)
            unread = {"ra": 0}

            def body(l, b, prev):
                seen = Tally()
                if prev is None:
                    v.wait_ge(S["w_dve"], seen.next(S["w_dve"], 16))

                def halves_of_pool():
                    if unread["ra"]:
                        v.wait_ge(S["ra_ready"], seen.next(S["ra_ready"]))
                        unread["ra"] = 0

                def rotate(a):
                    halves_of_pool()
                    src, cos, sin = R[a], tab[:, 2 * a, :], tab[:, 2 * a + 1, :]
                    for i, (half, table) in enumerate(((0, cos), (1, sin), (1, cos), (0, sin))):
                        last = nc.vector.scalar_tensor_tensor(out=t[i][:], in0=src[:, half, :], scalar=vec[:, 2 * a + half:2 * a + half + 1],
                                                              in1=table, op0=ALU.mult, op1=ALU.mult)
                    last.then_inc(S["rq_ready"], 1)
                    unread["ra"] = 1
                    v.drain().then_inc(S["r0_dve"] if a == 0 else S["r1_dve"], 1)

                for c in range(NC):
                    par1 = (c - 1) % 2
                    if b is not None:
                        v.wait_ge(S["q_dve"], seen.next(S["q_dve"]))
                        rotate(0)
                    if live(c, 3, b, prev):
                        v.wait_ge(S["pt_free"], seen.next(S["pt_free"]))
                        v.wait_ge(S["pn_ready"], seen.next(S["pn_ready"]))
                        nc.vector.transpose(pt[:], pn[:].rearrange("p a b -> p (a b)")).then_inc(S["pt_ready"], 1)
                    has_ss, has_var = live(c, 1, b, prev), c == 3 and prev is not None
                    if has_ss or has_var:
                        v.wait_ge(S["ss_ready"], seen.next(S["ss_ready"]))
                        lo, hi = (0 if has_ss else NSS), (NSS + NT if has_var else NSS)
                        if has_ss:
                            nc.vector.tensor_scalar(norm[:, 0:NSS], R[3][:, 0, 0:NSS], 1e-24, None, ALU.max).then_inc(S["step"], 1)
                            v.wait_ge(S["step"], seen.next(S["step"]))
                        if has_var:
                            nc.vector.tensor_scalar(norm[:, NSS:], R[3][:, 1, 0:NT], LN_EPS, None, ALU.add).then_inc(S["step"], 1)
                            v.wait_ge(S["step"], seen.next(S["step"]))
                        rsqrt(nc, v, seen, S["step"], norm[:, lo:hi], ntmp[:, lo:hi], rn[:, lo:hi]).then_inc(S["rn_ready"], 1)
                    if b is not None:
                        v.wait_ge(S["k_dve"], seen.next(S["k_dve"]))
                        rotate(1)
                    if live(c, 2, b, prev):
                        v.wait_ge(S["s_ready"], seen.next(S["s_ready"]))
                        sc = R[3][:].rearrange("p a b -> p (a b)").rearrange("p (u k) -> p u k", k=2 * WIN)
                        nc.vector.tensor_reduce(out=smax[:], in_=sc, op=ALU.max, axis=AX.X).then_inc(S["step"], 1)
                        v.wait_ge(S["step"], seen.next(S["step"]))
                        nc.vector.tensor_tensor(p[:], sc, smax[:].unsqueeze(2).to_broadcast([D, NT * CH, 2 * WIN]),
                                                ALU.subtract).then_inc(S["t_ready"], 1)
                        v.drain().then_inc(S["r3_dve"], 1)
                    if has_ss:
                        v.wait_ge(S["b_ready"], seen.next(S["b_ready"]))
                        halves_of_pool()
                        for i in range(2):
                            last = nc.vector.tensor_tensor(qn[i][:], u[par1][i][:], R[0][:, 0, :], ALU.mult)
                        last.then_inc(S["qn_ready"], 1)
                        for i in range(2):
                            last = nc.vector.tensor_tensor(kn[i][:], u[par1][2 + i][:], R[0][:, 1, :], ALU.mult)
                        last.then_inc(S["kn_ready"], 1)
                        v.drain().then_inc(S["r0_dve_b"], 1)
                    if has_var:
                        v.wait_ge(S["bc_ready"], seen.next(S["bc_ready"]))
                        nc.vector.scalar_tensor_tensor(out=xng[:], in0=xcn[:], scalar=vec[:, 4:5], in1=R[2][:, 0, :],
                                                       op0=ALU.mult, op1=ALU.mult).then_inc(S["xng_ready"], 1)
                    if live(c, 2, b, prev):
                        v.wait_ge(S["p_ready"], seen.next(S["p_ready"]))
                        nc.vector.tensor_reduce(out=ssum[:], in_=p[:], op=ALU.add, axis=AX.X).then_inc(S["step"], 1)
                        v.wait_ge(S["step"], seen.next(S["step"]))
                        nc.vector.reciprocal(srec[:], ssum[:]).then_inc(S["rec_ready"], 1)
                    if c == 2 and prev is not None:
                        v.wait_ge(S["wo_ready"], seen.next(S["wo_ready"]))
                        nc.vector.tensor_tensor(xs[0:64, prev, 0:T], xs[0:64, prev, 0:T], R[2][0:64, 0, :], ALU.add).then_inc(S["step"], 1)
                        nc.vector.tensor_tensor(xs[64:128, prev, 1:T + 1], xs[64:128, prev, 1:T + 1], R[2][64:128, 0, :],
                                                ALU.add).then_inc(S["x_ready"], 1)
                        v.wait_ge(S["step"], seen.next(S["step"]))
                        v.wait_ge(S["mean_ready"], seen.next(S["mean_ready"]))
                        nc.vector.tensor_tensor(xcn[:], xs[:, prev, 0:T], R[2][:, 1, :], ALU.subtract).then_inc(S["centred"], 1)
                    if c == 3:
                        if prev is not None:
                            for i, n in enumerate(FCH):
                                v.wait_ge(S["a_ready"], seen.next(S["a_ready"]))
                                v.wait_ge(S["gelu_ready"], seen.next(S["gelu_ready"]))
                                nc.vector.scalar_tensor_tensor(out=hid[i][0:n, :], in0=R[(2, 3, 0)[i]][0:n, 1, :],
                                                               scalar=vec[0:n, 5 + i:6 + i], in1=hid[i][0:n, :],
                                                               op0=ALU.add, op1=ALU.mult).then_inc(S["h_ready"], 1)
                            v.wait_ge(S["f_ready"], seen.next(S["f_ready"]))
                            nc.vector.scalar_tensor_tensor(out=xs[0:64, prev, 0:T], in0=R[2][0:64, 0, :], scalar=vec[0:64, 8:9],
                                                           in1=xs[0:64, prev, 0:T], op0=ALU.add, op1=ALU.add)
                            nc.vector.scalar_tensor_tensor(out=xs[64:128, prev, 1:T + 1], in0=R[2][64:128, 0, :], scalar=vec[64:128, 8:9],
                                                           in1=xs[64:128, prev, 1:T + 1], op0=ALU.add, op1=ALU.add).then_inc(S["ffn_done"], 1)
                        else:
                            v.sem_inc(S["ffn_done"], 1)
                seen.settle(v)

            layers(v, body)

        @block.tensor
        def _(pe):
            pe.sem_inc(S["pbd_free"], 1)
            pe.wait_ge(S["init"], 1)
            pe.wait_ge(S["consts_pe"], 16)
            pe.sem_inc(S["layer_done"], 1)
            due = {0: [], 1: [], 2: [], 3: []}

            def body(l, b, prev):
                seen = Tally()
                if prev is None:
                    pe.wait_ge(S["w_pe"], seen.next(S["w_pe"], 64))

                def read(i):
                    for n in due[i]:
                        pe.wait_ge(S[n], seen.next(S[n]))
                    due[i] = []

                def claim(i, *released_by):
                    read(i)
                    due[i] = list(released_by)

                for c in range(NC):
                    pv_before = live(c - 1, 3, b, prev) if c else prev is not None
                    if b is not None:
                        claim(0, "r0_dve")
                        for half in range(2):
                            o = 2 * D * c + D * half
                            last = nc.tensor.matmul(R[0][:, half, :], wqkv[:, o:o + D], xs[:, b, 0:T], start=True, stop=True)
                            if half == 0 and pv_before:
                                last.then_inc(S["pbd_free"], 1)
                        last.then_inc(S["q_act"], 1)
                        claim(1, "r1_dve")
                        for half in range(2):
                            o = INNER + 2 * D * c + D * half
                            last = nc.tensor.matmul(R[1][:, half, :], wqkv[:, o:o + D], xs[:, b, 0:T], start=True, stop=True)
                        last.then_inc(S["k_act"], 1)
                    elif pv_before:
                        pe.drain().then_inc(S["pbd_free"], 1)
                    has_ss, has_var = live(c, 1, b, prev), c == 3 and prev is not None
                    if has_ss or has_var:
                        claim(3)
                        if has_ss:
                            pe.wait_ge(S["sq_sum"], seen.next(S["sq_sum"]))
                            for k in range(NT):
                                for a in range(2):
                                    o = (k * 2 + a) * CH
                                    last = nc.tensor.matmul(R[3][:, 0, o:o + CH], sqs[a][:, 128 * k:128 * k + 128], block4[:],
                                                            start=True, stop=True)
                        if has_var:
                            pe.wait_ge(S["fsq_ready"], seen.next(S["fsq_ready"]))
                            for k in range(NT):
                                last = nc.tensor.matmul(R[3][:, 1, k:k + 1], fsq[:, 128 * k:128 * k + 128], C["inv"][:, 0:1],
                                                        start=True, stop=True)
                        last.then_inc(S["ss_ready"], 1)
                        due[3] = ["rnx_ready"]
                    if b is not None:
                        if c == 0:
                            pe.wait_ge(S["xc_ready"], seen.next(S["xc_ready"]))
                        claim(2, "r2_act")
                        for k in range(NT):
                            o = 2 * INNER + CH * DH * c
                            last = nc.tensor.matmul(R[2][:, k // 2, 256 * (k % 2):256 * (k % 2) + 256], xc[:, 128 * k:128 * k + 128],
                                                    wqkv[:, o:o + CH * DH], start=True, stop=True)
                        last.then_inc(S["v_act"], 1)
                    if live(c, 2, b, prev):
                        claim(3, "r3_dve")
                        pe.wait_ge(S["qn_ready"], seen.next(S["qn_ready"]))
                        pe.wait_ge(S["kbd_full"], seen.next(S["kbd_full"], 2 * CH * 16))
                        for bank in range(2):
                            nc.tensor.matmul(R[3][:, bank, :], ident16[:], mask[:, bank, :], start=True, stop=False, skip_group_check=True)
                            for w in range(8):
                                W, q = 8 * bank + w, 32 * (w % 4)
                                for half in range(2):
                                    last = nc.tensor.matmul(R[3][q:q + 32, bank, 256 * (w // 4):256 * (w // 4) + 256],
                                                            qn[half][:, WIN * W:WIN * W + WIN], kbd[half][:, :, WIN * W:WIN * W + 2 * WIN],
                                                            start=False, stop=(half == 1), skip_group_check=True)
                        last.then_inc(S["s_ready"], 1)
                    if has_ss or has_var:
                        if due[3] == ["rnx_ready"]:
                            read(3)
                    if has_ss:
                        claim(0, "r0_dve_b")
                        for a in range(2):
                            for k in range(NT):
                                o = (k * 2 + a) * CH
                                last = nc.tensor.transpose(R[0][:, a, 128 * k:128 * k + 128],
                                                           rnx[:, o:o + CH, :].rearrange("p h i -> p (h i)"), C["ident"][:])
                        last.then_inc(S["b_ready"], 1)
                    if has_var:
                        claim(2)
                        for k in range(NT):
                            last = nc.tensor.transpose(R[2][:, 0, 128 * k:128 * k + 128], rn[:, NSS + k:NSS + k + 1].to_broadcast([D, D]),
                                                       C["ident"][:])
                        last.then_inc(S["bc_ready"], 1)
                    if live(c, 3, b, prev):
                        claim(1, "ot_ready")
                        cc = (c - 3) % NC
                        pe.wait_ge(S["vp_full"], seen.next(S["vp_full"], 32))
                        pe.wait_ge(S["pbd_full"], seen.next(S["pbd_full"], 64))
                        for h in range(CH):
                            q = 64 * (h % 2)
                            for g in range(NT):
                                for half, vv in enumerate((vp[cc], va[cc])):
                                    o = ((g * CH + h) * 2 + half) * WIN
                                    last = nc.tensor.matmul(R[1][q:q + 64, h // 2, 128 * g:128 * g + 128], vv[:, g, DH * h:DH * h + DH],
                                                            pbd[:, :, o:o + WIN], start=(half == 0), stop=(half == 1))
                        last.then_inc(S["pv_ready"], 1)
                    if c == 2 and prev is not None:
                        read(1)
                        claim(2)
                        for j in range(INNER // D):
                            last = nc.tensor.matmul(R[2][:, 0, :], wo[:, j, :], ot[:, j, :], start=(j == 0), stop=(j == INNER // D - 1))
                        last.then_inc(S["wo_ready"], 1)
                        pe.wait_ge(S["x_ready"], seen.next(S["x_ready"]))
                        nc.tensor.matmul(R[2][:, 1, :], C["inv"][:], xs[:, prev, 0:T], start=True, stop=True).then_inc(S["mean_ready"], 1)
                    if c == 3 and prev is not None:
                        pe.wait_ge(S["xnf_ready"], seen.next(S["xnf_ready"]))
                        o = 0
                        for i, n in enumerate(FCH):
                            r = R[(2, 3, 0)[i]]
                            claim((2, 3, 0)[i])
                            nc.tensor.matmul(r[0:n, 0, :], w1[:, DI + o:DI + o + n], xnf[:], start=True, stop=True).then_inc(S["g_ready"], 1)
                            nc.tensor.matmul(r[0:n, 1, :], w1[:, o:o + n], xnf[:], start=True, stop=True).then_inc(S["a_ready"], 1)
                            o += n
                        for i, n in enumerate(FCH):
                            pe.wait_ge(S["h_ready"], seen.next(S["h_ready"]))
                            last = nc.tensor.matmul(R[2][:, 0, :], w2[0:n, i, :], hid[i][0:n, :], start=(i == 0), stop=(i == 2))
                        last.then_inc(S["f_ready"], 1)
                        due[2] = ["ffn_done"]
                    if c == 3 and prev is None:
                        for i in (0, 2, 3):
                            read(i)
                        due[2] = ["ffn_done"]
                if b is None:
                    for i in range(4):
                        read(i)
                    pe.drain().then_inc(S["layer_done"], 1)
                seen.settle(pe)

            layers(pe, body)


def gated_mix_pass(nc, C, x, xn, wr_d, wk_d, wv_d, mu_d, out):
    with ExitStack() as ctx:
        def sb(n, shape, dt=F32):
            return ctx.enter_context(nc.sbuf_tensor(f"d_{n}", shape, dt))

        sem = ctx.enter_context(semaphore_set(nc, "d"))

        wr, wk, wv = sb("wr", [D, D]), sb("wk", [D, D]), sb("wv", [D, D])
        mu, comu = sb("mu", [D, 2]), sb("comu", [D, 2])
        prev = [[sb(f"prev{p}{a}", [D, T]) for a in range(2)] for p in range(2)]
        mix = [[sb(f"mix{p}{a}", [D, T]) for a in range(2)] for p in range(2)]
        gate = [sb(f"gate{p}", [D, T]) for p in range(2)]
        act_k = [sb(f"act_k{p}", [D, T]) for p in range(2)]
        res = [sb(f"res{p}", [D, T]) for p in range(2)]
        r_ps, k_ps, v_ps = ([ctx.enter_context(nc.psum_tensor(f"d_{n}{p}", [D, T], F32)) for p in range(2)] for n in "rkv")
        w_pe, w_dve, comu_ready = sem("wpe"), sem("wdve"), sem("comu")
        prev_ready, mix_ready, r_ready, k_ready = sem("prev"), sem("mix"), sem("r"), sem("k")
        relu_ready, sq_ready, v_ready, out_ready = sem("relu"), sem("sqr"), sem("v"), sem("out")
        stored, res_free, step = sem("stored"), sem("resfree"), sem("step")
        block = ctx.enter_context(nc.Block())

        @block.sync
        def _(sp):
            for dst, src in ((wr, wr_d), (wk, wk_d), (wv, wv_d)):
                sp.dma_start(dst[:], src).then_inc(w_pe, 16)
            sp.dma_start(mu[:], mu_d).then_inc(w_dve, 16)
            with sp.Fori(0, NB // 2) as i:
                for p in range(2):
                    sp.wait_ge(out_ready, p + 1)
                    sp.dma_start(out[:, 2 * i + p, :], res[p][:]).then_inc(stored, 16)
                sp.sem_inc(out_ready, -2)
                sp.wait_ge(stored, 32)
                sp.sem_inc(stored, -32)
                sp.sem_inc(res_free, 1)

        @block.scalar
        def _(act):
            act.wait_ge(comu_ready, 1)
            with act.Fori(0, NB // 2) as i:
                for p in range(2):
                    for a in range(2):
                        last = nc.scalar.activation(prev[p][a][:], xn[:, 2 * i + p, 0:T], ACT.Copy, scale=comu[:, a:a + 1])
                    last.then_inc(prev_ready, 1)
                for p in range(2):
                    act.wait_ge(r_ready, p + 1)
                    nc.scalar.activation(gate[p][:], r_ps[p][:], ACT.Sigmoid)
                    act.wait_ge(k_ready, p + 1)
                    nc.scalar.activation(act_k[p][:], k_ps[p][:], ACT.Relu).then_inc(relu_ready, 1)
                act.sem_inc(r_ready, -2)
                act.sem_inc(k_ready, -2)

        @block.vector
        def _(v):
            v.sem_inc(res_free, 1)
            v.wait_ge(w_dve, 16)
            nc.vector.tensor_scalar(comu[:], mu[:], -1.0, 1.0, ALU.mult, ALU.add).then_inc(comu_ready, 1)
            with v.Fori(0, NB // 2) as i:
                for p in range(2):
                    v.wait_ge(prev_ready, p + 1)
                    for a in range(2):
                        last = nc.vector.scalar_tensor_tensor(out=mix[p][a][:], in0=xn[:, 2 * i + p, 1:T + 1], scalar=mu[:, a:a + 1],
                                                              in1=prev[p][a][:], op0=ALU.mult, op1=ALU.add)
                    last.then_inc(mix_ready, 1)
                for p in range(2):
                    v.wait_ge(relu_ready, p + 1)
                    nc.vector.tensor_tensor(act_k[p][:], act_k[p][:], act_k[p][:], ALU.mult).then_inc(sq_ready, 1)
                v.wait_ge(res_free, 1)
                for p in range(2):
                    v.wait_ge(v_ready, p + 1)
                    nc.vector.tensor_tensor(res[p][:], v_ps[p][:], gate[p][:], ALU.mult).then_inc(step, 1)
                for p in range(2):
                    v.wait_ge(step, p + 1)
                    nc.vector.tensor_tensor(res[p][:], res[p][:], x[:, 2 * i + p, :], ALU.add).then_inc(out_ready, 1)
                for s, n in ((prev_ready, 2), (relu_ready, 2), (res_free, 1), (v_ready, 2), (step, 2)):
                    v.sem_inc(s, -n)

        @block.tensor
        def _(pe):
            pe.wait_ge(w_pe, 48)
            with pe.Fori(0, NB // 2) as i:
                for p in range(2):
                    pe.wait_ge(mix_ready, p + 1)
                    nc.tensor.matmul(r_ps[p][:], wr[:], mix[p][0][:], start=True, stop=True).then_inc(r_ready, 1)
                    nc.tensor.matmul(k_ps[p][:], wk[:], mix[p][1][:], start=True, stop=True).then_inc(k_ready, 1)
                for p in range(2):
                    pe.wait_ge(sq_ready, p + 1)
                    nc.tensor.matmul(v_ps[p][:], wv[:], act_k[p][:], start=True, stop=True).then_inc(v_ready, 1)
                pe.sem_inc(mix_ready, -2)
                pe.sem_inc(sq_ready, -2)


def make_constants(nc, C):
    with ExitStack() as ctx:
        step = ctx.enter_context(semaphore_set(nc, "const"))("step")
        block = ctx.enter_context(nc.Block())

        @block.gpsimd
        def _(pool):
            nc.gpsimd.memset(C["ident"][:], 0.0).then_inc(step, 1)
            nc.gpsimd.memset(C["inv"][:], 1.0 / D)
            pool.wait_ge(step, 1)
            nc.gpsimd.affine_select(out=C["ident"][:], in_=C["ident"][:], compare_op=ALU.not_equal, fill=1.0, base=0,
                                    pattern=[[-1, D]], channel_multiplier=1)


def run_in_block(nc, name, engine, work):
    with ExitStack() as ctx:
        done = ctx.enter_context(semaphore_set(nc, name))("done")
        block = ctx.enter_context(nc.Block())
        if engine == "sync":
            @block.sync
            def _(eng):
                work(eng, done)
        else:
            @block.vector
            def _(eng):
                work(eng, done)


def model(nc, A, out):
    with ExitStack() as ctx:
        C = {"ident": ctx.enter_context(nc.sbuf_tensor("ident", [D, D], F32)),
             "inv": ctx.enter_context(nc.sbuf_tensor("inv", [D, D], F32))}
        make_constants(nc, C)
        x_in = A["x"].rearrange("d (b t) -> d b t", b=NB)
        x_out = out.rearrange("d (b t) -> d b t", b=NB)
        x_kept = nc.dram_tensor("x_kept", [D, NB, T], F32).ap()
        xs = ctx.enter_context(nc.sbuf_tensor("xs", [D, NB, T + 1], F32))

        def copy(name, dst, src):
            def work(sp, done):
                sp.dma_start(dst, src).then_inc(done, 16)
                sp.wait_ge(done, 16)
            run_in_block(nc, name, "sync", work)

        def skewed(b):
            return [(slice(0, 64), xs[0:64, b, 0:T]), (slice(64, 128), xs[64:128, b, 1:T + 1])]

        def attend(name, x, w, rope):
            with ExitStack() as c1:
                xn = c1.enter_context(nc.sbuf_tensor(f"{name}_xn", [D, NB, T], F32))
                layernorm_pass(nc, f"{name}_ln", C, x, lambda b: [(slice(0, D), xn[:, b, :])])
                attention_pass(nc, name, C, x, xn, w, rope)

        with ExitStack() as c1:
            x = c1.enter_context(nc.sbuf_tensor("x_first", [D, NB, T], F32))
            copy("load", x[:], x_in)
            attend("a0", x, [A[k] for k in ("L0_wq", "L0_bqk", "L0_wk", "L0_wv", "L0_bv", "L0_wo", "L0_bo")], None)
            layernorm_pass(nc, "b_ln", C, x, skewed)
            copy("keep", x_kept, x[:])

        def zero_before(v, done):
            nc.vector.memset(xs[64:128, :, 0:1], 0.0).then_inc(done, 1)
            v.wait_ge(done, 1)

        run_in_block(nc, "zero_before", "vector", zero_before)
        local_stack(nc, C, xs, A)

        x = ctx.enter_context(nc.sbuf_tensor("x_second", [D, NB, T], F32))
        copy("fetch", x[:], x_kept)

        def add_stack(v, done):
            for b in range(NB):
                for q, y in skewed(b):
                    nc.vector.tensor_tensor(x[q, b, :], x[q, b, :], y, ALU.add).then_inc(done, 1)
            v.wait_ge(done, 2 * NB)

        run_in_block(nc, "add_stack", "vector", add_stack)
        attend("a1", x, [A[k] for k in ("L1_wq", "L1_bqk", "L1_wk", "L1_wv", "L1_bv", "L1_wo", "L1_bo")],
               (A["cos1"], A["sin1"], A["turn1"]))

        xn = ctx.enter_context(nc.sbuf_tensor("d_xn", [D, NB, T + 1], F32))

        def zero_first(v, done):
            nc.vector.memset(xn[:, :, 0:1], 0.0).then_inc(done, 1)
            v.wait_ge(done, 1)

        run_in_block(nc, "zero_first", "vector", zero_first)
        layernorm_pass(nc, "d_ln", C, x, lambda b: [(slice(0, D), xn[:, b, 1:T + 1])])
        gated_mix_pass(nc, C, x, xn, A["d_wr"], A["d_wk"], A["d_wv"], A["d_mu"], x_out)


def rope_tables(n, width):
    inv = np.float32(1.0) / np.float32(10000.0) ** (np.arange(0, width, 2, dtype=np.float32) / np.float32(width))
    freqs = np.arange(n, dtype=np.float32)[:, None] * inv[None, :].astype(np.float32)
    return np.cos(freqs).astype(np.float32), np.sin(freqs).astype(np.float32)


def layouts(inputs):
    g = {k: np.asarray(v) for k, v in inputs.items()}
    col = lambda *v: np.ascontiguousarray(np.stack(v, axis=-1))
    a = {"x": np.ascontiguousarray(g["L0_attn_x"].reshape(NB * T, D).T)}
    by_place = np.arange(D).reshape(H, HD).T.reshape(-1)
    for n, p in ((0, "L0_attn_"), (1, "L1_attn_")):
        a[f"L{n}_wq"], a[f"L{n}_wk"], a[f"L{n}_wv"] = g[p + "Wq"][:, by_place], g[p + "Wk"][:, by_place], g[p + "Wv"]
        a[f"L{n}_bqk"] = col(g[p + "bq"], g[p + "bk"])[by_place]
        a[f"L{n}_bv"] = g[p + "bv"]
        a[f"L{n}_wo"] = g[p + ("Wo" if n == 0 else "Wp")]
        a[f"L{n}_bo"] = g[p + ("bo" if n == 0 else "bp")].reshape(D, 1)
    cos, sin = rope_tables(T, HD)
    a["cos1"] = np.repeat(np.repeat(cos, 2, axis=1).T, H, axis=0)
    a["sin1"] = np.repeat(np.repeat(sin, 2, axis=1).T, H, axis=0)
    turn = np.zeros((D, D), np.float32)
    for i in range(0, D, 2):
        turn[i + 1, i], turn[i, i + 1] = -1.0, 1.0
    a["turn1"] = turn[by_place][:, by_place]

    w = g["L0_ffn_Wqkv"]
    qk = w[:, :, :2 * INNER].reshape(DEPTH, D, 2, NC, CH, 2, HALF).transpose(0, 1, 2, 3, 5, 4, 6).reshape(DEPTH, D, 2 * INNER)
    a["wqkv"] = np.concatenate([qk, w[:, :, 2 * INNER:]], axis=2)
    a["wo"] = g["L0_ffn_Wo"].reshape(DEPTH, INNER // D, D, D).transpose(0, 2, 1, 3)
    a["w1"] = g["L0_ffn_W1"]
    w2 = np.zeros((DEPTH, 3 * D, D), np.float32)
    w2[:, :DI] = g["L0_ffn_W2"]
    a["w2"] = w2.reshape(DEPTH, 3, D, D).transpose(0, 2, 1, 3)
    vec = np.zeros((DEPTH, D, NVEC), np.float32)
    for i, n in enumerate(("L0_ffn_q_scale", "L0_ffn_k_scale")):
        for half in range(2):
            vec[:, :, 2 * i + half] = np.tile(g[n][:, HALF * half:HALF * half + HALF], (1, CH))
    vec[:, :, 4], vec[:, :, 8], vec[:, :, 9] = g["L0_ffn_ln_g"], g["L0_ffn_b2"], g["L0_ffn_ln_b"]
    o = 0
    for i, n in enumerate(FCH):
        vec[:, :n, 5 + i] = g["L0_ffn_b1"][:, o:o + n]
        vec[:, :n, 10 + i] = g["L0_ffn_b1"][:, DI + o:DI + o + n]
        o += n
    a["vec"] = vec
    cos, sin = rope_tables(T, DH)
    half = np.arange(0, DH, 2, dtype=np.float32)
    base = (half + np.float32(0.4 * DH)) / np.float32(1.4 * DH)
    power = (np.arange(T, dtype=np.float32) - T // 2) / np.float32(WIN // 2)
    scale = (base[None, :] ** power[:, None]).astype(np.float32)
    inv = (np.float32(1.0) / scale).astype(np.float32)
    a["tab"] = np.stack([np.tile((m * f).T, (CH, 1)) for f in (scale, inv) for m in (cos, sin)], axis=1)
    i, j = np.arange(D)[:, None] % WIN, np.arange(2 * WIN)[None, :]
    hidden = np.where(j < WIN, i > j, j - WIN > i)
    first = hidden | ((np.arange(D)[:, None] < WIN) & (j < WIN))
    tiles = [first] + [hidden] * (NT - 1)
    a["mask"] = np.concatenate([np.tile(m, (1, CH)) for m in tiles], axis=1).astype(np.float32) * np.float32(MASKED)
    a["d_wr"], a["d_wk"], a["d_wv"] = (g[f"L1_ffn_W_{n}"].T for n in "rkv")
    a["d_mu"] = col(g["L1_ffn_mu_r"], g["L1_ffn_mu_k"])
    a["block4"] = (np.arange(D)[:, None] // HALF == np.arange(CH)[None, :]).astype(np.float32)
    return {k: np.ascontiguousarray(v, dtype=np.float32) for k, v in a.items()}


def kernel(**inputs):
    import concourse.bacc as bacc
    from concourse.bass_utils import run_bass_kernel_spmd

    nc = bacc.Bacc("TRN2", target_bir_lowering=False, num_devices=1)
    arrays = layouts(inputs)
    aps = {k: nc.dram_tensor(f"in_{k}", v.shape, mybir.dt.from_np(v.dtype), kind="ExternalInput").ap()
           for k, v in arrays.items()}
    out = nc.dram_tensor("out", (D, NB * T), F32, kind="ExternalOutput").ap()
    model(nc, aps, out)
    r = run_bass_kernel_spmd(nc, [{f"in_{k}": v for k, v in arrays.items()}], core_ids=[0])
    return np.ascontiguousarray(np.asarray(r.results[0]["out"]).T.reshape(NB, T, D))
```

```python
import math
from contextlib import ExitStack, contextmanager

import numpy as np

import concourse.bass as bass
from concourse import mybir

F32 = mybir.dt.float32
BF16 = mybir.dt.bfloat16
I32 = mybir.dt.int32
ALU = mybir.AluOpType
ACT = mybir.ActivationFunctionType
AX = mybir.AxisListType

D = 128
NB = 8
T = 512
NT = T // 128
LN_EPS = 1e-5

H = 16
HD = D // H
SPLIT = 3
KROWS = SPLIT * SPLIT * HD
ROWS = KROWS + SPLIT
VW = 32

DEPTH = 6
DH = 64
HALF = DH // 2
INNER = H * DH
WIN = 32
NC = 4
CH = H // NC
KC = T + WIN
DI = int(D * 4 * 2 / 3)
FCH = [128, 128, DI - 256]
MASKED = -1e37
QK_SCALE = 8.0
NVEC = 13

RSQRT_MAGIC = float(0x5F3759DF)


class Tally:

    def __init__(self):
        self.used = {}

    def next(self, sem, n=1):
        count = self.used.get(sem.name, (sem, 0))[1] + n
        self.used[sem.name] = (sem, count)
        return count

    def settle(self, eng):
        for sem, count in self.used.values():
            if count:
                eng.sem_inc(sem, -count)
        self.used = {}


@contextmanager
def semaphore_set(nc, prefix):
    with ExitStack() as ctx:
        taken = []

        def sem(name):
            taken.append(ctx.enter_context(nc.semaphore(f"{prefix}_{name}")))
            return taken[-1]

        yield sem
        with nc.Block() as block:
            @block.sync
            def _(sp):
                for s in taken:
                    sp.sem_clear(s)


def rsqrt(nc, v, tally, step, a, t, y):
    nc.vector.tensor_scalar(t.bitcast(I32), a.bitcast(I32), 1, None, ALU.logical_shift_right).then_inc(step, 1)
    v.wait_ge(step, tally.next(step))
    nc.vector.tensor_scalar(y.bitcast(I32), t.bitcast(I32), -1.0, RSQRT_MAGIC, ALU.mult, ALU.add).then_inc(step, 1)
    for i in range(3):
        v.wait_ge(step, tally.next(step))
        nc.vector.scalar_tensor_tensor(out=t, in0=y, scalar=-0.5, in1=y, op0=ALU.mult, op1=ALU.mult).then_inc(step, 1)
        v.wait_ge(step, tally.next(step))
        nc.vector.tensor_tensor(t, t, a, ALU.mult).then_inc(step, 1)
        v.wait_ge(step, tally.next(step))
        last = nc.vector.scalar_tensor_tensor(out=y, in0=t, scalar=1.5, in1=y, op0=ALU.add, op1=ALU.mult)
        if i < 2:
            last.then_inc(step, 1)
    return last


def layernorm_pass(nc, name, C, src, dst_parts):
    with ExitStack() as ctx:
        def sb(n, shape, dt=F32):
            return ctx.enter_context(nc.sbuf_tensor(f"{name}_{n}", shape, dt))

        sem = ctx.enter_context(semaphore_set(nc, name))

        xc = sb("xc", [D, NB, T])
        sq = sb("sq", [D, 2, T])
        var = sb("var", [D, NB * NT])
        tmp = sb("tmp", [D, NB * NT])
        rstd = sb("rstd", [D, NB * NT])
        mean_ps = [ctx.enter_context(nc.psum_tensor(f"{name}_mean{i}", [D, T], F32)) for i in range(2)]
        var_ps = ctx.enter_context(nc.psum_tensor(f"{name}_varp", [D, NB * NT], F32))
        bc_ps = [ctx.enter_context(nc.psum_tensor(f"{name}_bc{i}", [D, T], F32)) for i in range(2)]
        mean_ready, centred, squared, var_ready = sem("mean"), sem("centred"), sem("squared"), sem("varr")
        sq_used, rstd_ready, bc_ready, bc_used, step = sem("squsd"), sem("rstd"), sem("bc"), sem("bcused"), sem("step")
        block = ctx.enter_context(nc.Block())

        @block.tensor
        def _(pe):
            def mean(b):
                if b >= 2:
                    pe.wait_ge(centred, b - 1)
                nc.tensor.matmul(mean_ps[b % 2][:], C["inv"][:], src[:, b, :], start=True, stop=True).then_inc(mean_ready, 1)

            mean(0)
            for b in range(NB):
                if b + 1 < NB:
                    mean(b + 1)
                pe.wait_ge(squared, b + 1)
                for t in range(NT):
                    last = nc.tensor.matmul(var_ps[:, b * NT + t:b * NT + t + 1], sq[:, b % 2, 128 * t:128 * t + 128],
                                            C["inv"][:, 0:1], start=True, stop=True)
                last.then_inc(var_ready, 1)
            pe.wait_ge(rstd_ready, 1)
            for b in range(NB):
                if b >= 2:
                    pe.wait_ge(bc_used, b - 1)
                for t in range(NT):
                    last = nc.tensor.transpose(bc_ps[b % 2][:, 128 * t:128 * t + 128],
                                               rstd[:, b * NT + t:b * NT + t + 1].to_broadcast([128, 128]), C["ident"][:])
                last.then_inc(bc_ready, 1)

        @block.scalar
        def _(act):
            for b in range(NB):
                act.wait_ge(centred, b + 1)
                if b >= 2:
                    act.wait_ge(var_ready, b - 1)
                nc.scalar.activation(sq[:, b % 2, :], xc[:, b, :], ACT.Square).then_inc(squared, 1)

        @block.vector
        def _(v):
            tally = Tally()
            for b in range(NB):
                v.wait_ge(mean_ready, b + 1)
                nc.vector.tensor_tensor(xc[:, b, :], src[:, b, :], mean_ps[b % 2][:], ALU.subtract).then_inc(centred, 1)
            v.wait_ge(var_ready, NB)
            nc.vector.tensor_scalar(var[:], var_ps[:], LN_EPS, None, ALU.add).then_inc(step, 1)
            v.wait_ge(step, tally.next(step))
            rsqrt(nc, v, tally, step, var[:], tmp[:], rstd[:]).then_inc(rstd_ready, 1)
            for b in range(NB):
                v.wait_ge(bc_ready, b + 1)
                for part, dst in dst_parts(b):
                    last = nc.vector.tensor_tensor(dst, xc[part, b, :], bc_ps[b % 2][part, :], ALU.mult)
                last.then_inc(bc_used, 1)


def attention_pass(nc, name, C, x, xn, w, rope):
    wq_d, bqkv_d, wk_d, wv_d, bv_d, wo_d, bo_d = w
    with ExitStack() as ctx:
        def sb(n, shape, dt=F32):
            return ctx.enter_context(nc.sbuf_tensor(f"{name}_{n}", shape, dt))

        sem = ctx.enter_context(semaphore_set(nc, name))

        wq, wk, wv, wo = sb("wq", [D, D]), sb("wk", [D, D]), sb("wv", [D, D]), sb("wo", [D, D])
        bqk = sb("bqk", [D, 2])
        bo = sb("bo", [D, 1])
        bv = sb("bv", [D, D])
        if rope is not None:
            cos, sin, turn = sb("cos", [D, T]), sb("sin", [D, T]), sb("turn", [D, D])
            rs = sb("rs", [D, 2, T])
        xs = sb("xs", [D, T])
        qk = sb("qk", [D, 2, T])
        parts = sb("parts", [D, SPLIT, 2, T], BF16)
        left = sb("left", [D, 2, T])
        qs = [sb(f"qs{i}", [ROWS, H, T], BF16) for i in range(2)]
        ks = [sb(f"ks{i}", [ROWS, H, T], BF16) for i in range(2)]
        vt = [sb(f"vt{i}", [D, NT, H, VW]) for i in range(2)]
        nmax = sb("nmax", [D, H, NT])
        rows = sb("rows", [H // 2, T])
        rleft = sb("rleft", [H // 2, T])
        rparts = sb("rparts", [H // 2, SPLIT, T], BF16)
        pt = [sb(f"pt{i}", [D, 4, T]) for i in range(2)]
        oe = sb("oe", [D, T])
        rsum = sb("rsum", [D, NT, 4])
        ot = sb("ot", [D, NT, D])
        of = sb("of", [D, T])
        scratch = [nc.dram_tensor(f"{name}_scr{i}", [2, SPLIT, D, T], BF16).ap() for i in range(2)]
        rscratch = [nc.dram_tensor(f"{name}_rscr{i}", [SPLIT, H // 2, T], BF16).ap() for i in range(2)]

        pair = [ctx.enter_context(nc.psum_tensor(f"{name}_pair{i}", [D, 2, T], F32)) for i in range(2)]
        st = [ctx.enter_context(nc.psum_tensor(f"{name}_st{i}", [D, T], F32)) for i in range(2)]
        op = [ctx.enter_context(nc.psum_tensor(f"{name}_o{i}", [D, T], F32)) for i in range(2)]

        loaded_pe, loaded_act, loaded_dve = sem("wpe"), sem("wact"), sem("wdve")
        loaded_pool = sem("wpool")
        xs_ready = sem("xs")
        proj_ready = sem("proj")
        v_ready = sem("vps")
        pair_act = sem("pair_act")
        pair_dve = [sem("pair_dve0"), sem("pair_dve1")]
        qk_ready = sem("qkready")
        turned = sem("turned")
        sin_ready = sem("sinr")
        rotated = sem("rotated")
        qk_split = sem("qksplit")
        pool_step, dve_step = sem("pstep"), sem("dstep")
        split_step = sem("splitstep")
        scratch_full = sem("scrf")
        qs_used = [sem("qsused0"), sem("qsused1")]
        qs_full = [sem("qsf0"), sem("qsf1")]
        s_ready = sem("sready")
        rows_ps = sem("rowsps")
        rows_ready = sem("rowsr")
        rows_split = sem("rowss")
        rscratch_full = sem("rscrf")
        rows_full = [sem("rowsf0"), sem("rowsf1")]
        st_ready = sem("stready")
        exp_done = sem("exp")
        pv_done = sem("pv")
        oe_ready = sem("oeready")
        otr_ready = sem("otr")
        of_ps = sem("ofps")
        of_ready = sem("ofr")
        wo_ready = sem("wor")
        ones_ready = sem("ones")
        rows_used = sem("rowsused")
        rparts_free = sem("rpfree")
        block = ctx.enter_context(nc.Block())

        SC = HD ** -0.5

        def program(eng, unit):
            unit(1, 0, None, None, None)
            unit(0, 1, 0, None, None)
            unit(1, 2, 1, 0, None)
            with eng.Fori(0, NB // 2 - 2) as i:
                unit(0, 2 * i + 3, 2 * i + 2, 2 * i + 1, 2 * i)
                unit(1, 2 * i + 4, 2 * i + 3, 2 * i + 2, 2 * i + 1)
            unit(0, NB - 1, NB - 2, NB - 3, NB - 4)
            unit(1, None, NB - 1, NB - 2, NB - 3)
            unit(0, None, None, NB - 1, NB - 2)
            unit(1, None, None, None, NB - 1)

        @block.sync
        def _(sp):
            for dst, src in ((wq, wq_d), (wk, wk_d), (wv, wv_d), (wo, wo_d)):
                sp.dma_start(dst[:], src).then_inc(loaded_pe, 16)
            sp.dma_start(bqk[:], bqkv_d).then_inc(loaded_act, 16)
            if rope is not None:
                sp.dma_start(turn[:], rope[2]).then_inc(loaded_pe, 16)
                sp.dma_start(sin[:], rope[1]).then_inc(loaded_dve, 16)
                sp.dma_start(cos[:], rope[0]).then_inc(loaded_pool, 16)
            sp.dma_start(bo[:], bo_d).then_inc(loaded_dve, 16)
            sp.dma_start(bv[:], bv_d.partition_broadcast(D)).then_inc(loaded_dve, 16)

            sp.wait_ge(ones_ready, 2)

            def unit(par, s, m, e, f):
                seen = Tally()

                def load_heads(half, p):
                    h = slice(8 * half, 8 * half + 8)
                    for i in range(SPLIT):
                        r = i * SPLIT * HD
                        sp.dma_start(ks[p][r:r + SPLIT * HD, h, :],
                                     scratch[p][1].rearrange("j (e h) t -> (j e) h t", e=HD)[:, h, :]).then_inc(qs_full[half], 16)
                        for j in range(SPLIT):
                            r = (i * SPLIT + j) * HD
                            sp.dma_start(qs[p][r:r + HD, h, :],
                                         scratch[p][0, i].rearrange("(e h) t -> e h t", e=HD)[:, h, :]).then_inc(qs_full[half], 16)

                def load_rows(half, p):
                    sp.wait_ge(rows_split, seen.next(rows_split))
                    sp.dma_start(rscratch[half].rearrange("s h t -> h s t"), rparts[:]).then_inc(rscratch_full, 16)
                    sp.wait_ge(rscratch_full, seen.next(rscratch_full, 16))
                    sp.sem_inc(rparts_free, 1)
                    sp.dma_start(qs[p][KROWS:ROWS, 8 * half:8 * half + 8, :], rscratch[half]).then_inc(rows_full[half], 16)

                if m is not None:
                    if f is not None:
                        sp.wait_ge(qs_used[1], seen.next(qs_used[1]))
                    load_heads(1, par)
                if e is not None:
                    load_rows(1, 1 - par)
                if s is not None:
                    sp.wait_ge(qk_split, seen.next(qk_split))
                    for i in range(SPLIT):
                        sp.dma_start(scratch[1 - par][:, i].rearrange("a d t -> d a t"), parts[:, i]).then_inc(scratch_full, 16)
                    sp.wait_ge(scratch_full, seen.next(scratch_full, SPLIT * 16))
                    if e is not None:
                        sp.wait_ge(qs_used[0], seen.next(qs_used[0]))
                    load_heads(0, 1 - par)
                if m is not None:
                    load_rows(0, par)
                seen.settle(sp)

            program(sp, unit)

        @block.gpsimd
        def _(pool):
            for i in range(2):
                nc.gpsimd.memset(ks[1 - i][64:ROWS], 1.0).then_inc(pool_step, 1)
            pool.wait_ge(pool_step, 2)
            pool.sem_inc(pool_step, -2)
            pool.sem_inc(ones_ready, 2)
            if rope is not None:
                pool.wait_ge(loaded_pool, 16)

            def unit(par, s, m, e, f):
                seen = Tally()

                def split_rows(wait):
                    pool.wait_ge(rows_ready, seen.next(rows_ready))
                    if wait:
                        pool.wait_ge(rparts_free, seen.next(rparts_free))
                    for i in range(SPLIT):
                        last = nc.gpsimd.tensor_copy(rparts[:, i, :], rows[:] if i == 0 else rleft[:])
                        if i < SPLIT - 1:
                            last.then_inc(pool_step, 1)
                            pool.wait_ge(pool_step, seen.next(pool_step))
                            nc.gpsimd.tensor_tensor(rleft[:], rows[:] if i == 0 else rleft[:], rparts[:, i, :],
                                                    ALU.subtract).then_inc(pool_step, 1)
                            pool.wait_ge(pool_step, seen.next(pool_step))
                    last.then_inc(rows_split, 1)
                    pool.drain().then_inc(rows_used, 1)

                if e is not None:
                    split_rows(True)
                if rope is not None and s is not None:
                    pool.wait_ge(qk_ready, seen.next(qk_ready))
                    pool.wait_ge(sin_ready, seen.next(sin_ready))
                    for a in range(2):
                        nc.gpsimd.tensor_tensor(qk[:, a, :], qk[:, a, :], cos[:], ALU.mult).then_inc(pool_step, 1)
                    for a in range(2):
                        pool.wait_ge(pool_step, seen.next(pool_step))
                        last = nc.gpsimd.tensor_tensor(qk[:, a, :], qk[:, a, :], rs[:, a, :], ALU.add)
                    last.then_inc(rotated, 1)
                if m is not None:
                    split_rows(e is not None)
                seen.settle(pool)

            program(pool, unit)

        @block.scalar
        def _(act):
            act.wait_ge(loaded_act, 16)

            def unit(par, s, m, e, f):
                seen = Tally()
                before = 0 if f is None else 2

                def exponentials(n, r):
                    act.wait_ge(st_ready, seen.next(st_ready))
                    if r == 0 and n - 1 + before > 0:
                        act.wait_ge(pv_done, n - 1 + before)
                    nc.scalar.activation(pt[n % 2][:, r, :], st[r % 2][:], ACT.Exp, scale=SC).then_inc(exp_done, 1)

                def output_copy(count, g):
                    act.wait_ge(pv_done, count)
                    nc.scalar.activation(oe[:], op[g % 2][:], ACT.Copy).then_inc(oe_ready, 1)

                def rows_copy(wait):
                    act.wait_ge(rows_ps, seen.next(rows_ps))
                    if wait:
                        act.wait_ge(rows_used, seen.next(rows_used))
                    nc.scalar.activation(rows[:], pair[0][0:H // 2, 0, :], ACT.Copy).then_inc(rows_ready, 1)
                    act.drain().then_inc(pair_act, 1)

                for n in range(H):
                    if n == H - 2:
                        seen.settle(act)
                    if e is not None:
                        for r in range(3):
                            exponentials(n, r)
                    if n == 1 and e is not None:
                        rows_copy(True)
                    if n == 1 and m is not None:
                        nc.scalar.activation(xs[:], xn[:, m, :], ACT.Copy).then_inc(xs_ready, 1)
                    if n == 2 and f is not None:
                        act.wait_ge(of_ps, seen.next(of_ps))
                        nc.scalar.activation(of[:], pair[0][:, 0, :], ACT.Copy).then_inc(of_ready, 1)
                    if n == 4 and s is not None:
                        act.wait_ge(proj_ready, seen.next(proj_ready))
                        nc.scalar.activation(qk[:, 0, :], pair[0][:, 0, :], ACT.Identity, bias=bqk[:, 0:1])
                        nc.scalar.activation(qk[:, 1, :], pair[0][:, 1, :], ACT.Identity, bias=bqk[:, 1:2]).then_inc(qk_ready, 1)
                        act.drain().then_inc(pair_act, 1)
                    if n == 9 and m is not None:
                        rows_copy(e is not None)
                    if e is not None:
                        exponentials(n, 3)
                        if n in (4, 8, 12):
                            output_copy(before + n, n // 4 - 1)
                    if f is not None and n == 0:
                        output_copy(2, 3)
                seen.next(pv_done, before + (H - 2 if e is not None else 0))
                seen.settle(act)

            program(act, unit)

        @block.vector
        def _(v):
            for i in range(2):
                nc.vector.memset(vt[i][:], 0.0).then_inc(dve_step, 1)
            v.wait_ge(dve_step, 2)
            for i in range(2):
                nc.vector.memset(vt[i][:, :, :, HD:HD + 1], 1.0).then_inc(dve_step, 1)
            v.wait_ge(dve_step, 4)
            v.sem_inc(dve_step, -4)
            v.wait_ge(loaded_dve, 32 if rope is None else 48)

            def unit(par, s, m, e, f):
                seen = Tally()

                def normalise(g):
                    v.wait_ge(otr_ready, seen.next(otr_ready))
                    o = pair[1][:, 0, :].rearrange("p (t r c) -> p t r c", t=NT, r=4)
                    nc.vector.reciprocal(rsum[:], o[:, :, :, HD]).then_inc(dve_step, 1)
                    v.wait_ge(dve_step, seen.next(dve_step))
                    nc.vector.tensor_tensor(ot[:, :, 4 * HD * g:4 * HD * (g + 1)].rearrange("p t (r e) -> p t r e", r=4),
                                            o[:, :, :, 0:HD], rsum[:].unsqueeze(3).to_broadcast([D, NT, 4, HD]),
                                            ALU.mult).then_inc(pair_dve[1], 1)

                def split(k):
                    i = k // 2
                    src = qk if i == 0 else left
                    if k > 0:
                        v.wait_ge(split_step, seen.next(split_step))
                    if k % 2 == 0:
                        last = nc.vector.tensor_copy(parts[:, i], src[:])
                    else:
                        last = nc.vector.tensor_tensor(left[:], src[:], parts[:, i], ALU.subtract)
                    last.then_inc(qk_split if k == 2 * SPLIT - 2 else split_step, 1)

                def maxima(n, i):
                    v.wait_ge(s_ready, seen.next(s_ready))
                    nc.vector.tensor_reduce(out=nmax[:, n, 2 * i:2 * i + 2], in_=pair[i][:], op=ALU.max,
                                            axis=AX.X, negate=True).then_inc(pair_dve[i], 1)

                split_slots = (4, 5, 6, 7, 8) if rope is None else (8, 8, 9, 10, 11)
                for n in range(H):
                    if n == H - 2:
                        seen.settle(v)
                    if m is not None:
                        maxima(n, 0)
                    if f is not None and n == 1:
                        normalise(3)
                    if m is not None and n == 2:
                        v.wait_ge(v_ready, seen.next(v_ready))
                        nc.vector.tensor_tensor(vt[par][:, :, :, 0:HD], pair[1][:, 0, :].rearrange("p (k h e) -> p k h e", k=NT, e=HD),
                                                bv[:].rearrange("p (h e) -> p h e", e=HD).unsqueeze(1).to_broadcast([D, NT, H, HD]),
                                                ALU.add).then_inc(pair_dve[1], 1)
                    if f is not None and n == 3:
                        v.wait_ge(wo_ready, seen.next(wo_ready))
                        nc.vector.scalar_tensor_tensor(out=x[:, f, :], in0=pair[1][:, 0, :], scalar=bo[:, 0:1], in1=x[:, f, :],
                                                       op0=ALU.add, op1=ALU.add).then_inc(pair_dve[1], 1)
                    if e is not None and n in (5, 9, 13):
                        normalise(n // 4 - 1)
                    if s is not None and rope is not None and n == 6:
                        v.wait_ge(turned, seen.next(turned))
                        for a in range(2):
                            last = nc.vector.tensor_tensor(rs[:, a, :], pair[1][:, a, :], sin[:], ALU.mult)
                        last.then_inc(sin_ready, 1)
                        v.drain().then_inc(pair_dve[1], 1)
                    if m is not None:
                        maxima(n, 1)
                    if s is not None and n == split_slots[0]:
                        ready = qk_ready if rope is None else rotated
                        v.wait_ge(ready, seen.next(ready))
                    if s is not None:
                        for k, slot in enumerate(split_slots):
                            if slot == n:
                                split(k)
                seen.settle(v)

            program(v, unit)

        @block.tensor
        def _(pe):
            pe.wait_ge(loaded_pe, 64 if rope is None else 80)
            due = {0: None, 1: None}

            def unit(par, s, m, e, f):
                seen = Tally()
                before = 0 if f is None else 4

                def read(i):
                    if due[i] is not None:
                        pe.wait_ge(due[i], seen.next(due[i]))
                    due[i] = None

                def claim(i, released_by):
                    read(i)
                    due[i] = released_by

                def scores(n, r):
                    k, h, kt = 4 * n + r, 4 * (n // 4) + r, n % 4
                    if k - 1 + before > 0:
                        pe.wait_ge(exp_done, k - 1 + before)
                    nc.tensor.matmul(st[r % 2][:], ks[1 - par][0:ROWS, h, 128 * kt:128 * kt + 128], qs[1 - par][0:ROWS, h, :],
                                     start=True, stop=True).then_inc(st_ready, 1)

                def pv(n, buf, count):
                    pe.wait_ge(exp_done, count)
                    for r in range(4):
                        last = nc.tensor.matmul(op[(n // 4) % 2][32 * r:32 * r + 32, :], vt[buf][:, n % 4, 4 * (n // 4) + r, :],
                                                pt[n % 2][:, r, :], start=(n % 4 == 0), stop=(n % 4 == 3), skip_group_check=True)
                    last.then_inc(pv_done, 1)

                def maxima(n, i):
                    claim(i, pair_dve[i])
                    for j in range(2):
                        q0 = 128 * (2 * i + j)
                        last = nc.tensor.matmul(pair[i][:, j, :], qs[par][0:KROWS, n, q0:q0 + 128], ks[par][0:KROWS, n, :],
                                                start=True, stop=True)
                    last.then_inc(s_ready, 1)

                def transposed_output():
                    pe.wait_ge(oe_ready, seen.next(oe_ready))
                    claim(1, pair_dve[1])
                    for t in range(NT):
                        last = nc.tensor.transpose(pair[1][:, 0, 128 * t:128 * t + 128], oe[:, 128 * t:128 * t + 128], C["ident"][:])
                    last.then_inc(otr_ready, 1)

                def row_maxima(half):
                    claim(0, pair_act)
                    if m is None:
                        read(1)
                    for t in range(NT):
                        last = nc.tensor.transpose(pair[0][0:H // 2, 0, 128 * t:128 * t + 128],
                                                   nmax[:, 8 * half:8 * half + 8, t], C["ident"][:])
                    last.then_inc(rows_ps, 1)

                for n in range(H):
                    if n == H - 2:
                        seen.settle(pe)
                    if n % 8 == 0:
                        half = n // 8
                        if e is not None:
                            if half == 1:
                                pe.wait_ge(rows_full[1], seen.next(rows_full[1], 16))
                            else:
                                pe.wait_ge(rows_full[0], seen.next(rows_full[0], 16))
                        if m is not None:
                            pe.wait_ge(qs_full[half], seen.next(qs_full[half], SPLIT * (SPLIT + 1) * 16))
                    if e is not None:
                        scores(n, 0)
                        scores(n, 1)
                    if m is not None:
                        maxima(n, 0)
                    if e is not None:
                        scores(n, 2)
                    if n == 1 and f is not None:
                        transposed_output()
                    if n == 2 and m is not None:
                        pe.wait_ge(xs_ready, seen.next(xs_ready))
                        claim(1, pair_dve[1])
                        for t in range(NT):
                            last = nc.tensor.matmul(pair[1][:, 0, 128 * t:128 * t + 128], xs[:, 128 * t:128 * t + 128], wv[:],
                                                    start=True, stop=True)
                        last.then_inc(v_ready, 1)
                    if n == 3 and f is not None:
                        if m is None:
                            read(0)
                        claim(1, pair_dve[1])
                        nc.tensor.matmul(pair[1][:, 0, :], wo[:], of[:], start=True, stop=True).then_inc(wo_ready, 1)
                    if n in (5, 9, 13) and e is not None:
                        transposed_output()
                    if n == 6 and rope is not None and s is not None:
                        if m is None:
                            read(0)
                        claim(1, pair_dve[1])
                        for a in range(2):
                            last = nc.tensor.matmul(pair[1][:, a, :], turn[:], qk[:, a, :], start=True, stop=True)
                        last.then_inc(turned, 1)
                    if n == 0 and f is not None:
                        pv(H - 1, par, 4)
                    if n > 0 and e is not None:
                        pv(n - 1, 1 - par, before + 4 * n)
                    if n == 1 and e is not None:
                        row_maxima(1)
                    if n == 2 and f is not None:
                        if m is None:
                            read(1)
                        claim(0, of_ready)
                        for t in range(NT):
                            last = nc.tensor.transpose(pair[0][:, 0, 128 * t:128 * t + 128], ot[:, t, :], C["ident"][:])
                        last.then_inc(of_ps, 1)
                    if n == 4 and s is not None:
                        claim(0, pair_act)
                        nc.tensor.matmul(pair[0][:, 0, :], wq[:], xn[:, s, :], start=True, stop=True)
                        nc.tensor.matmul(pair[0][:, 1, :], wk[:], xn[:, s, :], start=True, stop=True).then_inc(proj_ready, 1)
                    if n == 9 and m is not None:
                        row_maxima(0)
                    if e is not None:
                        scores(n, 3)
                        if n % 8 == 7:
                            pe.drain().then_inc(qs_used[n // 8], 1)
                    if m is not None:
                        maxima(n, 1)
                seen.next(exp_done, before + (4 * H - 4 if e is not None else 0))
                if m is None:
                    read(0)
                    read(1)
                seen.settle(pe)

            program(pe, unit)


def local_stack(nc, C, xs, A):
    with ExitStack() as ctx:
        def sb(n, shape, dt=F32):
            return ctx.enter_context(nc.sbuf_tensor(f"l_{n}", shape, dt))

        sem = ctx.enter_context(semaphore_set(nc, "l"))

        wqkv = [sb(f"wqkv{i}", [D, 3 * INNER]) for i in range(2)]
        qkvec = [sb(f"qkvec{i}", [D, 4]) for i in range(2)]
        wo, w1, w2 = sb("wo", [D, INNER // D, D]), sb("w1", [D, 2 * DI]), sb("w2", [D, 3, D])
        vec = sb("vec", [D, NVEC])
        vec_act = sb("vec_act", [D, NVEC])
        tab = sb("tab", [D, 4, T])
        mask = sb("mask", [D, 2, T], BF16)
        ident16 = sb("ident16", [D, D], BF16)
        block4 = sb("block4", [D, CH])
        xc = sb("xc", [D, T])
        t = sb("t", [D, 4, T])
        u = [sb(f"u{i}", [D, 4, T]) for i in range(2)]
        sq = [sb(f"sq{a}", [D, 2, T]) for a in range(2)]
        sqs = [sb(f"sqs{a}", [D, T]) for a in range(2)]
        qn, kn = sb("qn", [D, 2, T]), sb("kn", [D, 2, T])
        kbd = [sb(f"kbd{i}", [D, CH, KC]) for i in range(2)]
        norm = sb("norm", [D, NT * 2 * CH + NT])
        ntmp = sb("ntmp", [D, NT * 2 * CH + NT])
        rn = sb("rn", [D, NT * 2 * CH + NT])
        NSS = NT * 2 * CH
        rnx = sb("rnx", [D, NSS, HALF])
        p = sb("p", [D, NT * CH, 2 * WIN])
        pt = sb("pt", [D, NT * CH * 2 * WIN])
        smax = sb("smax", [D, NT * CH])
        ssum = sb("ssum", [D, NT * CH])
        srec = sb("srec", [D, NT * CH])
        pbd = sb("pbd", [D, 4, NT * CH * 2 * WIN])
        va = [sb(f"va{c}", [D, NT, CH * DH]) for c in range(NC)]
        vp = [sb(f"vp{c}", [D, NT, CH * DH]) for c in range(NC)]
        ot = sb("ot", [D, INNER // D, T])
        xcn, fsq = sb("xcn", [D, T]), sb("fsq", [D, T])
        xng, xnf = fsq, xc
        hid = [fsq, xcn, sb("hid2", [D, T])]

        R = [ctx.enter_context(nc.psum_tensor(f"l_r{i}", [D, 2, T], F32)) for i in range(4)]

        names = ("late_pe late_act late_dve late_free wqkv_free qkvec_free consts_pe consts_dve xc_ready q_dve q_act k_dve k_act v_act sq_free "
                 "r2_act r0_dve r1_dve r3_dve rq_ready ra_ready sq_sum ss_ready norm_read rn_ready rnx_ready b_ready r0_dve_b "
                 "qn_ready kn_ready kbd_full s_ready t_ready p_ready rec_ready pn_ready pt_ready pt_free pbd_free pbd_full "
                 "va_ready vp_full pv_ready ot_ready wo_ready x_ready mean_ready centred fsq_ready bc_ready xng_ready "
                 "xnf_ready g_ready a_ready gelu_ready h_ready f_ready ffn_done step pstep init mask_full").split()
        S = {n: sem(n) for n in names}
        wqkv_full, qkvec_full = ([sem(f"{n}{i}") for i in range(2)] for n in ("wqkv_full", "qkvec_full"))
        block = ctx.enter_context(nc.Block())

        def layers(eng, body):
            def layer(par, l, last=False):
                body(par, l, "last layer" if last else "layer", 0, NB - 1)
                with eng.Fori(1, NB) as b:
                    body(par, l, None, b, b - 1)

            body(0, 0, "layer", 0, None)
            with eng.Fori(1, NB) as b:
                body(0, 0, None, b, b - 1)
            with eng.Fori(0, DEPTH // 2 - 1) as i:
                layer(1, 2 * i + 1)
                layer(0, 2 * i + 2)
            layer(1, DEPTH - 1, last=True)
            body(1, None, None, None, NB - 1)

        def live(c, lag, b, prev):
            return b is not None if c >= lag else prev is not None

        @block.sync
        def _(sp):
            sp.dma_start(p[:].rearrange("p a b -> p (a b)"), A["mask"]).then_inc(S["mask_full"], 16)
            sp.dma_start(block4[:], A["block4"]).then_inc(S["consts_pe"], 16)
            sp.dma_start(tab[:], A["tab"]).then_inc(S["consts_dve"], 16)

            def load_early(p, l):
                sp.dma_start(wqkv[p][:], A["wqkv"][l]).then_inc(wqkv_full[p], 16)
                sp.dma_start(qkvec[p][:], A["vec"][l][:, 0:4]).then_inc(qkvec_full[p], 16)

            def load_late(l):
                sp.dma_start(wo[:], A["wo"][l]).then_inc(S["late_pe"], 16)
                sp.dma_start(w1[:], A["w1"][l]).then_inc(S["late_pe"], 16)
                sp.dma_start(w2[:], A["w2"][l]).then_inc(S["late_pe"], 16)
                sp.dma_start(vec[:], A["vec"][l]).then_inc(S["late_dve"], 16)
                sp.dma_start(vec_act[:], A["vec"][l]).then_inc(S["late_act"], 16)

            load_early(0, 0)
            load_late(0)

            def body(par, l, start, b, prev):
                seen = Tally()
                if start == "layer":
                    if prev is not None:
                        sp.wait_ge(S["wqkv_free"], seen.next(S["wqkv_free"]))
                        sp.wait_ge(S["qkvec_free"], seen.next(S["qkvec_free"]))
                    load_early(1 - par, l + 1)
                for c in range(NC):
                    if live(c, 3, b, prev):
                        sp.wait_ge(S["pbd_free"], seen.next(S["pbd_free"]))
                        sp.sem_inc(S["pt_free"], 1)
                        sp.wait_ge(S["pt_ready"], seen.next(S["pt_ready"]))
                        for w in range(4):
                            q = slice(32 * w, 32 * w + 32)
                            sp.dma_start(pbd[q, w, :], pt[q, :]).then_inc(S["pbd_full"], 16)
                    if b is not None:
                        sp.wait_ge(S["va_ready"], seen.next(S["va_ready"]))
                        sp.dma_start(vp[c][32:128], va[c][0:96]).then_inc(S["vp_full"], 16)
                        sp.dma_start(vp[c][0:32, 1:NT, :], va[c][96:128, 0:NT - 1, :]).then_inc(S["vp_full"], 16)
                    if live(c, 1, b, prev):
                        sp.wait_ge(S["kn_ready"], seen.next(S["kn_ready"]))
                        for i in range(2):
                            for r in range(CH):
                                q = slice(32 * r, 32 * r + 32)
                                sp.dma_start(kbd[i][q, r, WIN:KC], kn[q, i, :]).then_inc(S["kbd_full"], 16)
                if start and prev is not None:
                    sp.wait_ge(S["late_free"], seen.next(S["late_free"]))
                    load_late(l)
                seen.settle(sp)

            layers(sp, body)

        @block.gpsimd
        def _(pool):
            def body(par, l, start, b, prev):
                seen = Tally()
                for c in range(NC):
                    buf = c % 2
                    if b is not None:
                        for a in range(2):
                            pool.wait_ge(S["rq_ready"], seen.next(S["rq_ready"]))
                            nc.gpsimd.tensor_tensor(u[buf][:, 2 * a, :], t[:, 0, :], t[:, 3, :], ALU.subtract)
                            nc.gpsimd.tensor_tensor(u[buf][:, 2 * a + 1, :], t[:, 2, :], t[:, 1, :], ALU.add).then_inc(S["ra_ready"], 1)
                        nc.gpsimd.tensor_tensor(sqs[0][:], sq[0][:, 0, :], sq[0][:, 1, :], ALU.add)
                        nc.gpsimd.tensor_tensor(sqs[1][:], sq[1][:, 0, :], sq[1][:, 1, :], ALU.add).then_inc(S["sq_sum"], 1)
                        pool.drain().then_inc(S["sq_free"], 1)
                    if c == NC - 1:
                        seen.settle(pool)
                    if live(c, 2, b, prev):
                        pool.wait_ge(S["rec_ready"], seen.next(S["rec_ready"]))
                        nc.gpsimd.tensor_tensor(p[:], p[:], srec[:].unsqueeze(2).to_broadcast([D, NT * CH, 2 * WIN]),
                                                ALU.mult).then_inc(S["pn_ready"], 1)
                seen.settle(pool)

            layers(pool, body)

        @block.scalar
        def _(act):
            act.sem_inc(S["sq_free"], 1)

            def body(par, l, start, b, prev):
                seen = Tally()
                if start and prev is not None:
                    act.sem_inc(S["late_act"], -16)
                if b is not None:
                    nc.scalar.activation(xc[:], xs[:, b, 0:T], ACT.Copy).then_inc(S["xc_ready"], 1)
                for c in range(NC):
                    if b is not None:
                        act.wait_ge(S["sq_free"], seen.next(S["sq_free"]))
                        act.wait_ge(S["q_act"], seen.next(S["q_act"]))
                        nc.scalar.activation(sq[0][:], R[0][:], ACT.Square).then_inc(S["q_dve"], 1)
                        act.wait_ge(S["k_act"], seen.next(S["k_act"]))
                        nc.scalar.activation(sq[1][:], R[1][:], ACT.Square).then_inc(S["k_dve"], 1)
                    if c == 3 and prev is not None:
                        act.wait_ge(S["centred"], seen.next(S["centred"]))
                        nc.scalar.activation(fsq[:], xcn[:], ACT.Square).then_inc(S["fsq_ready"], 1)
                    if b is not None:
                        act.wait_ge(S["v_act"], seen.next(S["v_act"]))
                        nc.scalar.activation(va[c][:], R[2][:].rearrange("p a (k f) -> p (a k) f", k=2), ACT.Copy).then_inc(S["va_ready"], 1)
                        act.drain().then_inc(S["r2_act"], 1)
                    if live(c, 1, b, prev) or (c == 3 and prev is not None):
                        act.wait_ge(S["rn_ready"], seen.next(S["rn_ready"]))
                        if live(c, 1, b, prev):
                            nc.scalar.activation(rnx[:], rn[:, 0:NSS].unsqueeze(2).to_broadcast([D, NSS, HALF]), ACT.Copy)\
                                .then_inc(S["rnx_ready"], 1)
                        else:
                            act.sem_inc(S["rnx_ready"], 1)
                    if c == 3 and b is not None and not start:
                        act.wait_ge(S["late_act"], 16)
                    if live(c, 2, b, prev):
                        act.wait_ge(S["t_ready"], seen.next(S["t_ready"]))
                        nc.scalar.activation(p[:], p[:], ACT.Exp, scale=QK_SCALE).then_inc(S["p_ready"], 1)
                    if c == 3 and prev is not None:
                        act.wait_ge(S["xng_ready"], seen.next(S["xng_ready"]))
                        nc.scalar.activation(xnf[:], xng[:], ACT.Identity, bias=vec_act[:, 9:10]).then_inc(S["xnf_ready"], 1)
                    if live(c, 3, b, prev):
                        act.wait_ge(S["pv_ready"], seen.next(S["pv_ready"]))
                        cc = (c - 3) % NC
                        nc.scalar.activation(ot[:, 2 * cc:2 * cc + 2, :], R[1][:], ACT.Copy).then_inc(S["ot_ready"], 1)
                    if c == 3 and prev is not None:
                        seen.settle(act)
                        for i, n in enumerate(FCH):
                            act.wait_ge(S["g_ready"], seen.next(S["g_ready"]))
                            nc.scalar.activation(hid[i][0:n, :], R[(2, 3, 0)[i]][0:n, 0, :], ACT.Gelu,
                                                 bias=vec_act[0:n, 10 + i:11 + i]).then_inc(S["gelu_ready"], 1)
                seen.settle(act)

            layers(act, body)

        @block.vector
        def _(v):
            v.wait_ge(S["mask_full"], 16)
            nc.vector.tensor_copy(mask[:], p[:].rearrange("p a b -> p (a b)").rearrange("p (a b) -> p a b", a=2))
            nc.vector.tensor_copy(ident16[:], C["ident"][:])
            for i in range(2):
                nc.vector.memset(kbd[i][:], 0.0)
            nc.vector.memset(pbd[:], 0.0)
            for c in range(NC):
                nc.vector.memset(vp[c][:], 0.0)
            v.drain().then_inc(S["init"], 1)
            v.wait_ge(S["consts_dve"], 16)
            unread = {"ra": 0}

            def body(par, l, start, b, prev):
                seen = Tally()
                if start:
                    if prev is not None:
                        v.sem_inc(S["late_dve"], -16)
                        v.drain().then_inc(S["qkvec_free"], 1)
                    v.wait_ge(qkvec_full[par], seen.next(qkvec_full[par], 16))

                def halves_of_pool():
                    if unread["ra"]:
                        v.wait_ge(S["ra_ready"], seen.next(S["ra_ready"]))
                        unread["ra"] = 0

                def rotate(a):
                    halves_of_pool()
                    for half in range(2):
                        last = nc.vector.scalar_tensor_tensor(out=t[:, 2 * half:2 * half + 2, :],
                                                              in0=R[a][:, half, :].unsqueeze(1).to_broadcast([D, 2, T]),
                                                              scalar=qkvec[par][:, 2 * a + half:2 * a + half + 1],
                                                              in1=tab[:, 2 * a:2 * a + 2, :], op0=ALU.mult, op1=ALU.mult)
                    last.then_inc(S["rq_ready"], 1)
                    unread["ra"] = 1
                    v.drain().then_inc(S["r0_dve"] if a == 0 else S["r1_dve"], 1)

                def transpose_p(c):
                    if live(c, 3, b, prev):
                        v.wait_ge(S["pt_free"], seen.next(S["pt_free"]))
                        v.wait_ge(S["pn_ready"], seen.next(S["pn_ready"]))
                        nc.vector.transpose(pt[:], p[:].rearrange("p a b -> p (a b)")).then_inc(S["pt_ready"], 1)

                for c in range(NC):
                    par1 = (c - 1) % 2
                    if c == 3 and b is not None and not start:
                        v.wait_ge(S["late_dve"], 16)
                    if c == 3 and prev is not None:
                        v.wait_ge(S["wo_ready"], seen.next(S["wo_ready"]))
                        nc.vector.tensor_tensor(xs[0:64, prev, 0:T], xs[0:64, prev, 0:T], R[2][0:64, 0, :], ALU.add).then_inc(S["step"], 1)
                        nc.vector.tensor_tensor(xs[64:128, prev, 1:T + 1], xs[64:128, prev, 1:T + 1], R[2][64:128, 0, :],
                                                ALU.add).then_inc(S["x_ready"], 1)
                        v.wait_ge(S["step"], seen.next(S["step"]))
                        v.wait_ge(S["mean_ready"], seen.next(S["mean_ready"]))
                        nc.vector.tensor_tensor(xcn[:], xs[:, prev, 0:T], R[2][:, 1, :], ALU.subtract).then_inc(S["centred"], 1)
                    if b is not None:
                        v.wait_ge(S["q_dve"], seen.next(S["q_dve"]))
                        rotate(0)
                    has_ss, has_var = live(c, 1, b, prev), c == 3 and prev is not None
                    if has_ss or has_var:
                        v.wait_ge(S["ss_ready"], seen.next(S["ss_ready"]))
                        lo, hi = (0 if has_ss else NSS), (NSS + NT if has_var else NSS)
                        if has_ss:
                            nc.vector.tensor_scalar(norm[:, 0:NSS], R[3][:, 0, 0:NSS], 1e-24, None, ALU.max).then_inc(S["step"], 1)
                            v.wait_ge(S["step"], seen.next(S["step"]))
                        if has_var:
                            nc.vector.tensor_scalar(norm[:, NSS:], R[3][:, 1, 0:NT], LN_EPS, None, ALU.add).then_inc(S["step"], 1)
                            v.wait_ge(S["step"], seen.next(S["step"]))
                        v.sem_inc(S["norm_read"], 1)
                    transpose_p(c)
                    if has_ss or has_var:
                        rsqrt(nc, v, seen, S["step"], norm[:, lo:hi], ntmp[:, lo:hi], rn[:, lo:hi]).then_inc(S["rn_ready"], 1)
                    if b is not None:
                        v.wait_ge(S["k_dve"], seen.next(S["k_dve"]))
                        rotate(1)
                    if live(c, 2, b, prev):
                        v.wait_ge(S["s_ready"], seen.next(S["s_ready"]))
                        sc = R[3][:].rearrange("p a b -> p (a b)").rearrange("p (u k) -> p u k", k=2 * WIN)
                        nc.vector.tensor_reduce(out=smax[:], in_=sc, op=ALU.max, axis=AX.X).then_inc(S["step"], 1)
                        v.wait_ge(S["step"], seen.next(S["step"]))
                        nc.vector.tensor_tensor(p[:], sc, smax[:].unsqueeze(2).to_broadcast([D, NT * CH, 2 * WIN]),
                                                ALU.subtract).then_inc(S["t_ready"], 1)
                        v.drain().then_inc(S["r3_dve"], 1)
                    if has_var:
                        v.wait_ge(S["bc_ready"], seen.next(S["bc_ready"]))
                        nc.vector.scalar_tensor_tensor(out=xng[:], in0=xcn[:], scalar=vec[:, 4:5], in1=R[2][:, 0, :],
                                                       op0=ALU.mult, op1=ALU.mult).then_inc(S["xng_ready"], 1)
                    if has_ss:
                        v.wait_ge(S["b_ready"], seen.next(S["b_ready"]))
                        halves_of_pool()
                        for a, (dst, ready) in enumerate(((qn, "qn_ready"), (kn, "kn_ready"))):
                            nc.vector.tensor_tensor(dst[:], u[par1][:, 2 * a:2 * a + 2, :],
                                                    R[0][:, a, :].unsqueeze(1).to_broadcast([D, 2, T]), ALU.mult).then_inc(S[ready], 1)
                        v.drain().then_inc(S["r0_dve_b"], 1)
                    if live(c, 2, b, prev):
                        v.wait_ge(S["p_ready"], seen.next(S["p_ready"]))
                        nc.vector.tensor_reduce(out=ssum[:], in_=p[:], op=ALU.add, axis=AX.X).then_inc(S["step"], 1)
                        v.wait_ge(S["step"], seen.next(S["step"]))
                        nc.vector.reciprocal(srec[:], ssum[:]).then_inc(S["rec_ready"], 1)
                    if c == 3:
                        if prev is not None:
                            for i, n in enumerate(FCH):
                                v.wait_ge(S["a_ready"], seen.next(S["a_ready"]))
                                v.wait_ge(S["gelu_ready"], seen.next(S["gelu_ready"]))
                                nc.vector.scalar_tensor_tensor(out=hid[i][0:n, :], in0=R[(2, 3, 0)[i]][0:n, 1, :],
                                                               scalar=vec[0:n, 5 + i:6 + i], in1=hid[i][0:n, :],
                                                               op0=ALU.add, op1=ALU.mult).then_inc(S["h_ready"], 1)
                            seen.settle(v)
                            v.wait_ge(S["f_ready"], seen.next(S["f_ready"]))
                            nc.vector.scalar_tensor_tensor(out=xs[0:64, prev, 0:T], in0=R[2][0:64, 0, :], scalar=vec[0:64, 8:9],
                                                           in1=xs[0:64, prev, 0:T], op0=ALU.add, op1=ALU.add)
                            nc.vector.scalar_tensor_tensor(out=xs[64:128, prev, 1:T + 1], in0=R[2][64:128, 0, :], scalar=vec[64:128, 8:9],
                                                           in1=xs[64:128, prev, 1:T + 1], op0=ALU.add, op1=ALU.add).then_inc(S["ffn_done"], 1)
                            if start:
                                v.drain().then_inc(S["late_free"], 1)
                        else:
                            v.sem_inc(S["ffn_done"], 1)
                seen.settle(v)

            layers(v, body)

        @block.tensor
        def _(pe):
            pe.sem_inc(S["pbd_free"], 1)
            pe.wait_ge(S["init"], 1)
            pe.wait_ge(S["consts_pe"], 16)
            due = {0: [], 1: [], 2: [], 3: []}

            def body(par, l, start, b, prev):
                seen = Tally()
                if start:
                    if prev is not None:
                        pe.sem_inc(S["late_pe"], -48)
                        pe.drain().then_inc(S["wqkv_free"], 1)
                    pe.wait_ge(wqkv_full[par], seen.next(wqkv_full[par], 16))

                def read(i):
                    for n in due[i]:
                        pe.wait_ge(S[n], seen.next(S[n]))
                    due[i] = []

                def claim(i, *released_by):
                    read(i)
                    due[i] = list(released_by)

                def output_products(first, last):
                    for j in range(first, last):
                        product = nc.tensor.matmul(R[2][:, 0, :], wo[:, j, :], ot[:, j, :], start=(j == 0), stop=(j == INNER // D - 1),
                                                   skip_group_check=True)
                    return product

                for c in range(NC):
                    pv_before = live(c - 1, 3, b, prev) if c else prev is not None
                    if b is not None:
                        claim(0, "r0_dve")
                        for half in range(2):
                            o = 2 * D * c + D * half
                            last = nc.tensor.matmul(R[0][:, half, :], wqkv[par][:, o:o + D], xs[:, b, 0:T], start=True, stop=True)
                            if half == 0 and pv_before:
                                last.then_inc(S["pbd_free"], 1)
                        last.then_inc(S["q_act"], 1)
                    elif pv_before:
                        pe.drain().then_inc(S["pbd_free"], 1)
                    if c == 3 and prev is not None:
                        read(1)
                        output_products(2 * NC - 2, 2 * NC).then_inc(S["wo_ready"], 1)
                    if b is not None:
                        claim(1, "r1_dve")
                        for half in range(2):
                            o = INNER + 2 * D * c + D * half
                            last = nc.tensor.matmul(R[1][:, half, :], wqkv[par][:, o:o + D], xs[:, b, 0:T], start=True, stop=True)
                        last.then_inc(S["k_act"], 1)
                    if c == 3 and prev is not None:
                        pe.wait_ge(S["x_ready"], seen.next(S["x_ready"]))
                        nc.tensor.matmul(R[2][:, 1, :], C["inv"][:], xs[:, prev, 0:T], start=True, stop=True).then_inc(S["mean_ready"], 1)
                    has_ss, has_var = live(c, 1, b, prev), c == 3 and prev is not None
                    if has_ss or has_var:
                        claim(3)
                        if has_ss:
                            pe.wait_ge(S["sq_sum"], seen.next(S["sq_sum"]))
                            for k in range(NT):
                                for a in range(2):
                                    o = (k * 2 + a) * CH
                                    last = nc.tensor.matmul(R[3][:, 0, o:o + CH], sqs[a][:, 128 * k:128 * k + 128], block4[:],
                                                            start=True, stop=True)
                        if has_var:
                            pe.wait_ge(S["fsq_ready"], seen.next(S["fsq_ready"]))
                            for k in range(NT):
                                last = nc.tensor.matmul(R[3][:, 1, k:k + 1], fsq[:, 128 * k:128 * k + 128], C["inv"][:, 0:1],
                                                        start=True, stop=True)
                        last.then_inc(S["ss_ready"], 1)
                        due[3] = ["norm_read"]
                    if b is not None:
                        if c == 0:
                            pe.wait_ge(S["xc_ready"], seen.next(S["xc_ready"]))
                        claim(2, "r2_act")
                        for k in range(NT):
                            o = 2 * INNER + CH * DH * c
                            last = nc.tensor.matmul(R[2][:, k // 2, 256 * (k % 2):256 * (k % 2) + 256], xc[:, 128 * k:128 * k + 128],
                                                    wqkv[par][:, o:o + CH * DH], start=True, stop=True)
                        last.then_inc(S["v_act"], 1)
                    if live(c, 2, b, prev):
                        claim(3, "r3_dve")
                        pe.wait_ge(S["qn_ready"], seen.next(S["qn_ready"]))
                        pe.wait_ge(S["kbd_full"], seen.next(S["kbd_full"], 2 * CH * 16))
                        for bank in range(2):
                            nc.tensor.matmul(R[3][:, bank, :], ident16[:], mask[:, bank, :], start=True, stop=False, skip_group_check=True)
                            for w in range(8):
                                W, q = 8 * bank + w, 32 * (w % 4)
                                for half in range(2):
                                    last = nc.tensor.matmul(R[3][q:q + 32, bank, 256 * (w // 4):256 * (w // 4) + 256],
                                                            qn[:, half, WIN * W:WIN * W + WIN], kbd[half][:, :, WIN * W:WIN * W + 2 * WIN],
                                                            start=False, stop=(half == 1), skip_group_check=True)
                        last.then_inc(S["s_ready"], 1)
                    if has_ss or has_var:
                        pe.wait_ge(S["rnx_ready"], seen.next(S["rnx_ready"]))
                    if has_ss:
                        claim(0, "r0_dve_b")
                        for a in range(2):
                            for k in range(NT):
                                o = (k * 2 + a) * CH
                                last = nc.tensor.transpose(R[0][:, a, 128 * k:128 * k + 128],
                                                           rnx[:, o:o + CH, :].rearrange("p h i -> p (h i)"), C["ident"][:])
                        last.then_inc(S["b_ready"], 1)
                    if has_var:
                        claim(2)
                        for k in range(NT):
                            last = nc.tensor.transpose(R[2][:, 0, 128 * k:128 * k + 128], rn[:, NSS + k:NSS + k + 1].to_broadcast([D, D]),
                                                       C["ident"][:])
                        last.then_inc(S["bc_ready"], 1)
                    if c == 2 and b is not None and not start:
                        pe.wait_ge(S["late_pe"], 48)
                    if c == 2 and prev is not None:
                        if b is None:
                            read(1)
                        claim(2)
                        output_products(0, 2 * NC - 2)
                    if live(c, 3, b, prev):
                        claim(1, "ot_ready")
                        cc = (c - 3) % NC
                        pe.wait_ge(S["vp_full"], seen.next(S["vp_full"], 32))
                        pe.wait_ge(S["pbd_full"], seen.next(S["pbd_full"], 64))
                        for h in range(CH):
                            q = 64 * (h % 2)
                            for g in range(NT):
                                for half, vv in enumerate((vp[cc], va[cc])):
                                    o = ((g * CH + h) * 2 + half) * WIN
                                    last = nc.tensor.matmul(R[1][q:q + 64, h // 2, 128 * g:128 * g + 128], vv[:, g, DH * h:DH * h + DH],
                                                            pbd[:, :, o:o + WIN], start=(half == 0), stop=(half == 1))
                        last.then_inc(S["pv_ready"], 1)
                    if c == 3 and prev is not None:
                        pe.wait_ge(S["xnf_ready"], seen.next(S["xnf_ready"]))
                        o = 0
                        for i, n in enumerate(FCH):
                            r = R[(2, 3, 0)[i]]
                            claim((2, 3, 0)[i])
                            for half in ((1, 0) if i == len(FCH) - 1 else (0, 1)):
                                w = o if half else DI + o
                                nc.tensor.matmul(r[0:n, half, :], w1[:, w:w + n], xnf[:], start=True,
                                                 stop=True).then_inc(S["a_ready" if half else "g_ready"], 1)
                            o += n
                        seen.settle(pe)
                        for i, n in enumerate(FCH):
                            pe.wait_ge(S["h_ready"], seen.next(S["h_ready"]))
                            last = nc.tensor.matmul(R[2][:, 0, :], w2[0:n, i, :], hid[i][0:n, :], start=(i == 0), stop=(i == 2))
                        last.then_inc(S["f_ready"], 1)
                        due[2] = ["ffn_done"]
                    if c == 3 and prev is None:
                        for i in (0, 2, 3):
                            read(i)
                        due[2] = ["ffn_done"]
                if b is None:
                    for i in range(4):
                        read(i)
                seen.settle(pe)

            layers(pe, body)


def gated_mix_pass(nc, C, x, xn, wr_d, wk_d, wv_d, mu_d, out):
    with ExitStack() as ctx:
        def sb(n, shape, dt=F32):
            return ctx.enter_context(nc.sbuf_tensor(f"d_{n}", shape, dt))

        sem = ctx.enter_context(semaphore_set(nc, "d"))

        wr, wk, wv = sb("wr", [D, D]), sb("wk", [D, D]), sb("wv", [D, D])
        mu, comu = sb("mu", [D, 2]), sb("comu", [D, 2])
        prev = [[sb(f"prev{p}{a}", [D, T]) for a in range(2)] for p in range(2)]
        mix = [[sb(f"mix{p}{a}", [D, T]) for a in range(2)] for p in range(2)]
        gate = [sb(f"gate{p}", [D, T]) for p in range(2)]
        act_k = [sb(f"act_k{p}", [D, T]) for p in range(2)]
        res = [sb(f"res{p}", [D, T]) for p in range(2)]
        r_ps, k_ps, v_ps = ([ctx.enter_context(nc.psum_tensor(f"d_{n}{p}", [D, T], F32)) for p in range(2)] for n in "rkv")
        w_pe, w_dve, comu_ready = sem("wpe"), sem("wdve"), sem("comu")
        prev_ready, mix_ready, r_ready, k_ready = sem("prev"), sem("mix"), sem("r"), sem("k")
        relu_ready, sq_ready, v_ready, out_ready = sem("relu"), sem("sqr"), sem("v"), sem("out")
        stored, res_free, step = sem("stored"), sem("resfree"), sem("step")
        block = ctx.enter_context(nc.Block())

        @block.sync
        def _(sp):
            for dst, src in ((wr, wr_d), (wk, wk_d), (wv, wv_d)):
                sp.dma_start(dst[:], src).then_inc(w_pe, 16)
            sp.dma_start(mu[:], mu_d).then_inc(w_dve, 16)
            with sp.Fori(0, NB // 2) as i:
                for p in range(2):
                    sp.wait_ge(out_ready, p + 1)
                    sp.dma_start(out[:, 2 * i + p, :], res[p][:]).then_inc(stored, 16)
                sp.sem_inc(out_ready, -2)
                sp.wait_ge(stored, 32)
                sp.sem_inc(stored, -32)
                sp.sem_inc(res_free, 1)

        @block.scalar
        def _(act):
            act.wait_ge(comu_ready, 1)
            with act.Fori(0, NB // 2) as i:
                for p in range(2):
                    for a in range(2):
                        last = nc.scalar.activation(prev[p][a][:], xn[:, 2 * i + p, 0:T], ACT.Copy, scale=comu[:, a:a + 1])
                    last.then_inc(prev_ready, 1)
                for p in range(2):
                    act.wait_ge(r_ready, p + 1)
                    nc.scalar.activation(gate[p][:], r_ps[p][:], ACT.Sigmoid)
                    act.wait_ge(k_ready, p + 1)
                    nc.scalar.activation(act_k[p][:], k_ps[p][:], ACT.Relu).then_inc(relu_ready, 1)
                act.sem_inc(r_ready, -2)
                act.sem_inc(k_ready, -2)

        @block.vector
        def _(v):
            v.sem_inc(res_free, 1)
            v.wait_ge(w_dve, 16)
            nc.vector.tensor_scalar(comu[:], mu[:], -1.0, 1.0, ALU.mult, ALU.add).then_inc(comu_ready, 1)
            with v.Fori(0, NB // 2) as i:
                for p in range(2):
                    v.wait_ge(prev_ready, p + 1)
                    for a in range(2):
                        last = nc.vector.scalar_tensor_tensor(out=mix[p][a][:], in0=xn[:, 2 * i + p, 1:T + 1], scalar=mu[:, a:a + 1],
                                                              in1=prev[p][a][:], op0=ALU.mult, op1=ALU.add)
                    last.then_inc(mix_ready, 1)
                for p in range(2):
                    v.wait_ge(relu_ready, p + 1)
                    nc.vector.tensor_tensor(act_k[p][:], act_k[p][:], act_k[p][:], ALU.mult).then_inc(sq_ready, 1)
                v.wait_ge(res_free, 1)
                for p in range(2):
                    v.wait_ge(v_ready, p + 1)
                    nc.vector.tensor_tensor(res[p][:], v_ps[p][:], gate[p][:], ALU.mult).then_inc(step, 1)
                for p in range(2):
                    v.wait_ge(step, p + 1)
                    nc.vector.tensor_tensor(res[p][:], res[p][:], x[:, 2 * i + p, :], ALU.add).then_inc(out_ready, 1)
                for s, n in ((prev_ready, 2), (relu_ready, 2), (res_free, 1), (v_ready, 2), (step, 2)):
                    v.sem_inc(s, -n)

        @block.tensor
        def _(pe):
            pe.wait_ge(w_pe, 48)
            with pe.Fori(0, NB // 2) as i:
                for p in range(2):
                    pe.wait_ge(mix_ready, p + 1)
                    nc.tensor.matmul(r_ps[p][:], wr[:], mix[p][0][:], start=True, stop=True).then_inc(r_ready, 1)
                    nc.tensor.matmul(k_ps[p][:], wk[:], mix[p][1][:], start=True, stop=True).then_inc(k_ready, 1)
                for p in range(2):
                    pe.wait_ge(sq_ready, p + 1)
                    nc.tensor.matmul(v_ps[p][:], wv[:], act_k[p][:], start=True, stop=True).then_inc(v_ready, 1)
                pe.sem_inc(mix_ready, -2)
                pe.sem_inc(sq_ready, -2)


def make_constants(nc, C):
    with ExitStack() as ctx:
        step = ctx.enter_context(semaphore_set(nc, "const"))("step")
        block = ctx.enter_context(nc.Block())

        @block.gpsimd
        def _(pool):
            nc.gpsimd.memset(C["ident"][:], 0.0).then_inc(step, 1)
            nc.gpsimd.memset(C["inv"][:], 1.0 / D)
            pool.wait_ge(step, 1)
            nc.gpsimd.affine_select(out=C["ident"][:], in_=C["ident"][:], compare_op=ALU.not_equal, fill=1.0, base=0,
                                    pattern=[[-1, D]], channel_multiplier=1)


def run_in_block(nc, name, engine, work):
    with ExitStack() as ctx:
        done = ctx.enter_context(semaphore_set(nc, name))("done")
        block = ctx.enter_context(nc.Block())
        if engine == "sync":
            @block.sync
            def _(eng):
                work(eng, done)
        else:
            @block.vector
            def _(eng):
                work(eng, done)


def model(nc, A, out):
    with ExitStack() as ctx:
        C = {"ident": ctx.enter_context(nc.sbuf_tensor("ident", [D, D], F32)),
             "inv": ctx.enter_context(nc.sbuf_tensor("inv", [D, D], F32))}
        make_constants(nc, C)
        x_in = A["x"].rearrange("d (b t) -> d b t", b=NB)
        x_out = out.rearrange("d (b t) -> d b t", b=NB)
        x_kept = nc.dram_tensor("x_kept", [D, NB, T], F32).ap()
        xs = ctx.enter_context(nc.sbuf_tensor("xs", [D, NB, T + 1], F32))

        def copy(name, dst, src):
            def work(sp, done):
                sp.dma_start(dst, src).then_inc(done, 16)
                sp.wait_ge(done, 16)
            run_in_block(nc, name, "sync", work)

        def skewed(b):
            return [(slice(0, 64), xs[0:64, b, 0:T]), (slice(64, 128), xs[64:128, b, 1:T + 1])]

        def attend(name, x, w, rope):
            with ExitStack() as c1:
                xn = c1.enter_context(nc.sbuf_tensor(f"{name}_xn", [D, NB, T], F32))
                layernorm_pass(nc, f"{name}_ln", C, x, lambda b: [(slice(0, D), xn[:, b, :])])
                attention_pass(nc, name, C, x, xn, w, rope)

        with ExitStack() as c1:
            x = c1.enter_context(nc.sbuf_tensor("x_first", [D, NB, T], F32))
            copy("load", x[:], x_in)
            attend("a0", x, [A[k] for k in ("L0_wq", "L0_bqk", "L0_wk", "L0_wv", "L0_bv", "L0_wo", "L0_bo")], None)
            layernorm_pass(nc, "b_ln", C, x, skewed)
            copy("keep", x_kept, x[:])

        def zero_before(v, done):
            nc.vector.memset(xs[64:128, :, 0:1], 0.0).then_inc(done, 1)
            v.wait_ge(done, 1)

        run_in_block(nc, "zero_before", "vector", zero_before)
        local_stack(nc, C, xs, A)

        x = ctx.enter_context(nc.sbuf_tensor("x_second", [D, NB, T], F32))
        copy("fetch", x[:], x_kept)

        def add_stack(v, done):
            for b in range(NB):
                for q, y in skewed(b):
                    nc.vector.tensor_tensor(x[q, b, :], x[q, b, :], y, ALU.add).then_inc(done, 1)
            v.wait_ge(done, 2 * NB)

        run_in_block(nc, "add_stack", "vector", add_stack)
        attend("a1", x, [A[k] for k in ("L1_wq", "L1_bqk", "L1_wk", "L1_wv", "L1_bv", "L1_wo", "L1_bo")],
               (A["cos1"], A["sin1"], A["turn1"]))

        xn = ctx.enter_context(nc.sbuf_tensor("d_xn", [D, NB, T + 1], F32))

        def zero_first(v, done):
            nc.vector.memset(xn[:, :, 0:1], 0.0).then_inc(done, 1)
            v.wait_ge(done, 1)

        run_in_block(nc, "zero_first", "vector", zero_first)
        layernorm_pass(nc, "d_ln", C, x, lambda b: [(slice(0, D), xn[:, b, 1:T + 1])])
        gated_mix_pass(nc, C, x, xn, A["d_wr"], A["d_wk"], A["d_wv"], A["d_mu"], x_out)


def rope_tables(n, width):
    inv = np.float32(1.0) / np.float32(10000.0) ** (np.arange(0, width, 2, dtype=np.float32) / np.float32(width))
    freqs = np.arange(n, dtype=np.float32)[:, None] * inv[None, :].astype(np.float32)
    return np.cos(freqs).astype(np.float32), np.sin(freqs).astype(np.float32)


def layouts(inputs):
    g = {k: np.asarray(v) for k, v in inputs.items()}
    col = lambda *v: np.ascontiguousarray(np.stack(v, axis=-1))
    a = {"x": np.ascontiguousarray(g["L0_attn_x"].reshape(NB * T, D).T)}
    by_place = np.arange(D).reshape(H, HD).T.reshape(-1)
    for n, p in ((0, "L0_attn_"), (1, "L1_attn_")):
        a[f"L{n}_wq"], a[f"L{n}_wk"], a[f"L{n}_wv"] = g[p + "Wq"][:, by_place], g[p + "Wk"][:, by_place], g[p + "Wv"]
        a[f"L{n}_bqk"] = col(g[p + "bq"], g[p + "bk"])[by_place]
        a[f"L{n}_bv"] = g[p + "bv"]
        a[f"L{n}_wo"] = g[p + ("Wo" if n == 0 else "Wp")]
        a[f"L{n}_bo"] = g[p + ("bo" if n == 0 else "bp")].reshape(D, 1)
    cos, sin = rope_tables(T, HD)
    a["cos1"] = np.repeat(np.repeat(cos, 2, axis=1).T, H, axis=0)
    a["sin1"] = np.repeat(np.repeat(sin, 2, axis=1).T, H, axis=0)
    turn = np.zeros((D, D), np.float32)
    for i in range(0, D, 2):
        turn[i + 1, i], turn[i, i + 1] = -1.0, 1.0
    a["turn1"] = turn[by_place][:, by_place]

    w = g["L0_ffn_Wqkv"]
    qk = w[:, :, :2 * INNER].reshape(DEPTH, D, 2, NC, CH, 2, HALF).transpose(0, 1, 2, 3, 5, 4, 6).reshape(DEPTH, D, 2 * INNER)
    a["wqkv"] = np.concatenate([qk, w[:, :, 2 * INNER:]], axis=2)
    a["wo"] = g["L0_ffn_Wo"].reshape(DEPTH, INNER // D, D, D).transpose(0, 2, 1, 3)
    a["w1"] = g["L0_ffn_W1"]
    w2 = np.zeros((DEPTH, 3 * D, D), np.float32)
    w2[:, :DI] = g["L0_ffn_W2"]
    a["w2"] = w2.reshape(DEPTH, 3, D, D).transpose(0, 2, 1, 3)
    vec = np.zeros((DEPTH, D, NVEC), np.float32)
    for i, n in enumerate(("L0_ffn_q_scale", "L0_ffn_k_scale")):
        for half in range(2):
            vec[:, :, 2 * i + half] = np.tile(g[n][:, HALF * half:HALF * half + HALF], (1, CH))
    vec[:, :, 4], vec[:, :, 8], vec[:, :, 9] = g["L0_ffn_ln_g"], g["L0_ffn_b2"], g["L0_ffn_ln_b"]
    o = 0
    for i, n in enumerate(FCH):
        vec[:, :n, 5 + i] = g["L0_ffn_b1"][:, o:o + n]
        vec[:, :n, 10 + i] = g["L0_ffn_b1"][:, DI + o:DI + o + n]
        o += n
    a["vec"] = vec
    cos, sin = rope_tables(T, DH)
    half = np.arange(0, DH, 2, dtype=np.float32)
    base = (half + np.float32(0.4 * DH)) / np.float32(1.4 * DH)
    power = (np.arange(T, dtype=np.float32) - T // 2) / np.float32(WIN // 2)
    scale = (base[None, :] ** power[:, None]).astype(np.float32)
    inv = (np.float32(1.0) / scale).astype(np.float32)
    a["tab"] = np.stack([np.tile((m * f).T, (CH, 1)) for f in (scale, inv) for m in (cos, sin)], axis=1)
    i, j = np.arange(D)[:, None] % WIN, np.arange(2 * WIN)[None, :]
    hidden = np.where(j < WIN, i > j, j - WIN > i)
    first = hidden | ((np.arange(D)[:, None] < WIN) & (j < WIN))
    tiles = [first] + [hidden] * (NT - 1)
    a["mask"] = np.concatenate([np.tile(m, (1, CH)) for m in tiles], axis=1).astype(np.float32) * np.float32(MASKED)
    a["d_wr"], a["d_wk"], a["d_wv"] = (g[f"L1_ffn_W_{n}"].T for n in "rkv")
    a["d_mu"] = col(g["L1_ffn_mu_r"], g["L1_ffn_mu_k"])
    a["block4"] = (np.arange(D)[:, None] // HALF == np.arange(CH)[None, :]).astype(np.float32)
    return {k: np.ascontiguousarray(v, dtype=np.float32) for k, v in a.items()}


def kernel(**inputs):
    import concourse.bacc as bacc
    from concourse.bass_utils import run_bass_kernel_spmd

    nc = bacc.Bacc("TRN2", target_bir_lowering=False, num_devices=1)
    arrays = layouts(inputs)
    aps = {k: nc.dram_tensor(f"in_{k}", v.shape, mybir.dt.from_np(v.dtype), kind="ExternalInput").ap()
           for k, v in arrays.items()}
    out = nc.dram_tensor("out", (D, NB * T), F32, kind="ExternalOutput").ap()
    model(nc, aps, out)
    r = run_bass_kernel_spmd(nc, [{f"in_{k}": v for k, v in arrays.items()}], core_ids=[0])
    return np.ascontiguousarray(np.asarray(r.results[0]["out"]).T.reshape(NB, T, D))
```
